# Optimizing a Trainium2 kernel written in Bass

```python
import numpy as np
import jax
import jax.numpy as jnp

def _softmax(x, axis=-1):
    return jax.nn.softmax(x, axis=axis)

def _gelu(x):
    return jax.nn.gelu(x, approximate=True)

def _silu(x):
    return jax.nn.silu(x)

def _sigmoid(x):
    return jax.nn.sigmoid(x)

def _layernorm(x, axis=-1, eps=1e-05):
    m = jnp.mean(x, axis=axis, keepdims=True)
    v = jnp.var(x, axis=axis, keepdims=True)
    return (x - m) / jnp.sqrt(v + eps)

def _scatter_add(tgt, idx, src, axis=0):
    return tgt.at[idx].add(src)

def _segment_sum(src, seg, n):
    return jax.ops.segment_sum(src, seg, n)
kernel_name = 'mk_decoder_preln_d4_seqx_r8_6fa11c'

def setup_inputs(seed: int=0):
    np.random.seed(seed)
    _w = jnp.asarray

    def _rec_inputs():
        import jax
        import jax.numpy as jnp
        _rk = jax.random.key(seed)
        x = 2.818e-05 + 1 * jax.random.normal(jax.random.fold_in(_rk, 1), (128, 64, 128), jnp.float32)
        _lenS = 64 - jax.random.randint(jax.random.fold_in(_rk, 7), (128,), 0, max(1, 64 // 4) + 1, jnp.int32)
        _lenS2 = 64 - jax.random.randint(jax.random.fold_in(_rk, 8), (128,), 0, max(1, 64 // 4) + 1, jnp.int32)
        _ctx_2048P = jax.random.normal(jax.random.fold_in(_rk, 11), (128, 16, 256), jnp.float32)
        _ctx_2048c = jax.random.dirichlet(jax.random.fold_in(_rk, 511), 0.3 * jnp.ones((16,), jnp.float32), (128, 64))
        _ctx_2048t = jnp.einsum('bsk,bkd->bsd', _ctx_2048c, _ctx_2048P)
        _ctx_2048t = _ctx_2048t * jax.lax.rsqrt(jnp.mean(jnp.square(_ctx_2048t)) + 1e-12) * 0.953939
        ctx_2048 = -0.000125008 + 0.999885 * (_ctx_2048t + 0.3 * jax.random.normal(jax.random.fold_in(_rk, 611), (128, 64, 256), jnp.float32))
        _validS = jnp.arange(64)[None, :] < _lenS[:, None]
        _validS2 = jnp.arange(64)[None, :] < _lenS2[:, None]
        _causal = jnp.tril(jnp.ones((64, 64), dtype=bool))
        mask_BxS2_fk1 = jnp.where(jnp.broadcast_to(_validS2[:, :], (128, 64)), 1.0, 0.0).astype(jnp.float32)
        mask_BxS2_ik0 = jnp.where(jnp.broadcast_to(_validS2[:, :], (128, 64)), 0, 1).astype(jnp.int32)
        mask_BxS2_if0 = jnp.where(jnp.ones((128, 64), dtype=bool), 4, 0).astype(jnp.int32)
        return (x, ctx_2048, mask_BxS2_fk1, mask_BxS2_ik0, mask_BxS2_if0)
    x, ctx_2048, mask_BxS2_fk1, mask_BxS2_ik0, mask_BxS2_if0 = _rec_inputs()

    def _L0_attn_setup():
        import jax, jax.numpy as jnp
        import numpy as np
        DIM = 128
        N_HEADS = 16
        HEAD_DIM = DIM // N_HEADS

        def apply_rope(x):
            B, T, H, D = x.shape
            half = D // 2
            x1, x2 = (x[..., :half], x[..., half:])
            theta = 1.0 / 10000.0 ** (jnp.arange(0, half, 2, dtype=jnp.float32) / half)
            pos = jnp.arange(T, dtype=jnp.float32)
            freq = pos[:, None] * theta[None, :]
            sin = jnp.sin(freq)[None, :, None, :]
            cos = jnp.cos(freq)[None, :, None, :]
            x1e, x1o = (x1[..., ::2], x1[..., 1::2])
            x2e, x2o = (x2[..., ::2], x2[..., 1::2])
            x1r = jnp.concatenate([x1e * cos - x1o * sin, x1e * sin + x1o * cos], axis=-1)
            x2r = jnp.concatenate([x2e * cos - x2o * sin, x2e * sin + x2o * cos], axis=-1)
            return jnp.concatenate([x1r, x2r], axis=-1)
        key = jax.random.key(seed)
        ks = jax.random.split(key, 9)
        B, T, C, D = (2, 256, DIM, HEAD_DIM)
        s = 0.02
        return {'x': jax.random.normal(ks[0], (B, T, C), dtype=jnp.float32), 'Wq': jax.random.normal(ks[1], (C, C), dtype=jnp.float32) * s, 'bq': jnp.zeros((C,), dtype=jnp.float32), 'Wk': jax.random.normal(ks[2], (C, D), dtype=jnp.float32) * s, 'bk': jnp.zeros((D,), dtype=jnp.float32), 'Wv': jax.random.normal(ks[3], (C, D), dtype=jnp.float32) * s, 'bv': jnp.zeros((D,), dtype=jnp.float32), 'Wo': jax.random.normal(ks[4], (C, C), dtype=jnp.float32) * s, 'bo': jnp.zeros((C,), dtype=jnp.float32)}
    _L0_attn_all = _L0_attn_setup()
    _L0_attn_in = {k: v for k, v in _L0_attn_all.items() if k in ('Wq', 'bq', 'Wk', 'bk', 'Wv', 'bv', 'Wo', 'bo')}
    del _L0_attn_all

    def _L0_xattn_setup():
        import jax, jax.numpy as jnp
        import numpy as np
        B, S, T = (32, 64, 64)
        SRC_SIZE, TGT_SIZE, OUT_SIZE, NUM_HEAD = (256, 128, 128, 8)
        HEAD_DIM = OUT_SIZE // NUM_HEAD
        key = jax.random.key(seed)
        ks = jax.random.split(key, 12)
        src = jax.random.normal(ks[0], (B, S, SRC_SIZE), dtype=jnp.float32)
        tgt = jax.random.normal(ks[1], (B, T, TGT_SIZE), dtype=jnp.float32)
        src_mask = (jax.random.uniform(ks[2], (B, S)) > 0.3).astype(jnp.float32)
        src_mask = src_mask.at[:, 0].set(1.0)
        tgt_mask = (jax.random.uniform(ks[3], (B, T)) > 0.3).astype(jnp.float32)
        tgt_mask = tgt_mask.at[:, 0].set(1.0)

        def lin(k, out_f, in_f):
            return jax.random.normal(k, (out_f, in_f), dtype=jnp.float32) / np.sqrt(in_f)
        W_src = lin(ks[4], 2 * OUT_SIZE, SRC_SIZE)
        b_src = jnp.zeros((2 * OUT_SIZE,), jnp.float32)
        W_tgt = lin(ks[5], OUT_SIZE, TGT_SIZE)
        b_tgt = jnp.zeros((OUT_SIZE,), jnp.float32)
        W_out = lin(ks[6], OUT_SIZE, OUT_SIZE + TGT_SIZE)
        b_out = jnp.zeros((OUT_SIZE,), jnp.float32)
        return {'src': src, 'tgt': tgt, 'src_mask': src_mask, 'tgt_mask': tgt_mask, 'W_src': W_src, 'b_src': b_src, 'W_tgt': W_tgt, 'b_tgt': b_tgt, 'W_out': W_out, 'b_out': b_out}
    _L0_xattn_all = _L0_xattn_setup()
    _L0_xattn_in = {k: v for k, v in _L0_xattn_all.items() if k in ('W_src', 'b_src', 'W_tgt', 'b_tgt', 'W_out', 'b_out')}
    del _L0_xattn_all

    def _L0_ffn_setup():
        import jax, jax.numpy as jnp
        import numpy as np
        TOP_K = 2
        CAPACITY_FACTOR = 1.25

        def _moe_forward(x, gate_w, wi_gate, wi_up, wo):
            B, S, D = x.shape
            E = wi_gate.shape[0]
            N = B * S
            capacity = max(int(N / E * CAPACITY_FACTOR), 1)
            x_flat = x.reshape(N, D)
            router_logits = x_flat @ gate_w.T
            router_probs = jax.nn.softmax(router_logits, axis=-1)
            top_k_probs, top_k_idx = jax.lax.top_k(router_probs, TOP_K)
            top_k_probs = top_k_probs / jnp.sum(top_k_probs, axis=-1, keepdims=True)
            out = jnp.zeros_like(x_flat)
            experts = jnp.arange(E, dtype=jnp.int32)
            for k in range(TOP_K):
                eid = top_k_idx[:, k]
                ew = top_k_probs[:, k]
                onehot = (eid[:, None] == experts[None, :]).astype(jnp.int32)
                pos_all = jnp.cumsum(onehot, axis=0) - 1
                pos = jnp.take_along_axis(pos_all, eid[:, None].astype(jnp.int32), axis=1)[:, 0]
                valid = pos < capacity
                pos_c = jnp.where(valid, pos, 0)
                disp = jnp.zeros((E, capacity, D), x_flat.dtype).at[eid, pos_c].add(jnp.where(valid[:, None], x_flat, 0.0))
                gate = jax.nn.silu(jnp.einsum('ecd,efd->ecf', disp, wi_gate))
                up = jnp.einsum('ecd,efd->ecf', disp, wi_up)
                expert_out = jnp.einsum('ecf,edf->ecd', gate * up, wo)
                tok_out = expert_out[eid, pos_c]
                out = out + jnp.where(valid[:, None], ew[:, None] * tok_out, 0.0)
            return out.reshape(B, S, D)
        key = jax.random.key(seed)
        k1, k2, k3, k4, k5 = jax.random.split(key, 5)
        B, S, D, F, E = (4, 256, 128, 512, 8)
        return {'x': jax.random.normal(k1, (B, S, D), dtype=jnp.float32), 'gate_w': jax.random.normal(k2, (E, D), dtype=jnp.float32) * 0.02, 'wi_gate': jax.random.normal(k3, (E, F, D), dtype=jnp.float32) * 0.02, 'wi_up': jax.random.normal(k4, (E, F, D), dtype=jnp.float32) * 0.02, 'wo': jax.random.normal(k5, (E, D, F), dtype=jnp.float32) * 0.02}
    _L0_ffn_all = _L0_ffn_setup()
    _L0_ffn_in = {k: v for k, v in _L0_ffn_all.items() if k in ('gate_w', 'wi_gate', 'wi_up', 'wo')}
    del _L0_ffn_all

    def _L1_attn_setup():
        import jax, jax.numpy as jnp
        import numpy as np
        D_MODEL = 128
        D_STATE = 16
        D_CONV = 4
        EXPAND = 2
        D_INNER = D_MODEL * EXPAND
        DT_RANK = max(1, D_MODEL // 16)
        BSZ, SEQ = (2, 256)
        LN_EPS = 1e-05

        def _silu(v):
            return v * jax.nn.sigmoid(v)

        def _selective_scan(u, delta, A, B_s, C_s, D):
            b, l, d = u.shape
            n = A.shape[1]
            h0 = jnp.zeros((b, d, n), dtype=u.dtype)
            sw = lambda a: jnp.swapaxes(a, 0, 1)

            def step(h, inp):
                dt_t, u_t, b_t, c_t = inp
                dA = jnp.exp(dt_t[..., None] * A)
                h = dA * h + dt_t[..., None] * b_t[:, None, :] * u_t[..., None]
                y = jnp.einsum('bdn,bn->bd', h, c_t)
                return (h, y)
            _, ys = jax.lax.scan(step, h0, (sw(delta), sw(u), sw(B_s), sw(C_s)))
            return jnp.swapaxes(ys, 0, 1) + u * D[None, None, :]
        key = jax.random.key(seed)
        ks = jax.random.split(key, 9)
        x = jax.random.normal(ks[0], (BSZ, SEQ, D_MODEL), dtype=jnp.float32)
        W_in = jax.random.normal(ks[1], (2 * D_INNER + 2 * D_STATE + DT_RANK, D_MODEL), dtype=jnp.float32) * 0.02
        W_dt = jax.random.normal(ks[2], (D_INNER, DT_RANK), dtype=jnp.float32) * 0.1
        b_dt = jax.random.uniform(ks[3], (D_INNER,), minval=-4.0, maxval=-1.0, dtype=jnp.float32)
        A_log = jnp.log(jnp.broadcast_to(jnp.arange(1, D_STATE + 1, dtype=jnp.float32), (D_INNER, D_STATE)))
        D = jnp.ones((D_INNER,), dtype=jnp.float32)
        conv_w = jax.random.normal(ks[4], (D_INNER, 1, D_CONV), dtype=jnp.float32) * 0.3
        conv_b = jax.random.normal(ks[5], (D_INNER,), dtype=jnp.float32) * 0.1
        W_out = jax.random.normal(ks[6], (D_MODEL, D_INNER), dtype=jnp.float32) * 0.02
        ln_g = jnp.ones((D_MODEL,), dtype=jnp.float32)
        ln_b = jnp.zeros((D_MODEL,), dtype=jnp.float32)
        return {'x': x, 'W_in': W_in, 'W_dt': W_dt, 'b_dt': b_dt, 'A_log': A_log, 'D': D, 'conv_w': conv_w, 'conv_b': conv_b, 'W_out': W_out, 'ln_g': ln_g, 'ln_b': ln_b}
    _L1_attn_all = _L1_attn_setup()
    _L1_attn_in = {k: v for k, v in _L1_attn_all.items() if k in ('W_in', 'W_dt', 'b_dt', 'A_log', 'D', 'conv_w', 'conv_b', 'W_out', 'ln_g', 'ln_b')}
    del _L1_attn_all

    def _L1_xattn_setup():
        import jax, jax.numpy as jnp
        import numpy as np
        UNITS = 128
        NUM_HEADS = 8

        def _split_heads(x, n):
            B, S, D = x.shape
            return x.reshape(B, S, n, D // n).transpose(0, 2, 1, 3)
        key = jax.random.key(seed)
        k1, k2, k3 = jax.random.split(key, 3)
        B, S = (8, 128)
        memory = jax.random.normal(k1, (B, S, 2 * UNITS), dtype=jnp.float32)
        query = jax.random.normal(k2, (B, S, UNITS), dtype=jnp.float32)
        seq_mask = jax.random.randint(k3, (B, S), 0, 2, dtype=jnp.int32)
        b = jnp.zeros((1,), dtype=jnp.float32)
        return {'memory': memory, 'query': query, 'seq_mask': seq_mask, 'b': b}
    _L1_xattn_all = _L1_xattn_setup()
    _L1_xattn_in = {k: v for k, v in _L1_xattn_all.items() if k in ('b',)}
    del _L1_xattn_all

    def _L1_ffn_setup():
        import jax, jax.numpy as jnp
        import numpy as np
        DIM = 128
        INTER = 64
        E = 8
        TOP_K = 2
        ROUTE_SCALE = 1.0
        key = jax.random.key(seed)
        ks = jax.random.split(key, 8)
        s_d = 1.0 / np.sqrt(DIM)
        s_f = 1.0 / np.sqrt(INTER)
        x = jax.random.normal(ks[0], (2, 256, DIM), dtype=jnp.float32)
        gate_w = jax.random.uniform(ks[1], (E, DIM), jnp.float32, -s_d, s_d)
        wg = jax.random.uniform(ks[2], (E, INTER, DIM), jnp.float32, -s_d, s_d)
        wu = jax.random.uniform(ks[3], (E, INTER, DIM), jnp.float32, -s_d, s_d)
        wd = jax.random.uniform(ks[4], (E, DIM, INTER), jnp.float32, -s_f, s_f)
        sg = jax.random.uniform(ks[5], (INTER, DIM), jnp.float32, -s_d, s_d)
        su = jax.random.uniform(ks[6], (INTER, DIM), jnp.float32, -s_d, s_d)
        sd = jax.random.uniform(ks[7], (DIM, INTER), jnp.float32, -s_f, s_f)
        return {'x': x, 'gate_w': gate_w, 'wg': wg, 'wu': wu, 'wd': wd, 'sg': sg, 'su': su, 'sd': sd}
    _L1_ffn_all = _L1_ffn_setup()
    _L1_ffn_in = {k: v for k, v in _L1_ffn_all.items() if k in ('gate_w', 'wg', 'wu', 'wd', 'sg', 'su', 'sd')}
    del _L1_ffn_all

    def _L2_attn_setup():
        import jax, jax.numpy as jnp
        import numpy as np
        EMBED_DIM = 128
        NUM_HEADS = 16
        HEAD_DIM = EMBED_DIM // NUM_HEADS

        def _kernel_exp(x):
            return jnp.exp(x - jnp.max(x, axis=-1, keepdims=True))
        key = jax.random.key(seed)
        ks = jax.random.split(key, 9)
        s = 1.0 / np.sqrt(EMBED_DIM)
        inp = {'x': jax.random.normal(ks[0], (4, 1024, EMBED_DIM), dtype=jnp.float32)}
        for i, name in enumerate(['q', 'k', 'v', 'o']):
            inp[f'W{name}'] = jax.random.uniform(ks[1 + 2 * i], (EMBED_DIM, EMBED_DIM), jnp.float32, -s, s)
            inp[f'b{name}'] = jax.random.uniform(ks[2 + 2 * i], (EMBED_DIM,), jnp.float32, -s, s)
        return inp
    _L2_attn_all = _L2_attn_setup()
    _L2_attn_in = {k: v for k, v in _L2_attn_all.items() if k in ('Wq', 'bq', 'Wk', 'bk', 'Wv', 'bv', 'Wo', 'bo')}
    del _L2_attn_all

    def _L2_xattn_setup():
        import jax, jax.numpy as jnp
        import numpy as np
        NUM_HEADS = 16
        key = jax.random.key(seed)
        ks = jax.random.split(key, 5)
        dim = 128
        B, N, N_c = (4, 128, 32)
        x = jax.random.normal(ks[0], (B, N, dim), dtype=jnp.float32)
        context = jax.random.normal(ks[1], (B, N_c, 2 * dim), dtype=jnp.float32)
        w_qkv = jax.random.normal(ks[2], (3 * dim, dim), dtype=jnp.float32) * 0.02
        w_proj = jax.random.normal(ks[3], (dim, dim), dtype=jnp.float32) * 0.02
        b_proj = jax.random.normal(ks[4], (dim,), dtype=jnp.float32) * 0.02
        return {'x': x, 'context': context, 'w_qkv': w_qkv, 'w_proj': w_proj, 'b_proj': b_proj}
    _L2_xattn_all = _L2_xattn_setup()
    _L2_xattn_in = {k: v for k, v in _L2_xattn_all.items() if k in ('w_qkv', 'w_proj', 'b_proj')}
    del _L2_xattn_all

    def _L2_ffn_setup():
        import jax, jax.numpy as jnp
        import numpy as np
        HIDDEN = 128
        N_EXPERTS = 8
        TOP_K = 2
        INTER = 176
        N_SHARED = 2
        SCALE = 1.0
        key = jax.random.key(seed)
        ks = jax.random.split(key, 9)
        s_h = 1.0 / np.sqrt(HIDDEN)
        s_i = 1.0 / np.sqrt(INTER)
        x = jax.random.normal(ks[0], (2, 256, HIDDEN), dtype=jnp.float32)
        gate_w = jax.random.uniform(ks[1], (N_EXPERTS, HIDDEN), jnp.float32, -s_h, s_h)
        wg = jax.random.uniform(ks[2], (N_EXPERTS, HIDDEN, INTER), jnp.float32, -s_h, s_h)
        wu = jax.random.uniform(ks[3], (N_EXPERTS, HIDDEN, INTER), jnp.float32, -s_h, s_h)
        wd = jax.random.uniform(ks[4], (N_EXPERTS, INTER, HIDDEN), jnp.float32, -s_i, s_i)
        si = INTER * N_SHARED
        s_si = 1.0 / np.sqrt(si)
        swg = jax.random.uniform(ks[5], (HIDDEN, si), jnp.float32, -s_h, s_h)
        swu = jax.random.uniform(ks[6], (HIDDEN, si), jnp.float32, -s_h, s_h)
        swd = jax.random.uniform(ks[7], (si, HIDDEN), jnp.float32, -s_si, s_si)
        return {'x': x, 'gate_w': gate_w, 'wg': wg, 'wu': wu, 'wd': wd, 'swg': swg, 'swu': swu, 'swd': swd}
    _L2_ffn_all = _L2_ffn_setup()
    _L2_ffn_in = {k: v for k, v in _L2_ffn_all.items() if k in ('gate_w', 'wg', 'wu', 'wd', 'swg', 'swu', 'swd')}
    del _L2_ffn_all

    def _L3_attn_setup():
        import jax, jax.numpy as jnp
        import numpy as np
        B, S, D, H = (2, 256, 128, 16)
        DK = D // H
        key = jax.random.key(seed)
        ks = jax.random.split(key, 9)
        s = 0.02
        return {'embeddings': jax.random.normal(ks[0], (B, S, D), jnp.float32), 'Wq': jax.random.normal(ks[1], (H, D, DK), jnp.float32) * s, 'bq': jax.random.normal(ks[2], (H, DK), jnp.float32) * s, 'Wk': jax.random.normal(ks[3], (H, D, DK), jnp.float32) * s, 'bk': jax.random.normal(ks[4], (H, DK), jnp.float32) * s, 'Wv': jax.random.normal(ks[5], (H, D, DK), jnp.float32) * s, 'bv': jax.random.normal(ks[6], (H, DK), jnp.float32) * s, 'Wo': jax.random.normal(ks[7], (D, D), jnp.float32) * s, 'bo': jax.random.normal(ks[8], (D,), jnp.float32) * s}
    _L3_attn_all = _L3_attn_setup()
    _L3_attn_in = {k: v for k, v in _L3_attn_all.items() if k in ('Wq', 'bq', 'Wk', 'bk', 'Wv', 'bv', 'Wo', 'bo')}
    del _L3_attn_all

    def _L3_xattn_setup():
        import jax, jax.numpy as jnp
        import numpy as np
        B, L, P = (4, 512, 128)
        D_MODEL = 128
        D_GLOBAL = 256
        HEADDIM = 32
        EPSILON = 0.001
        RMS_EPS = 1e-05

        def rmsnorm(x, g, eps=RMS_EPS):
            var = jnp.mean(jnp.square(x), axis=-1, keepdims=True)
            return x * jax.lax.rsqrt(var + eps) * g

        def _hnet_depool(h, h_patch_full, patch_lens):
            h_patch = h_patch_full[..., :D_MODEL]
            bsz, plen = (h_patch.shape[0], h_patch.shape[1])
            seqlen = h.shape[1]
            logp = jnp.full((bsz, plen), -EPSILON, dtype=jnp.float32)
            bidx = jnp.cumsum(patch_lens, axis=1) - 1
            boundary_mask = jnp.zeros((bsz, seqlen), dtype=jnp.int32)
            boundary_mask = boundary_mask.at[jnp.arange(bsz)[:, None], bidx].set(1)
            dt = (-jnp.log(-jnp.expm1(logp))).astype(h_patch.dtype)
            x = h_patch / dt[..., None]
            n_heads = D_MODEL // HEADDIM
            A = -jnp.ones((n_heads,), dtype=jnp.float32)
            bcoef = jnp.exp(logp).astype(h_patch.dtype)
            x4 = x.reshape(bsz, plen, n_heads, HEADDIM)
            a = jnp.exp(dt[:, :, None] * A[None, None, :])
            u = (dt * bcoef)[:, :, None, None] * x4
            a_b = jnp.broadcast_to(a[..., None], u.shape)

            def comb(lft, rgt):
                aL, uL = lft
                aR, uR = rgt
                return (aL * aR, uL * aR + uR)
            _, s = jax.lax.associative_scan(comb, (a_b, u), axis=1)
            depool = s.reshape(bsz, plen, D_MODEL)
            plug = jnp.clip(jnp.cumsum(boundary_mask, axis=1) - 1, 0, plen - 1)
            depool_out = depool[jnp.arange(bsz)[:, None], plug]
            return depool_out + h
        key = jax.random.key(seed)
        k1, k2, k3, k4 = jax.random.split(key, 4)
        embeds = jax.random.normal(k1, (B, L, D_MODEL), dtype=jnp.float32)
        patch_embeds = jax.random.normal(k2, (B, P, D_GLOBAL), dtype=jnp.float32)
        patch_lens = jnp.full((B, P), L // P, dtype=jnp.int64)
        W_in = jax.random.normal(k3, (D_MODEL, D_MODEL), dtype=jnp.float32) * 0.02
        b_in = jnp.zeros((D_MODEL,), dtype=jnp.float32)
        g_res = jnp.ones((D_MODEL,), dtype=jnp.float32)
        g_init = jnp.ones((D_GLOBAL,), dtype=jnp.float32)
        return {'embeds': embeds, 'patch_embeds': patch_embeds, 'patch_lens': patch_lens, 'W_in': W_in, 'b_in': b_in, 'g_res': g_res, 'g_init': g_init}
    _L3_xattn_all = _L3_xattn_setup()
    _L3_xattn_in = {k: v for k, v in _L3_xattn_all.items() if k in ('W_in', 'b_in', 'g_res', 'g_init')}
    del _L3_xattn_all

    def _L3_ffn_setup():
        import jax, jax.numpy as jnp
        import numpy as np
        B, S, D = (1, 256, 128)
        F = 176
        E = 16
        K = 2
        CAP_FACTOR = 1.25

        def _mlp(h, wg, wu, wd):
            return jax.nn.silu(h @ wg) * (h @ wu) @ wd
        key = jax.random.key(seed)
        ks = jax.random.split(key, 10)
        sd = 0.02
        return {'x': jax.random.normal(ks[0], (B, S, D), jnp.float32), 'router_w': jax.random.normal(ks[1], (D, E), jnp.float32) * sd, 'router_b': jnp.zeros((E,), jnp.float32), 'w_gate': jax.random.normal(ks[2], (E, D, F), jnp.float32) * sd, 'w_up': jax.random.normal(ks[3], (E, D, F), jnp.float32) * sd, 'w_down': jax.random.normal(ks[4], (E, F, D), jnp.float32) * sd, 'sw_gate': jax.random.normal(ks[5], (D, F), jnp.float32) * sd, 'sw_up': jax.random.normal(ks[6], (D, F), jnp.float32) * sd, 'sw_down': jax.random.normal(ks[7], (F, D), jnp.float32) * sd}
    _L3_ffn_all = _L3_ffn_setup()
    _L3_ffn_in = {k: v for k, v in _L3_ffn_all.items() if k in ('router_w', 'router_b', 'w_gate', 'w_up', 'w_down', 'sw_gate', 'sw_up', 'sw_down')}
    del _L3_ffn_all
    return {'x': x, 'ctx_2048': ctx_2048, 'mask_BxS2_fk1': mask_BxS2_fk1, 'mask_BxS2_ik0': mask_BxS2_ik0, 'mask_BxS2_if0': mask_BxS2_if0, 'L0_attn_Wq': _L0_attn_in['Wq'], 'L0_attn_bq': _L0_attn_in['bq'], 'L0_attn_Wk': _L0_attn_in['Wk'], 'L0_attn_bk': _L0_attn_in['bk'], 'L0_attn_Wv': _L0_attn_in['Wv'], 'L0_attn_bv': _L0_attn_in['bv'], 'L0_attn_Wo': _L0_attn_in['Wo'], 'L0_attn_bo': _L0_attn_in['bo'], 'L0_xattn_W_src': _L0_xattn_in['W_src'], 'L0_xattn_b_src': _L0_xattn_in['b_src'], 'L0_xattn_W_tgt': _L0_xattn_in['W_tgt'], 'L0_xattn_b_tgt': _L0_xattn_in['b_tgt'], 'L0_xattn_W_out': _L0_xattn_in['W_out'], 'L0_xattn_b_out': _L0_xattn_in['b_out'], 'L0_ffn_gate_w': _L0_ffn_in['gate_w'], 'L0_ffn_wi_gate': _L0_ffn_in['wi_gate'], 'L0_ffn_wi_up': _L0_ffn_in['wi_up'], 'L0_ffn_wo': _L0_ffn_in['wo'], 'L1_attn_W_in': _L1_attn_in['W_in'], 'L1_attn_W_dt': _L1_attn_in['W_dt'], 'L1_attn_b_dt': _L1_attn_in['b_dt'], 'L1_attn_A_log': _L1_attn_in['A_log'], 'L1_attn_D': _L1_attn_in['D'], 'L1_attn_conv_w': _L1_attn_in['conv_w'], 'L1_attn_conv_b': _L1_attn_in['conv_b'], 'L1_attn_W_out': _L1_attn_in['W_out'], 'L1_attn_ln_g': _L1_attn_in['ln_g'], 'L1_attn_ln_b': _L1_attn_in['ln_b'], 'L1_xattn_b': _L1_xattn_in['b'], 'L1_ffn_gate_w': _L1_ffn_in['gate_w'], 'L1_ffn_wg': _L1_ffn_in['wg'], 'L1_ffn_wu': _L1_ffn_in['wu'], 'L1_ffn_wd': _L1_ffn_in['wd'], 'L1_ffn_sg': _L1_ffn_in['sg'], 'L1_ffn_su': _L1_ffn_in['su'], 'L1_ffn_sd': _L1_ffn_in['sd'], 'L2_attn_Wq': _L2_attn_in['Wq'], 'L2_attn_bq': _L2_attn_in['bq'], 'L2_attn_Wk': _L2_attn_in['Wk'], 'L2_attn_bk': _L2_attn_in['bk'], 'L2_attn_Wv': _L2_attn_in['Wv'], 'L2_attn_bv': _L2_attn_in['bv'], 'L2_attn_Wo': _L2_attn_in['Wo'], 'L2_attn_bo': _L2_attn_in['bo'], 'L2_xattn_w_qkv': _L2_xattn_in['w_qkv'], 'L2_xattn_w_proj': _L2_xattn_in['w_proj'], 'L2_xattn_b_proj': _L2_xattn_in['b_proj'], 'L2_ffn_gate_w': _L2_ffn_in['gate_w'], 'L2_ffn_wg': _L2_ffn_in['wg'], 'L2_ffn_wu': _L2_ffn_in['wu'], 'L2_ffn_wd': _L2_ffn_in['wd'], 'L2_ffn_swg': _L2_ffn_in['swg'], 'L2_ffn_swu': _L2_ffn_in['swu'], 'L2_ffn_swd': _L2_ffn_in['swd'], 'L3_attn_Wq': _L3_attn_in['Wq'], 'L3_attn_bq': _L3_attn_in['bq'], 'L3_attn_Wk': _L3_attn_in['Wk'], 'L3_attn_bk': _L3_attn_in['bk'], 'L3_attn_Wv': _L3_attn_in['Wv'], 'L3_attn_bv': _L3_attn_in['bv'], 'L3_attn_Wo': _L3_attn_in['Wo'], 'L3_attn_bo': _L3_attn_in['bo'], 'L3_xattn_W_in': _L3_xattn_in['W_in'], 'L3_xattn_b_in': _L3_xattn_in['b_in'], 'L3_xattn_g_res': _L3_xattn_in['g_res'], 'L3_xattn_g_init': _L3_xattn_in['g_init'], 'L3_ffn_router_w': _L3_ffn_in['router_w'], 'L3_ffn_router_b': _L3_ffn_in['router_b'], 'L3_ffn_w_gate': _L3_ffn_in['w_gate'], 'L3_ffn_w_up': _L3_ffn_in['w_up'], 'L3_ffn_w_down': _L3_ffn_in['w_down'], 'L3_ffn_sw_gate': _L3_ffn_in['sw_gate'], 'L3_ffn_sw_up': _L3_ffn_in['sw_up'], 'L3_ffn_sw_down': _L3_ffn_in['sw_down']}

def reference(x, ctx_2048, mask_BxS2_fk1, mask_BxS2_ik0, mask_BxS2_if0, L0_attn_Wq, L0_attn_bq, L0_attn_Wk, L0_attn_bk, L0_attn_Wv, L0_attn_bv, L0_attn_Wo, L0_attn_bo, L0_xattn_W_src, L0_xattn_b_src, L0_xattn_W_tgt, L0_xattn_b_tgt, L0_xattn_W_out, L0_xattn_b_out, L0_ffn_gate_w, L0_ffn_wi_gate, L0_ffn_wi_up, L0_ffn_wo, L1_attn_W_in, L1_attn_W_dt, L1_attn_b_dt, L1_attn_A_log, L1_attn_D, L1_attn_conv_w, L1_attn_conv_b, L1_attn_W_out, L1_attn_ln_g, L1_attn_ln_b, L1_xattn_b, L1_ffn_gate_w, L1_ffn_wg, L1_ffn_wu, L1_ffn_wd, L1_ffn_sg, L1_ffn_su, L1_ffn_sd, L2_attn_Wq, L2_attn_bq, L2_attn_Wk, L2_attn_bk, L2_attn_Wv, L2_attn_bv, L2_attn_Wo, L2_attn_bo, L2_xattn_w_qkv, L2_xattn_w_proj, L2_xattn_b_proj, L2_ffn_gate_w, L2_ffn_wg, L2_ffn_wu, L2_ffn_wd, L2_ffn_swg, L2_ffn_swu, L2_ffn_swd, L3_attn_Wq, L3_attn_bq, L3_attn_Wk, L3_attn_bk, L3_attn_Wv, L3_attn_bv, L3_attn_Wo, L3_attn_bo, L3_xattn_W_in, L3_xattn_b_in, L3_xattn_g_res, L3_xattn_g_init, L3_ffn_router_w, L3_ffn_router_b, L3_ffn_w_gate, L3_ffn_w_up, L3_ffn_w_down, L3_ffn_sw_gate, L3_ffn_sw_up, L3_ffn_sw_down):
    import jax
    import jax.numpy as jnp

    def _L0_attn_ref(x, Wq, bq, Wk, bk, Wv, bv, Wo, bo):
        import jax, jax.numpy as jnp
        import numpy as np
        DIM = 128
        N_HEADS = 16
        HEAD_DIM = DIM // N_HEADS

        def apply_rope(x):
            B, T, H, D = x.shape
            half = D // 2
            x1, x2 = (x[..., :half], x[..., half:])
            theta = 1.0 / 10000.0 ** (jnp.arange(0, half, 2, dtype=jnp.float32) / half)
            pos = jnp.arange(T, dtype=jnp.float32)
            freq = pos[:, None] * theta[None, :]
            sin = jnp.sin(freq)[None, :, None, :]
            cos = jnp.cos(freq)[None, :, None, :]
            x1e, x1o = (x1[..., ::2], x1[..., 1::2])
            x2e, x2o = (x2[..., ::2], x2[..., 1::2])
            x1r = jnp.concatenate([x1e * cos - x1o * sin, x1e * sin + x1o * cos], axis=-1)
            x2r = jnp.concatenate([x2e * cos - x2o * sin, x2e * sin + x2o * cos], axis=-1)
            return jnp.concatenate([x1r, x2r], axis=-1)
        B, T, C = x.shape
        H, D = (N_HEADS, HEAD_DIM)
        q = (x @ Wq + bq).reshape(B, T, H, D).transpose(0, 2, 1, 3)
        k = x @ Wk + bk
        v = x @ Wv + bv
        q = apply_rope(q)
        k = apply_rope(k[:, None])[:, 0]
        scores = jnp.einsum('bhtd,bsd->bhts', q, k) / jnp.sqrt(jnp.float32(D))
        mask = jnp.tril(jnp.ones((T, T), dtype=bool))
        scores = jnp.where(mask[None, None], scores, -jnp.inf)
        probs = jax.nn.softmax(scores, axis=-1)
        attn = jnp.einsum('bhts,bsd->bhtd', probs, v)
        attn = attn.transpose(0, 2, 1, 3).reshape(B, T, C)
        return attn @ Wo + bo

    def _L0_xattn_ref(src, tgt, src_mask, tgt_mask, W_src, b_src, W_tgt, b_tgt, W_out, b_out):
        import jax, jax.numpy as jnp
        import numpy as np
        B, S, T = (32, 64, 64)
        SRC_SIZE, TGT_SIZE, OUT_SIZE, NUM_HEAD = (256, 128, 128, 8)
        HEAD_DIM = OUT_SIZE // NUM_HEAD
        b, s, _ = src.shape
        t = tgt.shape[1]
        src_trans = jnp.einsum('bsf,of->bso', src, W_src) + b_src
        tgt_trans = jnp.einsum('btf,of->bto', tgt, W_tgt) + b_tgt
        src_trans = src_trans * src_mask[:, :, None]
        tgt_trans = tgt_trans * tgt_mask[:, :, None]
        src_key, src_val = jnp.split(src_trans, 2, axis=2)
        k = src_key.reshape(b, s, NUM_HEAD, HEAD_DIM)
        v = src_val.reshape(b, s, NUM_HEAD, HEAD_DIM)
        q = tgt_trans.reshape(b, t, NUM_HEAD, HEAD_DIM)
        scores = jnp.einsum('bthd,bshd->bhts', q, k) / np.sqrt(HEAD_DIM)
        scores = jnp.where(src_mask[:, None, None, :] == 0, -jnp.inf, scores)
        attn = jax.nn.softmax(scores, axis=-1)
        tgt_update = jnp.einsum('bhts,bshd->bthd', attn, v).reshape(b, t, OUT_SIZE)
        cat_tgt = jnp.concatenate([tgt, tgt_update], axis=2)
        return jnp.einsum('btf,of->bto', cat_tgt, W_out) + b_out

    def _L0_ffn_ref(x, gate_w, wi_gate, wi_up, wo):
        import jax, jax.numpy as jnp
        import numpy as np
        TOP_K = 2
        CAPACITY_FACTOR = 1.25

        def _moe_forward(x, gate_w, wi_gate, wi_up, wo):
            B, S, D = x.shape
            E = wi_gate.shape[0]
            N = B * S
            capacity = max(int(N / E * CAPACITY_FACTOR), 1)
            x_flat = x.reshape(N, D)
            router_logits = x_flat @ gate_w.T
            router_probs = jax.nn.softmax(router_logits, axis=-1)
            top_k_probs, top_k_idx = jax.lax.top_k(router_probs, TOP_K)
            top_k_probs = top_k_probs / jnp.sum(top_k_probs, axis=-1, keepdims=True)
            out = jnp.zeros_like(x_flat)
            experts = jnp.arange(E, dtype=jnp.int32)
            for k in range(TOP_K):
                eid = top_k_idx[:, k]
                ew = top_k_probs[:, k]
                onehot = (eid[:, None] == experts[None, :]).astype(jnp.int32)
                pos_all = jnp.cumsum(onehot, axis=0) - 1
                pos = jnp.take_along_axis(pos_all, eid[:, None].astype(jnp.int32), axis=1)[:, 0]
                valid = pos < capacity
                pos_c = jnp.where(valid, pos, 0)
                disp = jnp.zeros((E, capacity, D), x_flat.dtype).at[eid, pos_c].add(jnp.where(valid[:, None], x_flat, 0.0))
                gate = jax.nn.silu(jnp.einsum('ecd,efd->ecf', disp, wi_gate))
                up = jnp.einsum('ecd,efd->ecf', disp, wi_up)
                expert_out = jnp.einsum('ecf,edf->ecd', gate * up, wo)
                tok_out = expert_out[eid, pos_c]
                out = out + jnp.where(valid[:, None], ew[:, None] * tok_out, 0.0)
            return out.reshape(B, S, D)
        return _moe_forward(x, gate_w, wi_gate, wi_up, wo)

    def _L1_attn_ref(x, W_in, W_dt, b_dt, A_log, D, conv_w, conv_b, W_out, ln_g, ln_b):
        import jax, jax.numpy as jnp
        import numpy as np
        D_MODEL = 128
        D_STATE = 16
        D_CONV = 4
        EXPAND = 2
        D_INNER = D_MODEL * EXPAND
        DT_RANK = max(1, D_MODEL // 16)
        BSZ, SEQ = (2, 256)
        LN_EPS = 1e-05

        def _silu(v):
            return v * jax.nn.sigmoid(v)

        def _selective_scan(u, delta, A, B_s, C_s, D):
            b, l, d = u.shape
            n = A.shape[1]
            h0 = jnp.zeros((b, d, n), dtype=u.dtype)
            sw = lambda a: jnp.swapaxes(a, 0, 1)

            def step(h, inp):
                dt_t, u_t, b_t, c_t = inp
                dA = jnp.exp(dt_t[..., None] * A)
                h = dA * h + dt_t[..., None] * b_t[:, None, :] * u_t[..., None]
                y = jnp.einsum('bdn,bn->bd', h, c_t)
                return (h, y)
            _, ys = jax.lax.scan(step, h0, (sw(delta), sw(u), sw(B_s), sw(C_s)))
            return jnp.swapaxes(ys, 0, 1) + u * D[None, None, :]
        residual = x
        b, l, _ = x.shape
        proj = jnp.einsum('bld,od->blo', x, W_in)
        x_s, z, B_s, C_s, dt = jnp.split(proj, [D_INNER, 2 * D_INNER, 2 * D_INNER + D_STATE, 2 * D_INNER + 2 * D_STATE], axis=-1)
        xc = jnp.transpose(x_s, (0, 2, 1))
        xc = jax.lax.conv_general_dilated(xc, conv_w, window_strides=(1,), padding=[(D_CONV - 1, D_CONV - 1)], feature_group_count=D_INNER, dimension_numbers=('NCH', 'OIH', 'NCH'))
        xc = xc[..., :l] + conv_b[None, :, None]
        x_s = _silu(jnp.transpose(xc, (0, 2, 1)))
        dt = jax.nn.softplus(jnp.einsum('blr,dr->bld', dt, W_dt) + b_dt)
        A = -jnp.exp(A_log)
        y = _selective_scan(x_s, dt, A, B_s, C_s, D)
        y = y * _silu(z)
        out = residual + jnp.einsum('bld,od->blo', y, W_out)
        mu = jnp.mean(out, axis=-1, keepdims=True)
        var = jnp.mean(jnp.square(out - mu), axis=-1, keepdims=True)
        return (out - mu) * jax.lax.rsqrt(var + LN_EPS) * ln_g + ln_b

    def _L1_xattn_ref(memory, query, seq_mask, b):
        import jax, jax.numpy as jnp
        import numpy as np
        UNITS = 128
        NUM_HEADS = 8

        def _split_heads(x, n):
            B, S, D = x.shape
            return x.reshape(B, S, n, D // n).transpose(0, 2, 1, 3)
        H = NUM_HEADS
        depth = UNITS // H
        Q = _split_heads(query, H) * depth ** (-0.5)
        k_mem, v_mem = jnp.split(memory, 2, axis=2)
        K = _split_heads(k_mem, H)
        V = _split_heads(v_mem, H)
        logits = jnp.einsum('bhqd,bhkd->bhqk', Q, K) + b[0]
        mask = seq_mask.astype(jnp.float32)[:, None, None, :]
        logits = logits + -1e+30 * (1.0 - mask)
        weights = jax.nn.softmax(logits, axis=-1)
        out = jnp.einsum('bhqk,bhkd->bhqd', weights, V)
        B, _, S, _ = out.shape
        return out.transpose(0, 2, 1, 3).reshape(B, S, UNITS)

    def _L1_ffn_ref(x, gate_w, wg, wu, wd, sg, su, sd):
        import jax, jax.numpy as jnp
        import numpy as np
        DIM = 128
        INTER = 64
        E = 8
        TOP_K = 2
        ROUTE_SCALE = 1.0
        B, S, D = x.shape
        xf = x.reshape(-1, D)
        N = xf.shape[0]
        scores = jax.nn.softmax(xf @ gate_w.T, axis=-1)
        _, idx = jax.lax.top_k(scores, TOP_K)
        weights = jnp.take_along_axis(scores, idx, axis=-1) * ROUTE_SCALE
        cw = jnp.zeros((N, E), dtype=xf.dtype)
        cw = cw.at[jnp.arange(N)[:, None], idx].add(weights)
        g = jnp.einsum('nd,efd->nef', xf, wg)
        u = jnp.einsum('nd,efd->nef', xf, wu)
        h = jax.nn.silu(g) * u
        y = jnp.einsum('nef,edf->ned', h, wd)
        routed = jnp.einsum('ned,ne->nd', y, cw)
        shared = jax.nn.silu(xf @ sg.T) * (xf @ su.T) @ sd.T
        return (routed + shared).reshape(B, S, D)

    def _L2_attn_ref(x, Wq, bq, Wk, bk, Wv, bv, Wo, bo):
        import jax, jax.numpy as jnp
        import numpy as np
        EMBED_DIM = 128
        NUM_HEADS = 16
        HEAD_DIM = EMBED_DIM // NUM_HEADS

        def _kernel_exp(x):
            return jnp.exp(x - jnp.max(x, axis=-1, keepdims=True))
        b, s, e = x.shape

        def proj(W, bias):
            return (x @ W.T + bias).reshape(b, s, NUM_HEADS, HEAD_DIM).transpose(0, 2, 1, 3)
        q = proj(Wq, bq)
        k = proj(Wk, bk)
        v = proj(Wv, bv)
        q_kern = _kernel_exp(q)
        k_kern = _kernel_exp(k)
        kv = jnp.einsum('bhsd,bhse->bhde', k_kern, v)
        k_sum = jnp.sum(k_kern, axis=2)
        denom = jnp.einsum('bhqd,bhd->bhq', q_kern, k_sum) + 1e-06
        y = jnp.einsum('bhqd,bhde->bhqe', q_kern, kv) / denom[..., None]
        y = y.transpose(0, 2, 1, 3).reshape(b, s, e)
        return y @ Wo.T + bo

    def _L2_xattn_ref(x, context, w_qkv, w_proj, b_proj):
        import jax, jax.numpy as jnp
        import numpy as np
        NUM_HEADS = 16
        B, N, C = x.shape
        H = NUM_HEADS
        D = C // H
        scale = D ** (-0.5)
        qkv = (x @ w_qkv.T).reshape(B, N, 3, H, D).transpose(2, 0, 3, 1, 4)
        q, k, v = (qkv[0], qkv[1], qkv[2])
        N_c = context.shape[1]
        kv = context.reshape(B, N_c, 2, H, D).transpose(2, 0, 3, 1, 4)
        extra_k, extra_v = (kv[0], kv[1])
        k = jnp.concatenate([extra_k, k], axis=2)
        v = jnp.concatenate([extra_v, v], axis=2)
        dtype = q.dtype
        attn = jnp.einsum('bhnd,bhmd->bhnm', q * scale, k).astype(jnp.float32)
        attn = jax.nn.softmax(attn, axis=-1).astype(dtype)
        out = jnp.einsum('bhnm,bhmd->bhnd', attn, v)
        out = out.transpose(0, 2, 1, 3).reshape(B, N, C)
        return out @ w_proj.T + b_proj

    def _L2_ffn_ref(x, gate_w, wg, wu, wd, swg, swu, swd):
        import jax, jax.numpy as jnp
        import numpy as np
        HIDDEN = 128
        N_EXPERTS = 8
        TOP_K = 2
        INTER = 176
        N_SHARED = 2
        SCALE = 1.0
        B, S, H = x.shape
        xf = x.reshape(-1, H)
        T = xf.shape[0]
        logits = xf.astype(jnp.float32) @ gate_w.astype(jnp.float32).T
        scores = jax.nn.softmax(logits, axis=-1)
        topw, topi = jax.lax.top_k(scores, TOP_K)
        denom = topw.sum(axis=-1, keepdims=True) + 1e-20
        topw = topw / denom * SCALE
        wdense = jnp.zeros((T, N_EXPERTS), jnp.float32).at[jnp.arange(T)[:, None], topi].set(topw)
        hg = jnp.einsum('th,ehi->eti', xf, wg)
        hu = jnp.einsum('th,ehi->eti', xf, wu)
        eo = jnp.einsum('eti,eih->eth', jax.nn.silu(hg) * hu, wd)
        y = jnp.einsum('te,eth->th', wdense, eo)
        shared = jax.nn.silu(xf @ swg) * (xf @ swu) @ swd
        return (y + shared).reshape(B, S, H)

    def _L3_attn_ref(embeddings, Wq, bq, Wk, bk, Wv, bv, Wo, bo):
        import jax, jax.numpy as jnp
        import numpy as np
        B, S, D, H = (2, 256, 128, 16)
        DK = D // H
        b, s, d = embeddings.shape
        dk = Wq.shape[-1]
        q = jnp.einsum('bsd,hdk->bhsk', embeddings, Wq) + bq[None, :, None, :]
        k = jnp.einsum('bsd,hdk->bhsk', embeddings, Wk) + bk[None, :, None, :]
        v = jnp.einsum('bsd,hdk->bhsk', embeddings, Wv) + bv[None, :, None, :]
        scores = jnp.einsum('bhqk,bhsk->bhqs', q, k) / jnp.sqrt(jnp.float32(dk))
        causal_mask = jnp.triu(jnp.ones((s, s), dtype=bool), k=1)
        scores = jnp.where(causal_mask, jnp.float32(-1000000000.0), scores)
        weights = jax.nn.softmax(scores, axis=-1)
        ctx = jnp.einsum('bhqs,bhsk->bhqk', weights, v)
        concat = ctx.transpose(0, 2, 1, 3).reshape(b, s, d)
        return concat @ Wo + bo

    def _L3_xattn_ref(embeds, patch_embeds, patch_lens, W_in, b_in, g_res, g_init):
        import jax, jax.numpy as jnp
        import numpy as np
        B, L, P = (4, 512, 128)
        D_MODEL = 128
        D_GLOBAL = 256
        HEADDIM = 32
        EPSILON = 0.001
        RMS_EPS = 1e-05

        def rmsnorm(x, g, eps=RMS_EPS):
            var = jnp.mean(jnp.square(x), axis=-1, keepdims=True)
            return x * jax.lax.rsqrt(var + eps) * g

        def _hnet_depool(h, h_patch_full, patch_lens):
            h_patch = h_patch_full[..., :D_MODEL]
            bsz, plen = (h_patch.shape[0], h_patch.shape[1])
            seqlen = h.shape[1]
            logp = jnp.full((bsz, plen), -EPSILON, dtype=jnp.float32)
            bidx = jnp.cumsum(patch_lens, axis=1) - 1
            boundary_mask = jnp.zeros((bsz, seqlen), dtype=jnp.int32)
            boundary_mask = boundary_mask.at[jnp.arange(bsz)[:, None], bidx].set(1)
            dt = (-jnp.log(-jnp.expm1(logp))).astype(h_patch.dtype)
            x = h_patch / dt[..., None]
            n_heads = D_MODEL // HEADDIM
            A = -jnp.ones((n_heads,), dtype=jnp.float32)
            bcoef = jnp.exp(logp).astype(h_patch.dtype)
            x4 = x.reshape(bsz, plen, n_heads, HEADDIM)
            a = jnp.exp(dt[:, :, None] * A[None, None, :])
            u = (dt * bcoef)[:, :, None, None] * x4
            a_b = jnp.broadcast_to(a[..., None], u.shape)

            def comb(lft, rgt):
                aL, uL = lft
                aR, uR = rgt
                return (aL * aR, uL * aR + uR)
            _, s = jax.lax.associative_scan(comb, (a_b, u), axis=1)
            depool = s.reshape(bsz, plen, D_MODEL)
            plug = jnp.clip(jnp.cumsum(boundary_mask, axis=1) - 1, 0, plen - 1)
            depool_out = depool[jnp.arange(bsz)[:, None], plug]
            return depool_out + h
        h = rmsnorm(embeds, g_res)
        h = jnp.einsum('bld,ed->ble', h, W_in) + b_in
        h_patch = rmsnorm(patch_embeds, g_init)
        return _hnet_depool(h, h_patch, patch_lens)

    def _L3_ffn_ref(x, router_w, router_b, w_gate, w_up, w_down, sw_gate, sw_up, sw_down):
        import jax, jax.numpy as jnp
        import numpy as np
        B, S, D = (1, 256, 128)
        F = 176
        E = 16
        K = 2
        CAP_FACTOR = 1.25

        def _mlp(h, wg, wu, wd):
            return jax.nn.silu(h @ wg) * (h @ wu) @ wd
        b, s, d = x.shape
        N = b * s
        NK = N * K
        C = int(np.ceil(CAP_FACTOR * NK / E))
        x_tokens = x.reshape(N, d)
        logits = x_tokens @ router_w + router_b
        probs = jax.nn.softmax(logits, axis=-1)
        vals, idx = jax.lax.top_k(probs, K)
        vals = vals / (jnp.sum(vals, axis=-1, keepdims=True) + 1e-09)
        idx_flat = idx.reshape(NK)
        vals_flat = vals.reshape(NK)
        oh_e = jax.nn.one_hot(idx_flat, E, dtype=x.dtype)
        pos = (jnp.cumsum(oh_e, axis=0) * oh_e).sum(axis=1) - 1
        within = (pos < C).astype(x.dtype)
        pos_c = jnp.clip(pos, 0, C - 1).astype(jnp.int32)
        token_ids = jnp.arange(NK) // K
        x_pair = x_tokens[token_ids] * within[:, None]
        expert_inputs = jnp.zeros((E, C, d), x.dtype).at[idx_flat, pos_c].add(x_pair)
        expert_outputs = jax.vmap(_mlp)(expert_inputs, w_gate, w_up, w_down)
        gathered = expert_outputs[idx_flat, pos_c] * (vals_flat * within)[:, None]
        output_tokens = gathered.reshape(N, K, d).sum(axis=1)
        return x + _mlp(x, sw_gate, sw_up, sw_down) + output_tokens.reshape(b, s, d)
    x = x + _L0_attn_ref(_layernorm(x, axis=-1), L0_attn_Wq, L0_attn_bq, L0_attn_Wk, L0_attn_bk, L0_attn_Wv, L0_attn_bv, L0_attn_Wo, L0_attn_bo)
    x = x + _L0_xattn_ref(ctx_2048, _layernorm(x, axis=-1), mask_BxS2_fk1, mask_BxS2_fk1, L0_xattn_W_src, L0_xattn_b_src, L0_xattn_W_tgt, L0_xattn_b_tgt, L0_xattn_W_out, L0_xattn_b_out)
    x = x + _L0_ffn_ref(_layernorm(x, axis=-1), L0_ffn_gate_w, L0_ffn_wi_gate, L0_ffn_wi_up, L0_ffn_wo)
    x = x + _L1_attn_ref(_layernorm(x, axis=-1), L1_attn_W_in, L1_attn_W_dt, L1_attn_b_dt, L1_attn_A_log, L1_attn_D, L1_attn_conv_w, L1_attn_conv_b, L1_attn_W_out, L1_attn_ln_g, L1_attn_ln_b)
    x = x + _L1_xattn_ref(ctx_2048, _layernorm(x, axis=-1), mask_BxS2_ik0, L1_xattn_b)
    x = x + _L1_ffn_ref(_layernorm(x, axis=-1), L1_ffn_gate_w, L1_ffn_wg, L1_ffn_wu, L1_ffn_wd, L1_ffn_sg, L1_ffn_su, L1_ffn_sd)
    x = x + _L2_attn_ref(_layernorm(x, axis=-1), L2_attn_Wq, L2_attn_bq, L2_attn_Wk, L2_attn_bk, L2_attn_Wv, L2_attn_bv, L2_attn_Wo, L2_attn_bo)
    x = x + _L2_xattn_ref(_layernorm(x, axis=-1), ctx_2048, L2_xattn_w_qkv, L2_xattn_w_proj, L2_xattn_b_proj)
    x = x + _L2_ffn_ref(_layernorm(x, axis=-1), L2_ffn_gate_w, L2_ffn_wg, L2_ffn_wu, L2_ffn_wd, L2_ffn_swg, L2_ffn_swu, L2_ffn_swd)
    x = x + _L3_attn_ref(_layernorm(x, axis=-1), L3_attn_Wq, L3_attn_bq, L3_attn_Wk, L3_attn_bk, L3_attn_Wv, L3_attn_bv, L3_attn_Wo, L3_attn_bo)
    x = x + _L3_xattn_ref(_layernorm(x, axis=-1), ctx_2048, mask_BxS2_if0, L3_xattn_W_in, L3_xattn_b_in, L3_xattn_g_res, L3_xattn_g_init)
    x = x + _L3_ffn_ref(_layernorm(x, axis=-1), L3_ffn_router_w, L3_ffn_router_b, L3_ffn_w_gate, L3_ffn_w_up, L3_ffn_w_down, L3_ffn_sw_gate, L3_ffn_sw_up, L3_ffn_sw_down)
    return x

_drawn_inputs = setup_inputs


def setup_inputs(seed=0):
    import zlib

    import numpy as np

    out = dict(_drawn_inputs(seed))
    spreads = {'L0_attn_bq': (0.0, 0.8),
     'L0_attn_bk': (0.0, 2.0),
     'L0_attn_bv': (0.0, 0.393),
     'L0_attn_bo': (0.0, 0.1),
     'L0_xattn_b_src': (0.0, 0.1),
     'L0_xattn_b_tgt': (0.0, 0.69),
     'L0_xattn_b_out': (0.0, 0.1),
     'L1_attn_D': (1.0, 0.6),
     'L1_attn_ln_g': (1.0, 0.2),
     'L1_attn_ln_b': (0.0, 0.1),
     'L3_xattn_b_in': (0.0, 0.274),
     'L3_xattn_g_res': (1.0, 0.6),
     'L3_xattn_g_init': (1.0, 0.2),
     'L3_ffn_router_b': (0.0, 0.8)}
    factors = {'L0_attn_Wq': 8.0,
     'L0_attn_Wk': 8.0,
     'L0_attn_Wv': 4.967,
     'L0_ffn_gate_w': 8.0,
     'L0_ffn_wi_gate': 8.0,
     'L0_ffn_wi_up': 8.0,
     'L0_ffn_wo': 8.0,
     'L1_attn_W_in': 8.0,
     'L1_attn_W_dt': 8.0,
     'L1_attn_b_dt': 8.0,
     'L1_attn_A_log': 8.0,
     'L1_attn_conv_w': 8.0,
     'L1_attn_conv_b': 8.0,
     'L1_attn_W_out': 8.0,
     'L1_ffn_gate_w': 4.889,
     'L1_ffn_wg': 4.416,
     'L1_ffn_wu': 4.318,
     'L1_ffn_wd': 4.304,
     'L2_attn_Wq': 24.987,
     'L2_attn_bq': 64.0,
     'L2_attn_Wk': 26.242,
     'L2_attn_bk': 55.948,
     'L2_attn_bv': 4.762,
     'L2_attn_bo': 2.752,
     'L2_xattn_w_qkv': 8.0,
     'L2_xattn_b_proj': 7.046,
     'L3_attn_Wq': 8.0,
     'L3_attn_bq': 8.0,
     'L3_attn_Wk': 8.0,
     'L3_attn_bk': 200.0,
     'L3_attn_Wv': 6.39,
     'L3_attn_bv': 8.0,
     'L3_attn_Wo': 5.998,
     'L3_attn_bo': 7.114,
     'L3_ffn_router_w': 8.0,
     'L3_ffn_w_gate': 8.0,
     'L3_ffn_w_up': 8.0,
     'L3_ffn_w_down': 8.0,
     'L3_ffn_sw_gate': 8.0,
     'L3_ffn_sw_up': 8.0,
     'L3_ffn_sw_down': 8.0,
     'L2_attn_Wv': 2.83,
     'L2_ffn_gate_w': 3.213,
     'L2_ffn_wg': 3.272,
     'L2_ffn_wu': 3.027,
     'L2_ffn_wd': 2.998,
     'L2_ffn_swg': 2.672,
     'L2_ffn_swu': 2.84}
    for name, (base, spread) in spreads.items():
        noise = np.random.default_rng([zlib.crc32(name.encode()), seed]).standard_normal(out[name].shape)
        drawn = base * np.exp(spread * noise) if base else spread * noise
        out[name] = jnp.asarray(drawn.astype(out[name].dtype))
    for name, factor in factors.items():
        out[name] = (out[name] * factor).astype(out[name].dtype)
    return out
```

```python
from contextlib import ExitStack

import numpy as np

import concourse.bass as bass
from concourse import mybir

F32 = mybir.dt.float32
I32 = mybir.dt.int32
ALU = mybir.AluOpType
ACT = mybir.ActivationFunctionType
AXX = mybir.AxisListType.X

P = 128
BATCH, SEQ, CTX = 128, 64, 256
TOKENS = BATCH * SEQ
TILES = 4
NT = TILES * P
GROUPS = TOKENS // NT
SEQS = NT // SEQ
EPS = 1e-5
NEG = -1e30

L0A, L0X, L0F, L1A, L1X, L1F, L2A, L2X, L2F, L3A, L3X, L3F = range(12)
PHASES = range(12)

MOE = {
    L0F: dict(e=8, f=512, shared=0, cap=int(TOKENS / 8 * 1.25)),
    L1F: dict(e=8, f=64, shared=64, cap=None),
    L2F: dict(e=8, f=176, shared=352, cap=None),
    L3F: dict(e=16, f=176, shared=176, cap=int(np.ceil(1.25 * TOKENS * 2 / 16))),
}
for _m in MOE.values():
    _m["nf"] = _m["e"] * _m["f"] + _m["shared"]
    _m["tiles"] = -(-_m["nf"] // P)
    _m["cols"] = _m["e"] + (1 if _m["shared"] else 0)

ATT = {
    L0A: dict(dh=8, units=4), L0X: dict(dh=16, units=4), L1X: dict(dh=16, units=4),
    L2X: dict(dh=8, units=8), L3A: dict(dh=8, units=4),
}
D_STATE = 16

SQUARES = [
    "l0_q", "l0_qb", "l0_k", "l0_v", "l0_o",
    "l0x_k0", "l0x_k1", "l0x_v0", "l0x_v1", "l0x_q", "l0x_o0", "l0x_o1",
    "l1_x0", "l1_x1", "l1_z0", "l1_z1", "l1_o0", "l1_o1",
    "l2_q", "l2_k", "l2_v", "l2_o", "l2x_q", "l2x_k", "l2x_v", "l2x_o",
    "l3_q", "l3_k", "l3_v", "l3_o", "l3_in",
    "ident", "ones", "before", "block8", "decay", "block64",
]
COLS = [
    "l0_q", "l0_qb", "l0_k", "cos", "sin", "l0x_k", "l0x_q", "l3_q", "l3_k",
    "l1_cb0", "l1_cb1", "l1_dt0", "l1_dt1", "l1_d0", "l1_d1", "l1x_b", "l3_res",
    "iota64", "one", "zero",
]
ROWS = ["l0_v", "l0_o", "l0x_v", "l0x_o", "l2_q", "l2_k", "l2_v", "l2_o", "l2x_o",
        "l3_v", "l3_o", "l3_in", "ones"]
ROUTERS = [L0F, L1F, L2F, L3F]


def per_group():
    units = {ph: a["units"] for ph, a in ATT.items()}
    tiles = {ph: m["tiles"] for ph, m in MOE.items()}
    every = {ph: 1 for ph in range(12)}
    steps = {L1A: 2 * D_STATE}
    states = {L1A: D_STATE}
    return {
        "x_updated": every, "var_ready": {**every, L1A: 2, L3X: 3}, "rstd_ready": {**every, L1A: 2, L3X: 3},
        "xn_ready": every, "xnt_psum": every, "xnt_ready": every,
        "ctx_landed": {L0X: 16, L1X: 16, L2X: 16, L3X: 16}, "ctx_values_landed": {L2X: 16}, "ctx_psum": {L0X: 2, L1X: 1, L2X: 1},
        "ctxt_ready": {L0X: 2, L1X: 1, L2X: 1}, "ctx_used": {L3X: 1},
        "row_landed": {L0X: 16, L1X: 16, L3X: 16}, "row_used": {L1X: 1, L3X: 1},
        "proj_psum": {L0A: 3, L0X: 3, L1A: 7, L2A: 3, L2X: 2, L3A: 3},
        "qt_ready": {ph: 1 for ph in ATT}, "kt_ready": {ph: 1 for ph in ATT},
        "v_ready": {L0A: 1, L0X: 1, L1X: 1, L2A: 1, L2X: 1, L3A: 1},
        "qbd_ready": {ph: 1 for ph in ATT},
        "scores_psum": units, "shifted_ready": units, "exp_ready": units,
        "rsum_ready": units, "probs_ready": units, "probst_psum": units, "probst_ready": units,
        "heads_psum": units, "heads_read": units, "out_psum": {**every},
        "logits_psum": {ph: 1 for ph in MOE}, "logits_shifted": {ph: 1 for ph in MOE},
        "logits_exp": {ph: 1 for ph in MOE}, "picks_ready": {L0F: 1, L3F: 1}, "ranks_psum": {L0F: 1, L3F: 1},
        "cw_ready": {ph: 1 for ph in MOE}, "cwt_psum": {ph: 1 for ph in MOE}, "cwt_ready": {ph: 1 for ph in MOE},
        "gate_psum": tiles, "up_psum": tiles, "silu_ready": tiles, "h_ready": tiles, "down_done": tiles,
        "wbc_psum": {**tiles, L0F: 8}, "wbc_read": {**tiles, L0F: 8},
        "yt_ready": {**{ph: 1 for ph in MOE}},
        "conv_ready": {L1A: 1}, "xs_padded": {L1A: 1}, "u_ready": {L1A: 1}, "zs_ready": {L1A: 1},
        "dtr_ready": {L1A: 1}, "soft_exp": {L1A: 1}, "soft_ready": {L1A: 1}, "dt_ready": {L1A: 1}, "du_ready": {L1A: 1},
        "b_psum": states, "c_psum": states, "c_ready": states, "b_read": states,
        "da_ready": steps, "scan_ready": steps, "hc_ready": steps, "hc_used": steps,
        "ym_psum": {L1A: 1}, "ym_ready": {L1A: 1},
        "qk_shifted": {L2A: 2}, "qk_exp": {L2A: 2}, "qkt_psum": {L2A: 1}, "qkt_ready": {L2A: 1},
        "kv_psum": {L2A: 1}, "kv_ready": {L2A: 1}, "den_psum": {L2A: 1}, "y_ready": {L2A: 1},
        "dep_psum": {L3X: 1}, "dep_ready": {L3X: 1}, "u_scaled": {L3X: 1},
    }


class Signal:

    def __init__(self, sem, per):
        self.sem, self.per, self.base = sem, per, {}
        total = 0
        for ph in PHASES:
            self.base[ph] = total
            total += GROUPS * per.get(ph, 0)

    def at(self, ph, i, k):
        return self.base[ph] + i * self.per[ph] + k


class Chain:

    def __init__(self, sem, per):
        self.sem, self.base, self.per = sem, {}, per
        total = 0
        for ph in PHASES:
            self.base[ph] = total
            total += GROUPS * per.get(ph, 0)

    def enter(self, eng, ph, i):
        self.eng, self.ph, self.i, self.n = eng, ph, i, 0

    def __call__(self, ins):
        self.n += 1
        ins.then_inc(self.sem, 1)
        self.eng.wait_ge(self.sem, self.base[self.ph] + self.i * self.per.get(self.ph, 0) + self.n)


def decoder(nc, d, out_dram, counts):
    ctx = ExitStack()
    with ctx:
        def sb(name, shape, dt=F32):
            return ctx.enter_context(nc.sbuf_tensor(name, shape, dt))

        xs = sb("xs", [P, TOKENS // P, P])
        square = {n: k for k, n in enumerate(SQUARES)}
        squares = sb("squares", [P, len(SQUARES), P])
        cols = sb("cols", [P, len(COLS)])
        rows = sb("rows", [1, len(ROWS), P])
        gates = sb("gates", [P, 4 * 16])
        rbias = sb("rbias", [1, 64])
        rank = sb("rank", [P, 16])
        headmask = sb("headmask", [P, 12])
        causal = sb("causal", [P, SEQ])
        rope = sb("rope", [P, 2, P])
        l1w = sb("l1w", [P, 2, 4 + D_STATE])
        bcw = sb("bcw", [P, 2 * D_STATE + 8])
        wdt = sb("wdt", [8, 2, P])
        fbc = sb("fbc", [P, 3, P])
        maskcol = sb("maskcol", [P, TOKENS // P])

        big = sb("big", [P, 3, 8 * 512])
        small = sb("small", [P, 3, (MOE[L1F]["tiles"] + MOE[L2F]["tiles"]) * P])
        sel = sb("sel", [17, 24 * P])

        stats = sb("stats", [P, TILES, 6])
        mv = sb("mv", [P, TILES, 2])
        vare = sb("vare", [P, 4])
        rstd = sb("rstd", [P, 4])
        power = sb("power", [P, 4])
        xn = sb("xn", [P, TILES, P])
        xnt = sb("xnt", [P, NT])
        xpad = sb("xpad", [P, 2, SEQS, SEQ + 3])
        work = sb("work", [P, 20 * 512])

        def wk(k, n=1):
            return work[:, k * 512:(k + n) * 512]

        banks = ctx.enter_context(nc.psum_tensor("banks", [P, 8, 512], F32))

        names = per_group()
        S = {n: Signal(ctx.enter_context(nc.semaphore(n)), per) for n, per in names.items()}
        chains = {e: Chain(ctx.enter_context(nc.semaphore(e + "_step")), counts.get(e, {}))
                  for e in ("vector", "scalar", "gpsimd", "tensor")}
        loaded = ctx.enter_context(nc.semaphore("loaded"))
        l0_loaded = ctx.enter_context(nc.semaphore("l0_loaded"))
        l3_loaded = ctx.enter_context(nc.semaphore("l3_loaded"))
        sel_loaded = ctx.enter_context(nc.semaphore("sel_loaded"))
        plug_step = ctx.enter_context(nc.semaphore("plug_step"))
        a_exp = ctx.enter_context(nc.semaphore("a_exp"))
        a_ready = ctx.enter_context(nc.semaphore("a_ready"))
        setup_done = ctx.enter_context(nc.semaphore("setup_done"))
        plug_done = ctx.enter_context(nc.semaphore("plug_done"))
        plug_stored = ctx.enter_context(nc.semaphore("plug_stored"))
        out_stored = ctx.enter_context(nc.semaphore("out_stored"))
        seen = {}

        def sq(n):
            return squares[:, square[n], :]

        def col(n):
            k = COLS.index(n)
            return cols[:, k:k + 1]

        def row(n):
            return rows[0:1, ROWS.index(n), :]

        ones_row = rows[0:1, ROWS.index("ones"), 0:P]
        ident = sq("ident")

        def over(ap, n):
            return ap.unsqueeze(2).broadcast_to([ap.shape[0], ap.shape[1], n])

        def times(ap, n):
            return ap.unsqueeze(1).broadcast_to([ap.shape[0], n, ap.shape[1]])

        def t4(ap):
            return ap.rearrange("p (t f) -> p t f", t=TILES)

        qt, kt, vt = wk(0), wk(1), wk(2)
        qbd = wk(3, 4)
        sc = [wk(7, 2), wk(9, 2)]
        pt = wk(11, 2)
        ht = wk(13)
        ctxn = wk(14, 2).rearrange("p (t f) -> p t f", t=TILES)
        ctxt = wk(16, 2)
        mask_bc = wk(18)
        mask_add = wk(19)
        tmp1, tmp2 = wk(7), wk(8)
        att_small = sb("att_small", [P, 3, 16])
        RT = sb("rt", [P, 24, 4, 17])
        cnt = sb("cnt", [P, 5, 16])
        NB, OB = banks[:, 0, :], banks[:, 1, :]

        def groups(eng, name, program, before=None):
            chain = chains[name]
            for ph in PHASES:
                def one(i, first=False):
                    chain.enter(eng, ph, i)
                    if not first:
                        eng.wait_ge(S["x_updated"].sem, S["x_updated"].at(ph, i, 0))
                    program(ph, i)
                    seen[name, ph] = chain.n
                if before:
                    before(ph)
                if ph == PHASES[0]:
                    one(0, True)
                    with eng.Fori(1, GROUPS) as i:
                        one(i)
                else:
                    with eng.Fori(0, GROUPS) as i:
                        one(i)

        def values_of(ph, i):
            return lambda name, k=1: (S[name].sem, S[name].at(ph, i, k))

        def ffn_weights(ph):
            m = MOE[ph]
            nf = m["nf"]
            if ph in (L0F, L3F):
                r = big
                a = 0
            else:
                r = small
                a = 0 if ph == L1F else MOE[L1F]["tiles"] * P
            n = m["tiles"] * P
            return (r[:, 0, a:a + nf], r[:, 1, a:a + nf],
                    r[:, 2, a:a + n].rearrange("p (t f) -> p t f", f=P))

        def apart(eng):
            eng.wait_ge(loaded, N_LOADED)

        N_LOADED = 16 * 18
        block = ctx.enter_context(nc.Block())

        @block.sync
        def _(sp):
            x_src = d["x"].rearrange("(t p) f -> p t f", p=P)
            sp.dma_start(xs[:, :, :], x_src).then_inc(loaded, 16)
            for dst, name in ((squares[:, :, :], "squares"), (cols[:, :], "cols"), (rows[:, :, :], "rows"),
                              (gates[:, :], "gates"), (rbias[:, :], "rbias"), (rank[:, :], "rank"),
                              (headmask[:, :], "headmask"), (causal[:, :], "causal"), (rope[:, :, :], "rope"),
                              (l1w[:, :, :], "l1w"), (bcw[:, :], "bcw"), (wdt[:, :, :], "wdt"),
                              (maskcol[:, :], "maskcol"), (work[:, 0:SEQ].bitcast(I32), "patch_lens")):
                sp.dma_start(dst, d[name]).then_inc(loaded, 16)
            for k, name in enumerate(("ln_g", "ln_b", "g_init")):
                sp.dma_start(fbc[:, k, :], d[name].partition_broadcast(P)).then_inc(loaded, 16)
            sp.dma_start(big[:, :, :], d["ffn_l0"]).then_inc(l0_loaded, 16)
            sp.dma_start(small[:, :, 0:d["ffn_mid"].shape[2]], d["ffn_mid"]).then_inc(l0_loaded, 16)
            sp.wait_ge(plug_done, 1)
            sp.dma_start(d["plug"], work[:, SEQ:2 * SEQ]).then_inc(plug_stored, 16)
            sp.wait_ge(plug_stored, 16)
            nsel = 0
            for ph in PHASES:
                if ph in MOE:
                    m = MOE[ph]
                    if ph != PHASES[0]:
                        sp.wait_ge(S["x_updated"].sem, S["x_updated"].at(ph, 0, 0))
                    n = m["e"] * P if ph == L0F else m["nf"]
                    sp.dma_start(sel[0:m["cols"], 0:n], d[f"sel{ph}"]).then_inc(sel_loaded, 16)
                if ph == L0F + 1:
                    sp.wait_ge(S["x_updated"].sem, S["x_updated"].at(ph, 0, 0))
                    sp.dma_start(big[:, :, 0:24 * P], d["ffn_l3"]).then_inc(l3_loaded, 16)
                if ph in (L0X, L1X, L2X, L3X):
                    if ph != PHASES[0]:
                        sp.wait_ge(S["x_updated"].sem, S["x_updated"].at(ph, 0, 0))
                    def load(i, first=False):
                        if not first:
                            for name in {L1X: ("ctx_psum", "v_ready"), L3X: ("ctx_used",)}.get(ph, ("ctx_psum",)):
                                sp.wait_ge(S[name].sem, S[name].at(ph, i, 0))
                        src = d["ctx"][bass.ds(i * NT, NT), :]
                        sp.dma_start(ctxn, src.rearrange("(t p) f -> p t f", p=P))\
                            .then_inc(S["ctx_landed"].sem, 16)
                        if ph == L2X:
                            if not (first and ph == PHASES[0]):
                                sp.wait_ge(S["x_updated"].sem, S["x_updated"].at(ph, i, 0))
                            sp.dma_start(wk(18, 2).rearrange("p (s f) -> p s f", s=SEQS)[0:SEQ],
                                         src[:, P:CTX].rearrange("(s k) f -> k s f", k=SEQ))\
                                .then_inc(S["ctx_values_landed"].sem, 16)
                        else:
                            if not first:
                                used = S["kt_ready" if ph == L0X else "row_used"]
                                sp.wait_ge(used.sem, used.at(ph, i, 0))
                            name = {L0X: "mask_f", L1X: "mask_i", L3X: "plug"}[ph]
                            dst = mask_bc.bitcast(I32) if ph == L1X else mask_bc
                            per_token = d[name][bass.ds(i * SEQS, SEQS), :].rearrange("b s -> (b s)")
                            sp.dma_start(dst, per_token.partition_broadcast(P)).then_inc(S["row_landed"].sem, 16)
                    load(0, True)
                    with sp.Fori(1, GROUPS) as i:
                        load(i)
            last = S["x_updated"]
            sp.wait_ge(last.sem, last.at(PHASES[-1], GROUPS, 0))
            sp.dma_start(out_dram.rearrange("(t p) f -> p t f", p=P), xs[:, :, :]).then_inc(out_stored, 16)
            sp.wait_ge(out_stored, 16)

        def pool_softmax(ph, i, eng, at):
            for u in range(ATT[ph]["units"]):
                n = (16 if ATT[ph]["dh"] == 8 else 8) if ph != L2X else 8
                kl = (NT * 2 if ATT[ph]["dh"] == 8 else NT) // n
                e = sc[u % 2][:, 0:n * kl].rearrange("p (r k) -> p r k", k=kl)
                eng.wait_ge(*at("rsum_ready", u + 1))
                eng.tensor_tensor(e, e, over(att_small[:, 2, 0:n], kl), ALU.mult)\
                    .then_inc(S["probs_ready"].sem, 1)

        def pool_rstd(at, eng, k):
            eng.wait_ge(*at("var_ready", k))
            eng.tensor_tensor(rstd[:, :], vare[:, :], power[:, :], ALU.pow).then_inc(S["rstd_ready"].sem, 1)

        @block.gpsimd
        def _(eng):
            eng.memset(power[:, :], -0.5).then_inc(setup_done, 1)
            eng.wait_ge(setup_done, 1)

            def program(ph, i):
                at = values_of(ph, i)
                pool_rstd(at, eng, 1)
                if ph in ATT:
                    pool_softmax(ph, i, eng, at)
                if ph == L3X:
                    pool_rstd(at, eng, 2)
                    pool_rstd(at, eng, 3)
                if ph == L1A:
                    eng.wait_ge(*at("dt_ready"))
                    eng.tensor_tensor(wk(6, 2), wk(2, 2), wk(4, 2), ALU.mult).then_inc(S["du_ready"].sem, 1)
                    for s in range(2 * D_STATE):
                        eng.wait_ge(*at("scan_ready", s + 1))
                        eng.wait_ge(*at("c_ready", s // 2 + 1))
                        if s >= 2:
                            eng.wait_ge(*at("hc_used", s - 1))
                        eng.tensor_tensor(wk(16 + s % 2), wk(14 + s % 2), wk(18 + s // 2 % 2), ALU.mult)\
                            .then_inc(S["hc_ready"].sem, 1)
                    pool_rstd(at, eng, 2)
            groups(eng, "gpsimd", program)

        @block.scalar
        def _(eng):
            link = chains["scalar"]
            eng.wait_ge(loaded, N_LOADED)
            eng.activation(l1w[:, :, 4:], l1w[:, :, 4:], ACT.Exp).then_inc(a_exp, 1)

            def transposed(at):
                eng.wait_ge(*at("xnt_psum"))
                eng.activation(xnt[:, :], NB, ACT.Copy).then_inc(S["xnt_ready"].sem, 1)

            def attention(ph, at):
                a = ATT[ph]
                hg = 32 // a["dh"]
                eng.wait_ge(*at("qt_ready"))
                dst = qbd.rearrange("p (b h s) -> p b h s", h=4, s=SEQ)
                m = 4 if a["dh"] == 8 else 10
                for h in range(hg):
                    ins = eng.activation(dst[:, :, h, :], qt.rearrange("p (b s) -> p b s", s=SEQ), ACT.Copy,
                                         scale=headmask[:, m + h:m + h + 1])
                ins.then_inc(S["qbd_ready"].sem, 1)
                n = 1024 if a["dh"] == 8 else 512
                for u in range(a["units"] + 1):
                    if u < a["units"]:
                        eng.wait_ge(*at("shifted_ready", u + 1))
                        eng.activation(sc[u % 2][:, 0:n], sc[u % 2][:, 0:n], ACT.Exp)\
                            .then_inc(S["exp_ready"].sem, 1)
                    if u >= 1:
                        eng.wait_ge(*at("probst_psum", u))
                        if u >= 2:
                            eng.wait_ge(*at("heads_psum", u - 1))
                        eng.activation(pt[:, 0:n], banks[:, 6:8, :].rearrange("p a n -> p (a n)")[:, 0:n],
                                       ACT.Copy).then_inc(S["probst_ready"].sem, 1)

            def ffn(ph, at):
                m = MOE[ph]
                eng.wait_ge(*at("logits_shifted"))
                eng.activation(RT[:, 1, :, 0:m["e"]], RT[:, 0, :, 0:m["e"]], ACT.Exp)\
                    .then_inc(S["logits_exp"].sem, 1)
                eng.wait_ge(*at("cwt_psum"))
                eng.activation(wk(0)[0:m["cols"], :], OB[0:m["cols"], :], ACT.Copy)\
                    .then_inc(S["cwt_ready"].sem, 1)
                for f in range(m["tiles"]):
                    r = min(P, m["nf"] - f * P)
                    eng.wait_ge(*at("gate_psum", f + 1))
                    if f >= 2:
                        eng.wait_ge(*at("h_ready", f - 1))
                    eng.activation(wk(1 + f % 2)[0:r], banks[0:r, 2 + f % 2, :], ACT.Silu)\
                        .then_inc(S["silu_ready"].sem, 1)
                eng.wait_ge(*at("down_done", m["tiles"]))
                eng.activation(wk(7), banks[:, 7, :], ACT.Copy).then_inc(S["yt_ready"].sem, 1)

            def token_major_v(at, k, bank):
                eng.wait_ge(*at("proj_psum", k))
                eng.activation(vt, bank, ACT.Copy).then_inc(S["v_ready"].sem, 1)

            def program(ph, i):
                at = values_of(ph, i)
                if ph in (L0X, L1X, L2X):
                    for k in range(2 if ph == L0X else 1):
                        eng.wait_ge(*at("ctx_psum", k + 1))
                        eng.activation(ctxt[:, k * 512:(k + 1) * 512], banks[:, 6 + k, :], ACT.Copy)\
                            .then_inc(S["ctxt_ready"].sem, 1)
                if ph != L3X:
                    transposed(at)
                if ph == L0X:
                    eng.wait_ge(*at("proj_psum", 3))
                    for t in range(TILES):
                        ins = eng.activation(t4(vt)[:, t, :], t4(OB)[:, t, :], ACT.Copy,
                                             scale=maskcol[:, bass.ds(i * TILES + t, 1)])
                    ins.then_inc(S["v_ready"].sem, 1)
                    attention(ph, at)
                if ph == L1X:
                    eng.activation(t4(vt), ctxn[:, :, P:CTX], ACT.Copy).then_inc(S["v_ready"].sem, 1)
                    attention(ph, at)
                if ph == L2X:
                    eng.wait_ge(*at("proj_psum", 2))
                    eng.activation(wk(18, 2)[SEQ:P], banks[SEQ:P, 6:8, :].rearrange("p a n -> p (a n)"),
                                   ACT.Copy).then_inc(S["v_ready"].sem, 1)
                    attention(ph, at)
                if ph in (L0A, L3A):
                    token_major_v(at, 3, OB)
                    attention(ph, at)
                if ph in MOE:
                    ffn(ph, at)
                if ph == L2A:
                    for k in range(2):
                        eng.wait_ge(*at("qk_shifted", k + 1))
                        eng.activation(wk(k), wk(k), ACT.Exp).then_inc(S["qk_exp"].sem, 1)
                    eng.wait_ge(*at("proj_psum", 3))
                    eng.activation(wk(2), banks[:, 4, :], ACT.Copy).then_inc(S["v_ready"].sem, 1)
                    eng.wait_ge(*at("qkt_psum"))
                    eng.activation(wk(3), banks[:, 5, :], ACT.Copy).then_inc(S["qkt_ready"].sem, 1)
                if ph == L1A:
                    mamba(at)
                if ph == L3X:
                    eng.wait_ge(*at("xnt_psum"))
                    eng.activation(xnt[:, :], NB, ACT.Copy, scale=col("l3_res"))\
                        .then_inc(S["xnt_ready"].sem, 1)
                    eng.wait_ge(*at("dep_psum"))
                    eng.activation(wk(2), banks[:, 2, :], ACT.Copy).then_inc(S["dep_ready"].sem, 1)

            def mamba(at):
                for h in range(2):
                    eng.wait_ge(*at("proj_psum", h + 1))
                    ins = eng.activation(xpad[:, h, :, 3:], banks[:, 2 + h, :].rearrange("p (b s) -> p b s", s=SEQ),
                                         ACT.Copy)
                ins.then_inc(S["xs_padded"].sem, 1)
                eng.wait_ge(*at("proj_psum", 5))
                eng.activation(wk(12)[0:8], banks[0:8, 6, :], ACT.Copy).then_inc(S["dtr_ready"].sem, 1)
                for h in range(2):
                    eng.wait_ge(*at("proj_psum", 3 + h))
                    ins = eng.activation(wk(10 + h), banks[:, 4 + h, :], ACT.Silu)
                ins.then_inc(S["zs_ready"].sem, 1)
                eng.wait_ge(*at("conv_ready"))
                for h in range(2):
                    ins = eng.activation(wk(4 + h), wk(h), ACT.Silu, bias=col(f"l1_cb{h}"))
                ins.then_inc(S["u_ready"].sem, 1)
                for h in range(2):
                    eng.wait_ge(*at("proj_psum", 6 + h))
                    link(eng.activation(wk(8 + h), banks[:, (7, 1)[h], :], ACT.Abs, bias=col(f"l1_dt{h}")))
                for h in range(2):
                    ins = eng.activation(wk(8 + h), wk(8 + h), ACT.Exp, scale=-1.0)
                ins.then_inc(S["soft_exp"].sem, 1)
                eng.wait_ge(*at("soft_exp"))
                for h in range(2):
                    ins = eng.activation(wk(12 + h), wk(8 + h), ACT.Ln, bias=col("one"))
                ins.then_inc(S["soft_ready"].sem, 1)
                eng.wait_ge(*at("dt_ready"))
                for n in range(D_STATE):
                    eng.wait_ge(*at("c_psum", n + 1))
                    if n >= 2:
                        eng.wait_ge(*at("hc_ready", 2 * n - 2))
                    eng.activation(wk(18 + n % 2), banks[:, 4 + n % 2, :], ACT.Copy)\
                        .then_inc(S["c_ready"].sem, 1)
                    for h in range(2):
                        s = 2 * n + h
                        if s >= 2:
                            eng.wait_ge(*at("scan_ready", s - 1))
                        eng.activation(wk(h), wk(8 + h), ACT.Exp, scale=l1w[:, h, 4 + n:5 + n])\
                            .then_inc(S["da_ready"].sem, 1)
            groups(eng, "scalar", program)

        @block.tensor
        def _(eng):
            eng.wait_ge(loaded, N_LOADED)
            mm = eng.matmul

            def transposes(dst, src_tiles):
                for t, src in enumerate(src_tiles):
                    ins = eng.transpose(dst[:, t * P:(t + 1) * P], src, ident)
                return ins

            def token_major(out, bias, *products):
                for t in range(TILES):
                    c = slice(t * P, (t + 1) * P)
                    mm(out[:, c], ones_row, row(bias), start=True, stop=False)
                    for k, (src, weight) in enumerate(products):
                        ins = mm(out[:, c], src[:, c], weight if weight.shape[1] == P else weight[:, c],
                                 start=False, stop=k == len(products) - 1)
                return ins

            def attention(ph, at):
                a = ATT[ph]
                dh = a["dh"]
                hg, units = 32 // dh, a["units"]
                pairs = hg // 2
                J = 4 * pairs
                q = qbd.rearrange("p (b n) -> p b n", b=SEQS)
                probs_bank = banks[:, 6:8, :].rearrange("p a n -> p (a n)")

                def scores(u):
                    if u == 0:
                        eng.wait_ge(*at("qbd_ready"))
                        eng.wait_ge(*at("kt_ready"))
                    else:
                        eng.wait_ge(*at("shifted_ready", u))
                    for j in range(J):
                        g, jj = divmod(j, pairs)
                        part = slice(32 * g, 32 * g + 32)
                        for b in range(2):
                            if ph == L2X:
                                seq, keys = u, (ctxt[part, u * SEQ:(u + 1) * SEQ] if b == 0 else
                                                kt[part, u * SEQ:(u + 1) * SEQ])
                            else:
                                seq = 2 * u + b
                                keys = kt[part, seq * SEQ:(seq + 1) * SEQ]
                            c = (jj * 2 + b) * SEQ
                            ins = mm(banks[:, 2 + g, c:c + SEQ], q[part, seq, jj * P:(jj + 1) * P], keys,
                                     start=True, stop=True, tile_position=(32 * g, 0))
                    ins.then_inc(S["scores_psum"].sem, 1)

                def turn(u):
                    if u == 0:
                        eng.wait_ge(*at("v_ready"))
                    eng.wait_ge(*at("probs_ready", u + 1))
                    if u >= 1:
                        eng.wait_ge(*at("probst_ready", u))
                    for j in range(J):
                        ins = eng.transpose(probs_bank[:, j * P:(j + 1) * P], sc[u % 2][:, j * P:(j + 1) * P],
                                            ident)
                    ins.then_inc(S["probst_psum"].sem, 1)

                def values(u):
                    apart(eng)
                    if u == 0:
                        eng.wait_ge(*at("v_ready"))
                        if ph == L2X:
                            eng.wait_ge(*at("ctx_values_landed", 16))
                    eng.wait_ge(*at("probst_ready", u + 1))
                    if u >= 1:
                        eng.wait_ge(*at("heads_read", u))
                    n = hg * SEQ
                    for g in range(4):
                        if ph == L2X:
                            v = wk(18, 2).rearrange("p (s f) -> p s f", s=SEQS)[:, u, 32 * g:32 * g + 32]
                            ins = mm(banks[32 * g:32 * g + 32, 0, 0:n], v, pt[:, g * n:(g + 1) * n],
                                     start=True, stop=True, tile_position=(0, 32 * g))
                        else:
                            for b in range(2):
                                part = slice(b * SEQ, (b + 1) * SEQ)
                                v = t4(vt)[part, u, 32 * g:32 * g + 32]
                                ins = mm(banks[32 * g:32 * g + 32, b, 0:n], v,
                                         pt[part, g * n:(g + 1) * n], start=True, stop=True,
                                         tile_position=(b * SEQ, 32 * g))
                    ins.then_inc(S["heads_psum"].sem, 1)

                scores(0)
                for u in range(units):
                    if u + 1 < units:
                        scores(u + 1)
                    turn(u)
                    if u >= 1:
                        values(u - 1)
                values(units - 1)
                eng.wait_ge(*at("heads_read", units))

            def ffn(ph, i, at):
                m = MOE[ph]
                e, ncol = m["e"], m["cols"]
                wg, wu, wd = ffn_weights(ph)
                gate_w = gates[:, 16 * ROUTERS.index(ph):16 * ROUTERS.index(ph) + e]
                for t in range(TILES):
                    if ph == L3F:
                        mm(banks[:, 6, t * e:(t + 1) * e], ones_row, rbias[0:1, 0:e], start=True, stop=False)
                    ins = mm(banks[:, 6, t * e:(t + 1) * e], xnt[:, t * P:(t + 1) * P], gate_w,
                             start=ph != L3F, stop=True)
                ins.then_inc(S["logits_psum"].sem, 1)
                if m["cap"] is not None:
                    eng.wait_ge(*at("picks_ready"))
                    picks = RT[:, 8, :, 0:16]
                    mm(banks[:, 4, 0:64].rearrange("p (t e) -> p t e", t=4), sq("before"), picks,
                       start=True, stop=True)
                    mm(banks[:, 5, 0:64].rearrange("p (t e) -> p t e", t=4), sq("ones"), picks,
                       start=True, stop=True).then_inc(S["ranks_psum"].sem, 1)
                eng.wait_ge(*at("cw_ready"))
                for t in range(TILES):
                    ins = eng.transpose(OB[0:ncol, t * P:(t + 1) * P], RT[:, 16, t, 0:ncol], ident)
                ins.then_inc(S["cwt_psum"].sem, 1)
                eng.wait_ge(*at("cwt_ready"))
                cwt = wk(0)[0:ncol, :]
                WB = banks[:, 6, :]
                per = m["f"] // P
                eng.wait_ge(sel_loaded, 16 * (1 + [p for p in PHASES if p in MOE].index(ph)))
                eng.wait_ge(l0_loaded, 32)
                if ph == L3F and L1A in PHASES:
                    eng.wait_ge(l3_loaded, 16)

                def down(f):
                    r = min(P, m["nf"] - f * P)
                    eng.wait_ge(*at("h_ready", f + 1))
                    mm(banks[:, 7, :], wd[0:r, f, :], wk(3 + f % 2)[0:r], start=f == 0,
                       stop=f == m["tiles"] - 1).then_inc(S["down_done"].sem, 1)

                for f in range(m["tiles"]):
                    r = min(P, m["nf"] - f * P)
                    if f >= 2:
                        eng.wait_ge(*at("silu_ready", f - 1))
                    if ph == L0F and f % per == 0:
                        x = f // per
                        if x >= 1:
                            eng.wait_ge(*at("wbc_read", x))
                        mm(WB, sel[0:ncol, x * P:(x + 1) * P], cwt, start=True, stop=True)\
                            .then_inc(S["wbc_psum"].sem, 1)
                    mm(banks[0:r, 2 + f % 2, :], wg[:, f * P:f * P + r], xnt[:, :], start=True, stop=True)\
                        .then_inc(S["gate_psum"].sem, 1)
                    if ph != L0F:
                        if f >= 1:
                            eng.wait_ge(*at("wbc_read", f))
                        mm(WB[0:r], sel[0:ncol, f * P:f * P + r], cwt, start=True, stop=True)\
                            .then_inc(S["wbc_psum"].sem, 1)
                    if f >= 2:
                        eng.wait_ge(*at("h_ready", f - 1))
                    if ph == L0F:
                        if f % per == 0:
                            eng.wait_ge(*at("wbc_read", f // per + 1))
                        up_in = wk(5 + f // per % 2)
                    else:
                        up_in = xnt[:, :]
                    mm(banks[0:r, 4 + f % 2, :], wu[:, f * P:f * P + r], up_in, start=True, stop=True)\
                        .then_inc(S["up_psum"].sem, 1)
                    if f >= 1:
                        down(f - 1)
                down(m["tiles"] - 1)
                eng.wait_ge(*at("yt_ready"))
                transposes(OB, [wk(7)[:, t * P:(t + 1) * P] for t in range(TILES)])\
                    .then_inc(S["out_psum"].sem, 1)

            def mamba(at):
                for h in range(2):
                    mm(banks[:, 2 + h, :], sq(f"l1_x{h}"), xnt[:, :], start=True, stop=True)\
                        .then_inc(S["proj_psum"].sem, 1)
                for h in range(2):
                    mm(banks[:, 4 + h, :], sq(f"l1_z{h}"), xnt[:, :], start=True, stop=True)\
                        .then_inc(S["proj_psum"].sem, 1)
                mm(banks[0:8, 6, :], bcw[:, 2 * D_STATE:2 * D_STATE + 8], xnt[:, :], start=True, stop=True)\
                    .then_inc(S["proj_psum"].sem, 1)
                eng.wait_ge(*at("dtr_ready"))
                for h in range(2):
                    mm(banks[:, (7, 1)[h], :], wdt[0:8, h, :], wk(12)[0:8, :], start=True, stop=True)\
                        .then_inc(S["proj_psum"].sem, 1)
                eng.wait_ge(*at("xs_padded"))
                eng.wait_ge(*at("zs_ready"))
                eng.wait_ge(*at("dt_ready"))

                def spread(n):
                    if n >= 2:
                        eng.wait_ge(*at("b_read", n - 1))
                        eng.wait_ge(*at("c_ready", n - 1))
                    mm(banks[:, 2 + n % 2, :], bcw[:, n:n + 1].broadcast_to([P, P]), xnt[:, :],
                       start=True, stop=True).then_inc(S["b_psum"].sem, 1)
                    mm(banks[:, 4 + n % 2, :], bcw[:, D_STATE + n:D_STATE + n + 1].broadcast_to([P, P]),
                       xnt[:, :], start=True, stop=True).then_inc(S["c_psum"].sem, 1)

                spread(0)
                for n in range(D_STATE):
                    if n + 1 < D_STATE:
                        spread(n + 1)
                    for h in range(2):
                        eng.wait_ge(*at("hc_ready", 2 * n + h + 1))
                        ins = mm(banks[:, 6 + h, :], ident, wk(16 + h), start=n == 0, stop=n == D_STATE - 1)
                        ins.then_inc(S["hc_used"].sem, 1)
                eng.wait_ge(*at("ym_ready"))
                for t in range(TILES):
                    for h in range(2):
                        ins = mm(OB[:, t * P:(t + 1) * P], wk(6 + h)[:, t * P:(t + 1) * P], sq(f"l1_o{h}"),
                                 start=h == 0, stop=h == 1)
                ins.then_inc(S["out_psum"].sem, 1)

            def linear_attention(at):
                for k, w in enumerate(("l2_q", "l2_k", "l2_v")):
                    ins = token_major(banks[:, 2 + k, :], w, (xnt, sq(w)))
                    ins.then_inc(S["proj_psum"].sem, 1)
                eng.wait_ge(*at("qk_exp", 1))
                transposes(banks[:, 5, :], [wk(0)[:, t * P:(t + 1) * P] for t in range(TILES)])\
                    .then_inc(S["qkt_psum"].sem, 1)
                eng.wait_ge(*at("qk_exp", 2))
                eng.wait_ge(*at("v_ready"))
                for s in range(SEQS):
                    part = slice(s % 2 * SEQ, s % 2 * SEQ + SEQ)
                    c = slice((s // 2) * P, (s // 2 + 1) * P)
                    tp = (s % 2 * SEQ, 0)
                    mm(banks[:, 2 + s % 2, c], wk(1)[part, c], wk(2)[part, c], start=True, stop=True,
                       tile_position=tp)
                    ins = mm(banks[:, 6 + s % 2, c], wk(1)[part, c], sq("ones")[part, :], start=True,
                             stop=True, tile_position=tp)
                ins.then_inc(S["kv_psum"].sem, 1)
                eng.wait_ge(*at("kv_ready"))
                eng.wait_ge(*at("qkt_ready"))
                for s in range(SEQS):
                    c = slice(s * SEQ, (s + 1) * SEQ)
                    k = slice((s % 2 * 4 + s // 2) * P, (s % 2 * 4 + s // 2 + 1) * P)
                    mm(banks[:, 4, c], wk(4, 2)[:, k], wk(3)[:, c], start=True, stop=True)
                    ins = mm(banks[:, 5, c], wk(6, 2)[:, k], wk(3)[:, c], start=True, stop=True)
                ins.then_inc(S["den_psum"].sem, 1)
                eng.wait_ge(*at("y_ready"))
                token_major(OB, "l2_o", (wk(10), sq("l2_o"))).then_inc(S["out_psum"].sem, 1)

            def project(name, bank, src=None):
                return mm(bank, sq(name), xnt[:, :] if src is None else src, start=True, stop=True)

            def program(ph, i):
                at = values_of(ph, i)
                if ph in (L0X, L1X, L2X):
                    eng.wait_ge(*at("ctx_landed", 16))
                    for k in range(2 if ph == L0X else 1):
                        ins = transposes(banks[:, 6 + k, :], [ctxn[:, t, k * P:(k + 1) * P] for t in range(TILES)])
                        ins.then_inc(S["ctx_psum"].sem, 1)
                if ph != L3X:
                    eng.wait_ge(*at("xn_ready"))
                    transposes(NB, [xn[:, t, :] for t in range(TILES)]).then_inc(S["xnt_psum"].sem, 1)
                    eng.wait_ge(*at("xnt_ready"))
                if ph == L0X:
                    eng.wait_ge(*at("ctxt_ready", 2))
                    project("l0x_q", banks[:, 2, :]).then_inc(S["proj_psum"].sem, 1)
                    mm(banks[:, 3, :], sq("l0x_k0"), ctxt[:, 0:NT], start=True, stop=False)
                    mm(banks[:, 3, :], sq("l0x_k1"), ctxt[:, NT:2 * NT], start=False, stop=True)\
                        .then_inc(S["proj_psum"].sem, 1)
                    ins = token_major(OB, "l0x_v", (ctxt[:, 0:NT], sq("l0x_v0")), (ctxt[:, NT:], sq("l0x_v1")))
                    ins.then_inc(S["proj_psum"].sem, 1)
                    attention(ph, at)
                    ins = token_major(OB, "l0x_o", (xnt, sq("l0x_o0")), (ht, sq("l0x_o1")))
                    ins.then_inc(S["out_psum"].sem, 1)
                if ph == L1X:
                    eng.wait_ge(*at("ctxt_ready"))
                    attention(ph, at)
                    transposes(OB, [ht[:, t * P:(t + 1) * P] for t in range(TILES)])\
                        .then_inc(S["out_psum"].sem, 1)
                if ph == L2X:
                    eng.wait_ge(*at("ctxt_ready"))
                    project("l2x_q", banks[:, 2, :])
                    project("l2x_k", banks[:, 3, :]).then_inc(S["proj_psum"].sem, 1)
                    own = banks[SEQ:P, 6:8, :].rearrange("p a n -> p (a n)")
                    for s in range(SEQS):
                        ins = mm(own[:, s * P:(s + 1) * P], xnt[:, s * SEQ:(s + 1) * SEQ], sq("l2x_v"),
                                 start=True, stop=True, tile_position=(0, SEQ))
                    ins.then_inc(S["proj_psum"].sem, 1)
                    attention(ph, at)
                    token_major(OB, "l2x_o", (ht, sq("l2x_o"))).then_inc(S["out_psum"].sem, 1)
                if ph in (L0A, L3A):
                    n = "l0" if ph == L0A else "l3"
                    project(n + "_q", banks[:, 2, :]).then_inc(S["proj_psum"].sem, 1)
                    project(n + "_k", banks[:, 3, :]).then_inc(S["proj_psum"].sem, 1)
                    token_major(OB, n + "_v", (xnt, sq(n + "_v"))).then_inc(S["proj_psum"].sem, 1)
                    attention(ph, at)
                    token_major(OB, n + "_o", (ht, sq(n + "_o"))).then_inc(S["out_psum"].sem, 1)
                if ph in MOE:
                    ffn(ph, i, at)
                if ph == L1A:
                    mamba(at)
                if ph == L2A:
                    linear_attention(at)
                if ph == L3X:
                    eng.wait_ge(*at("u_scaled"))
                    for t in range(TILES):
                        ins = mm(banks[:, 2, t * P:(t + 1) * P], sq("decay"), wk(0)[:, t * P:(t + 1) * P],
                                 start=True, stop=True)
                    ins.then_inc(S["dep_psum"].sem, 1)
                    eng.wait_ge(*at("xn_ready"))
                    transposes(NB, [wk(3)[:, t * P:(t + 1) * P] for t in range(TILES)])\
                        .then_inc(S["xnt_psum"].sem, 1)
                    eng.wait_ge(*at("xnt_ready"))
                    eng.wait_ge(*at("dep_ready"))
                    eng.wait_ge(*at("row_used"))
                    ins = token_major(OB, "l3_in", (xnt, sq("l3_in")), (wk(4), wk(2)))
                    ins.then_inc(S["out_psum"].sem, 1)
            groups(eng, "tensor", program)

        @block.vector
        def _(eng):
            link = chains["vector"]
            eng.wait_ge(loaded, N_LOADED)
            n = [0]

            def step(ins):
                n[0] += 1
                ins.then_inc(plug_step, 1)
                eng.wait_ge(plug_step, n[0])

            TT, TS, STT = eng.tensor_tensor, eng.tensor_scalar, eng.scalar_tensor_tensor
            step(eng.memset(xpad[:, :, :, :], 0.0))
            step(eng.memset(cnt[:, :, :], 0.0))
            step(eng.memset(RT[:, :, :, :], 1.0))
            step(eng.memset(work[:, 3 * SEQ:4 * SEQ], 1.0))
            lens, plug = work[:, 2 * SEQ:3 * SEQ], work[:, SEQ:2 * SEQ]
            onesw, wrap = work[:, 3 * SEQ:4 * SEQ], work[:, 4 * SEQ:5 * SEQ]
            hits = work[:, 512:512 + SEQ * SEQ].rearrange("p (t i) -> p t i", i=SEQ)
            bound = work[:, 5 * SEQ:6 * SEQ]
            step(eng.tensor_copy(lens, work[:, 0:SEQ].bitcast(I32)))
            step(eng.tensor_tensor_scan(bound, onesw, lens, 0.0, ALU.mult, ALU.add))
            step(TS(bound, bound, 1.0, None, ALU.subtract))
            step(TS(wrap, bound, 0.0, float(SEQ), ALU.is_lt, ALU.mult))
            step(TT(bound, bound, wrap, ALU.add))
            step(eng.tensor_tensor_scan(wrap, onesw, onesw, -1.0, ALU.mult, ALU.add))
            step(TT(hits, over(wrap, SEQ), times(bound, SEQ), ALU.is_equal))
            step(eng.tensor_reduce(lens, hits, AXX, ALU.max))
            step(eng.tensor_tensor_scan(plug, onesw, lens, -1.0, ALU.mult, ALU.add))
            TS(plug, plug, 0.0, None, ALU.max).then_inc(plug_done, 1)
            eng.wait_ge(a_exp, 1)
            TS(l1w[:, :, 4:], l1w[:, :, 4:], -1.0, None, ALU.mult).then_inc(a_ready, 1)
            eng.wait_ge(a_ready, 1)
            step(TT(sq("l0_q"), sq("l0_q"), rope[:, 0, :], ALU.mult))
            step(TT(sq("l0_qb"), sq("l0_qb"), rope[:, 1, :], ALU.mult))
            step(TT(sq("l0_q"), sq("l0_q"), sq("l0_qb"), ALU.add))
            step(TT(col("l0_q"), col("l0_q"), col("cos"), ALU.mult))
            step(STT(col("l0_q"), col("l0_qb"), col("sin"), col("l0_q"), ALU.mult, ALU.add))
            eng.wait_ge(plug_stored, 16)

            def norm(i, at):
                for t in range(TILES):
                    ins = eng.bn_stats(stats[:, t, :], xs[:, bass.ds(i * TILES + t, 1), :])
                link(ins)
                eng.memset(att_small[0:1, 0, 15:16], 0.0)
                for t in range(TILES):
                    ins = eng.bn_aggr(mv[:, t, :], stats[:, t, :])
                link(ins)
                TS(vare[:, :], mv[:, :, 1], EPS, None, ALU.add).then_inc(S["var_ready"].sem, 1)
                eng.wait_ge(*at("rstd_ready", 1))
                for t in range(TILES):
                    ins = TS(xn[:, t, :], xs[:, bass.ds(i * TILES + t, 1), :].rearrange("p a f -> p (a f)"),
                             mv[:, t, 0:1], rstd[:, t:t + 1], ALU.subtract, ALU.mult)
                return ins

            def add_out(i, at):
                eng.wait_ge(*at("out_psum"))
                x4 = xs[:, bass.ds(i * TILES, TILES), :]
                TT(x4, x4, t4(OB), ALU.add).then_inc(S["x_updated"].sem, 1)

            def attention(ph, at):
                a = ATT[ph]
                dh, units = a["dh"], a["units"]
                n = 1024 if dh == 8 else 512
                kl = P if ph == L2X else SEQ
                r = n // kl
                hg = 32 // dh
                bank = banks[:, 2:6, 0:n // 4].rearrange("p g (r k) -> p g r k", k=kl)
                mx, sm, rc = (att_small[:, k, 0:r] for k in range(3))

                def rk(ap):
                    return ap.rearrange("p (r k) -> p r k", k=kl)

                for u in range(units + 2):
                    if u < units:
                        s = sc[u % 2][:, 0:n].rearrange("p (g r k) -> p g r k", g=4, k=kl)
                        eng.wait_ge(*at("scores_psum", u + 1))
                        if u >= 2:
                            eng.wait_ge(*at("probst_psum", u - 1))
                        src = s
                        if ph in (L0A, L3A):
                            m = causal[:, :].unsqueeze(1).unsqueeze(1).broadcast_to([P, 4, r // 4, SEQ])
                            link(TT(s, bank, m, ALU.add))
                        elif ph in (L0X, L1X):
                            s2 = sc[u % 2][:, 0:n].rearrange("p (g k) -> p g k", g=4)
                            b2 = banks[:, 2:6, 0:P]
                            m = times(mask_add[:, u * P:(u + 1) * P], 4)
                            if ph == L0X:
                                link(TT(s2, b2, m, ALU.add))
                            else:
                                link(STT(s2, b2, col("l1x_b"), m, ALU.add, ALU.add))
                        else:
                            src = bank
                        link(eng.tensor_reduce(mx, src, AXX, ALU.max))
                        mx4 = mx.rearrange("p (g r) -> p g r", g=4).unsqueeze(3).broadcast_to([P, 4, r // 4, kl])
                        TT(s, src, mx4, ALU.subtract).then_inc(S["shifted_ready"].sem, 1)
                    if 1 <= u <= units:
                        eng.wait_ge(*at("exp_ready", u))
                        if u >= 2:
                            eng.wait_ge(*at("probs_ready", u - 1))
                        link(eng.tensor_reduce(sm, rk(sc[(u - 1) % 2][:, 0:n]), AXX, ALU.add))
                        eng.reciprocal(rc, sm).then_inc(S["rsum_ready"].sem, 1)
                    if u >= 2:
                        v = u - 2
                        eng.wait_ge(*at("heads_psum", v + 1))
                        nb = 1 if ph == L2X else 2
                        dst = ht[:, v * nb * SEQ:(v + 1) * nb * SEQ].rearrange("p (b s) -> p b s", b=nb)
                        src = banks[:, 0:nb, 0:hg * SEQ].rearrange("p b (h s) -> p b h s", h=hg)
                        m = 0 if dh == 8 else 8
                        for h in range(hg):
                            hm = headmask[:, m + h:m + h + 1]
                            if h == 0:
                                ins = TS(dst, src[:, :, h, :], hm, None, ALU.mult)
                            else:
                                ins = STT(dst, src[:, :, h, :], hm, dst, ALU.mult, ALU.add)
                            if h < hg - 1:
                                link(ins)
                        ins.then_inc(S["heads_read"].sem, 1)

            def route(ph, at):
                m = MOE[ph]
                e = m["e"]
                R = lambda k: RT[:, k, :, 0:e]
                sm = lambda k: RT[:, 20, :, k]
                bc = lambda k: over(sm(k), e)
                lg = banks[:, 6, 0:4 * e].rearrange("p (t e) -> p t e", t=4)
                eng.wait_ge(*at("logits_psum"))
                link(eng.tensor_reduce(sm(0), lg, AXX, ALU.max))
                TT(R(0), lg, bc(0), ALU.subtract).then_inc(S["logits_shifted"].sem, 1)
                eng.wait_ge(*at("logits_exp"))
                link(eng.tensor_reduce(sm(1), R(1), AXX, ALU.add))
                link(eng.reciprocal(sm(2), sm(1)))
                link(TT(R(2), R(1), bc(2), ALU.mult))

                def best(probs, k, out, signal=None):
                    link(eng.tensor_reduce(sm(k), probs, AXX, ALU.max))
                    link(TT(R(3), probs, bc(k), ALU.is_equal))
                    link(TT(R(3), R(3), times(rank[:, 16 - e:16], 4), ALU.mult))
                    link(eng.tensor_reduce(sm(5), R(3), AXX, ALU.max))
                    ins = TT(out, R(3), bc(5), ALU.is_equal)
                    if signal is None:
                        link(ins)
                    else:
                        ins.then_inc(S[signal].sem, 1)
                        eng.wait_ge(*at(signal))
                oh1, oh2 = (RT[:, 8, :, 0:8], RT[:, 8, :, 8:16]) if ph == L0F else (R(9), R(10))
                best(R(2), 3, oh1)
                link(STT(R(4), oh1, -2.0, R(2), ALU.mult, ALU.add))
                best(R(4), 4, oh2, "picks_ready" if ph == L0F else None)
                if ph != L1F:
                    eps = {L0F: 0.0, L2F: 1e-20, L3F: 1e-9}[ph]
                    link(TT(sm(6), sm(3), sm(4), ALU.add))
                    if eps:
                        link(TS(sm(6), sm(6), eps, None, ALU.add))
                    link(eng.reciprocal(sm(7), sm(6)))
                    link(TT(sm(3), sm(3), sm(7), ALU.mult))
                    link(TT(sm(4), sm(4), sm(7), ALU.mult))
                if ph == L3F:
                    TT(RT[:, 8, :, 0:16], oh1, oh2, ALU.add).then_inc(S["picks_ready"].sem, 1)
                    eng.wait_ge(*at("picks_ready"))
                if m["cap"] is not None:
                    eng.wait_ge(*at("ranks_psum"))
                    tot = banks[:, 5, 0:64].rearrange("p (t e) -> p t e", t=4)
                    for t in range(TILES):
                        link(TT(cnt[:, t + 1, :], cnt[:, t, :], tot[:, t, :], ALU.add))
                    link(TT(RT[:, 11, :, 0:16], banks[:, 4, 0:64].rearrange("p (t e) -> p t e", t=4),
                            cnt[:, 0:4, :], ALU.add))
                    link(eng.tensor_copy(cnt[:, 0, :], cnt[:, 4, :]))
                    link(TS(RT[:, 12, :, 0:16], RT[:, 11, :, 0:16], float(m["cap"]), None, ALU.is_lt))
                if ph == L0F:
                    link(TT(RT[:, 8, :, 0:16], RT[:, 8, :, 0:16], RT[:, 12, :, 0:16], ALU.mult))
                link(TT(R(5), oh1, bc(3), ALU.mult))
                link(TT(R(6), oh2, bc(4), ALU.mult))
                if ph == L3F:
                    link(TT(R(5), R(5), R(6), ALU.add))
                    TT(R(16), R(5), R(12), ALU.mult).then_inc(S["cw_ready"].sem, 1)
                else:
                    TT(R(16), R(5), R(6), ALU.add).then_inc(S["cw_ready"].sem, 1)

            def ffn(ph, at):
                m = MOE[ph]
                per = m["f"] // P
                for f in range(m["tiles"]):
                    r = min(P, m["nf"] - f * P)
                    if ph == L0F and f % per == 0:
                        x = f // per
                        eng.wait_ge(*at("wbc_psum", x + 1))
                        if x >= 2:
                            eng.wait_ge(*at("up_psum", (x - 1) * per))
                        TT(wk(5 + x % 2), xnt[:, :], banks[:, 6, :], ALU.mult).then_inc(S["wbc_read"].sem, 1)
                    sg = wk(1 + f % 2)[0:r]
                    eng.wait_ge(*at("silu_ready", f + 1))
                    if ph != L0F:
                        eng.wait_ge(*at("wbc_psum", f + 1))
                        TT(sg, sg, banks[0:r, 6, :], ALU.mult).then_inc(S["wbc_read"].sem, 1)
                        eng.wait_ge(*at("wbc_read", f + 1))
                    eng.wait_ge(*at("up_psum", f + 1))
                    if f >= 2:
                        eng.wait_ge(*at("down_done", f - 1))
                    TT(wk(3 + f % 2)[0:r], sg, banks[0:r, 4 + f % 2, :], ALU.mult)\
                        .then_inc(S["h_ready"].sem, 1)

            def mamba(at):
                eng.wait_ge(*at("xs_padded"))
                for k in range(4):
                    for h in range(2):
                        o = wk(h).rearrange("p (b s) -> p b s", s=SEQ)
                        src = xpad[:, h, :, k:k + SEQ]
                        if k == 0:
                            ins = TS(o, src, l1w[:, h, 0:1], None, ALU.mult)
                        else:
                            ins = STT(o, src, l1w[:, h, k:k + 1], o, ALU.mult, ALU.add)
                    if k < 3:
                        link(ins)
                ins.then_inc(S["conv_ready"].sem, 1)
                eng.wait_ge(*at("soft_exp"))
                e1, w1, z1 = wk(8, 2), wk(14, 2), wk(16, 2)
                link(TS(w1, e1, 1.0, None, ALU.add))
                link(TS(w1, w1, 1.0, None, ALU.subtract))
                link(TS(z1, w1, 0.0, None, ALU.is_equal))
                link(TT(w1, w1, z1, ALU.add))
                link(eng.reciprocal(w1, w1))
                eng.wait_ge(*at("soft_ready"))
                link(TT(e1, e1, w1, ALU.mult))
                link(TT(z1, z1, wk(12, 2), ALU.add))
                link(TT(e1, e1, z1, ALU.mult))
                for h in range(2):
                    ins = TS(wk(2 + h), banks[:, (7, 1)[h], :], col(f"l1_dt{h}"), 0.0, ALU.add, ALU.max)
                link(ins)
                link(TT(wk(2, 2), wk(2, 2), wk(8, 2), ALU.add))
                link(eng.tensor_copy(wk(8, 2), wk(2, 2)))
                eng.wait_ge(*at("u_ready"))
                eng.memset(wk(8, 2).rearrange("p (b s) -> p b s", s=SEQ)[:, :, 0:1], 1e25)\
                    .then_inc(S["dt_ready"].sem, 1)
                eng.wait_ge(*at("du_ready"))
                for s in range(2 * D_STATE):
                    st, h = divmod(s, 2)
                    eng.wait_ge(*at("b_psum", st + 1))
                    db = wk(12 + h)
                    ins = TT(db, wk(6 + h), banks[:, 2 + st % 2, :], ALU.mult)
                    if h == 1:
                        ins.then_inc(S["b_read"].sem, 1)
                        eng.wait_ge(*at("b_read", st + 1))
                    else:
                        link(ins)
                    eng.wait_ge(*at("da_ready", s + 1))
                    if s >= 2:
                        eng.wait_ge(*at("hc_ready", s - 1))
                    eng.tensor_tensor_scan(wk(14 + h), wk(h), db, 0.0, ALU.mult, ALU.add)\
                        .then_inc(S["scan_ready"].sem, 1)
                eng.wait_ge(*at("hc_used", 2 * D_STATE))
                eng.wait_ge(*at("zs_ready"))
                for h in range(2):
                    ins = STT(wk(12 + h), wk(4 + h), col(f"l1_d{h}"), banks[:, 6 + h, :], ALU.mult, ALU.add)
                link(ins)
                TT(wk(6, 2), wk(12, 2), wk(10, 2), ALU.mult).then_inc(S["ym_ready"].sem, 1)
                eng.wait_ge(*at("out_psum"))
                res = t4(wk(12))
                link(TT(res, xn[:, :, :], t4(OB), ALU.add))
                for t in range(TILES):
                    ins = eng.bn_stats(stats[:, t, :], res[:, t, :])
                link(ins)
                eng.memset(att_small[0:1, 0, 15:16], 0.0)
                for t in range(TILES):
                    ins = eng.bn_aggr(mv[:, t, :], stats[:, t, :])
                link(ins)
                TS(vare[:, :], mv[:, :, 1], EPS, None, ALU.add).then_inc(S["var_ready"].sem, 1)
                eng.wait_ge(*at("rstd_ready", 2))
                for t in range(TILES):
                    ins = TS(res[:, t, :], res[:, t, :], mv[:, t, 0:1], rstd[:, t:t + 1],
                             ALU.subtract, ALU.mult)
                link(ins)
                link(TT(res, res, times(fbc[:, 0, :], TILES), ALU.mult))
                link(TT(res, res, times(fbc[:, 1, :], TILES), ALU.add))
                return res

            def program(ph, i):
                at = values_of(ph, i)
                if ph == L3X:
                    link(norm(i, at))
                else:
                    norm(i, at).then_inc(S["xn_ready"].sem, 1)
                if ph == L0X:
                    eng.wait_ge(*at("row_landed", 16))
                    TS(mask_add, mask_bc, 0.0, NEG, ALU.is_equal, ALU.mult)
                    eng.wait_ge(*at("proj_psum", 1))
                    STT(qt, banks[:, 2, :], col("l0x_q"), mask_bc, ALU.add, ALU.mult)\
                        .then_inc(S["qt_ready"].sem, 1)
                    eng.wait_ge(*at("proj_psum", 2))
                    STT(kt, banks[:, 3, :], col("l0x_k"), mask_bc, ALU.add, ALU.mult)\
                        .then_inc(S["kt_ready"].sem, 1)
                if ph == L1X:
                    eng.wait_ge(*at("row_landed", 16))
                    link(eng.tensor_copy(mask_add, mask_bc.bitcast(I32)))
                    link(TS(mask_add, mask_add, -1.0, 1.0, ALU.mult, ALU.add))
                    TS(mask_add, mask_add, NEG, None, ALU.mult).then_inc(S["row_used"].sem, 1)
                    eng.wait_ge(*at("row_used"))
                    eng.wait_ge(*at("xnt_ready"))
                    eng.tensor_copy(qt, xnt[:, :]).then_inc(S["qt_ready"].sem, 1)
                    eng.wait_ge(*at("ctxt_ready"))
                    eng.tensor_copy(kt, ctxt[:, 0:NT]).then_inc(S["kt_ready"].sem, 1)
                if ph == L2X:
                    eng.wait_ge(*at("proj_psum", 1))
                    eng.tensor_copy(qt, banks[:, 2, :]).then_inc(S["qt_ready"].sem, 1)
                    eng.tensor_copy(kt, banks[:, 3, :]).then_inc(S["kt_ready"].sem, 1)
                if ph in (L0A, L3A):
                    n = "l0" if ph == L0A else "l3"
                    eng.wait_ge(*at("proj_psum", 1))
                    TS(qt, banks[:, 2, :], col(n + "_q"), None, ALU.add).then_inc(S["qt_ready"].sem, 1)
                    eng.wait_ge(*at("proj_psum", 2))
                    TS(kt, banks[:, 3, :], col(n + "_k"), None, ALU.add).then_inc(S["kt_ready"].sem, 1)
                if ph in ATT:
                    attention(ph, at)
                if ph in MOE:
                    route(ph, at)
                    ffn(ph, at)
                    if ph == L3F:
                        x4 = xs[:, bass.ds(i * TILES, TILES), :]
                        link(TT(x4, x4, xn[:, :, :], ALU.add))
                if ph == L1A:
                    res = mamba(at)
                    x4 = xs[:, bass.ds(i * TILES, TILES), :]
                    TT(x4, x4, res, ALU.add).then_inc(S["x_updated"].sem, 1)
                    return
                if ph == L2A:
                    for k in range(2):
                        eng.wait_ge(*at("proj_psum", k + 1))
                        b = banks[:, 2 + k, :].rearrange("p (r d) -> p r d", d=8)
                        link(eng.tensor_reduce(wk(9)[:, 0:SEQ], b, AXX, ALU.max))
                        TT(wk(k).rearrange("p (r d) -> p r d", d=8), b, over(wk(9)[:, 0:SEQ], 8),
                           ALU.subtract).then_inc(S["qk_shifted"].sem, 1)
                        eng.wait_ge(*at("qk_shifted", k + 1))
                    eng.wait_ge(*at("kv_psum"))
                    kv = banks[:, 2:4, :].rearrange("p a (s f) -> p (a s) f", f=P)
                    ks = banks[:, 6:8, :].rearrange("p a (s f) -> p (a s) f", f=P)
                    m = times(sq("block8"), SEQS)
                    TT(wk(4, 2).rearrange("p (s f) -> p s f", f=P), kv, m, ALU.mult)
                    TT(wk(6, 2).rearrange("p (s f) -> p s f", f=P), ks, m, ALU.mult)\
                        .then_inc(S["kv_ready"].sem, 1)
                    eng.wait_ge(*at("den_psum"))
                    link(TS(wk(8), banks[:, 5, :], 1e-6, None, ALU.add))
                    link(eng.reciprocal(wk(9), wk(8)))
                    TT(wk(10), wk(9), banks[:, 4, :], ALU.mult).then_inc(S["y_ready"].sem, 1)
                if ph == L3X:
                    link(TT(t4(wk(5)), xn[:, :, :], xn[:, :, :], ALU.mult))
                    link(eng.tensor_reduce(vare[:, :], t4(wk(5)), AXX, ALU.add))
                    TS(vare[:, :], vare[:, :], 1.0 / P, EPS, ALU.mult, ALU.add)\
                        .then_inc(S["var_ready"].sem, 1)
                    eng.wait_ge(*at("rstd_ready", 2))
                    for t in range(TILES):
                        ins = TS(wk(3)[:, t * P:(t + 1) * P], xn[:, t, :], rstd[:, t:t + 1], None, ALU.mult)
                    ins.then_inc(S["xn_ready"].sem, 1)
                    eng.wait_ge(*at("ctx_landed", 16))
                    link(TT(wk(5, 2).rearrange("p (t f) -> p t f", t=TILES), ctxn, ctxn, ALU.mult))
                    link(eng.tensor_reduce(vare[:, :], wk(5, 2).rearrange("p (t f) -> p t f", t=TILES),
                                           AXX, ALU.add))
                    TS(vare[:, :], vare[:, :], 1.0 / CTX, EPS, ALU.mult, ALU.add)\
                        .then_inc(S["var_ready"].sem, 1)
                    eng.wait_ge(*at("rstd_ready", 3))
                    for t in range(TILES):
                        ins = TS(wk(7)[:, t * P:(t + 1) * P], ctxn[:, t, 0:P], rstd[:, t:t + 1], None, ALU.mult)
                    ins.then_inc(S["ctx_used"].sem, 1)
                    eng.wait_ge(*at("ctx_used"))
                    TT(t4(wk(0)), t4(wk(7)), times(fbc[:, 2, :], TILES), ALU.mult)\
                        .then_inc(S["u_scaled"].sem, 1)
                    eng.wait_ge(*at("row_landed", 16))
                    STT(t4(wk(4)), t4(mask_bc), col("iota64"), times(sq("block64"), TILES),
                        ALU.is_equal, ALU.mult).then_inc(S["row_used"].sem, 1)
                add_out(i, at)

            def before(ph):
                if ph == L3F:
                    step(eng.memset(cnt[:, :, :], 0.0))
            groups(eng, "vector", program, before)
    return seen


def host_arrays(a):
    f = lambda n: np.asarray(a[n], np.float32)
    z = {}
    perm_a, perm_b = [0, 2, 1, 3, 4, 6, 5, 7], [1, 3, 0, 2, 5, 7, 4, 6]
    heads = lambda w, p: w.reshape(P, 16, 8)[:, :, p].reshape(P, P)
    heads1 = lambda b, p: b.reshape(16, 8)[:, p].reshape(P)
    rep16 = lambda w: np.tile(w, (1, 16))
    wsrc, wtgt, wout = f("L0_xattn_W_src"), f("L0_xattn_W_tgt"), f("L0_xattn_W_out")
    win, w_out1 = f("L1_attn_W_in"), f("L1_attn_W_out")
    qkv = f("L2_xattn_w_qkv")
    h3 = lambda n: f(n).transpose(1, 0, 2).reshape(P, P)
    tok = np.arange(P)
    step_ = np.exp(-0.001)
    dt = -np.log(-np.expm1(-0.001))
    lag = tok[None, :] % SEQ - tok[:, None] % SEQ
    same = tok[None, :] // SEQ == tok[:, None] // SEQ
    decay = np.where(same & (lag >= 0), step_ * np.exp(-dt * np.maximum(lag, 0)), 0.0)
    q = {
        "l0_q": heads(f("L0_attn_Wq"), perm_a), "l0_qb": heads(f("L0_attn_Wq"), perm_b),
        "l0_k": rep16(f("L0_attn_Wk")[:, perm_a]),
        "l0_v": rep16(f("L0_attn_Wv")), "l0_o": f("L0_attn_Wo"),
        "l0x_k0": wsrc[:P, :P].T, "l0x_k1": wsrc[:P, P:].T, "l0x_v0": wsrc[P:, :P].T, "l0x_v1": wsrc[P:, P:].T,
        "l0x_q": wtgt.T, "l0x_o0": wout[:, :P].T, "l0x_o1": wout[:, P:].T,
        "l1_x0": win[0:P].T, "l1_x1": win[P:2 * P].T, "l1_z0": win[2 * P:3 * P].T, "l1_z1": win[3 * P:4 * P].T,
        "l1_o0": w_out1[:, :P].T, "l1_o1": w_out1[:, P:].T,
        "l2_q": f("L2_attn_Wq").T, "l2_k": f("L2_attn_Wk").T, "l2_v": f("L2_attn_Wv").T, "l2_o": f("L2_attn_Wo").T,
        "l2x_q": qkv[:P].T, "l2x_k": qkv[P:2 * P].T, "l2x_v": qkv[2 * P:].T, "l2x_o": f("L2_xattn_w_proj").T,
        "l3_q": h3("L3_attn_Wq"), "l3_k": h3("L3_attn_Wk"), "l3_v": h3("L3_attn_Wv"), "l3_o": f("L3_attn_Wo"),
        "l3_in": f("L3_xattn_W_in").T,
        "ident": np.eye(P), "ones": np.ones((P, P)), "before": tok[:, None] < tok[None, :],
        "block8": tok[:, None] // 8 == tok[None, :] // 8, "decay": decay, "block64": same,
    }
    theta = (1.0 / 10000.0 ** (np.arange(0, 4, 2, dtype=np.float32) / 4)).astype(np.float32)
    ang = (tok // 8).astype(np.float32) * theta[np.array([0, 1, 0, 1])[tok % 4]]
    cos, sin = np.cos(ang), np.sin(ang) * np.where(tok % 4 < 2, -1, 1)
    z["squares"] = np.stack([q[n] for n in SQUARES], 1).astype(np.float32)
    bsrc = f("L0_xattn_b_src")
    rep_b = lambda b: np.tile(b, 16)
    cb, bdt, dd = f("L1_attn_conv_b"), f("L1_attn_b_dt"), f("L1_attn_D")
    c = {
        "cos": cos, "sin": sin, "l0_q": heads1(f("L0_attn_bq"), perm_a), "l0_qb": heads1(f("L0_attn_bq"), perm_b),
        "l0_k": rep_b(f("L0_attn_bk")[perm_a]),
        "l0x_k": bsrc[:P], "l0x_q": f("L0_xattn_b_tgt"), "l3_q": f("L3_attn_bq").reshape(P),
        "l3_k": f("L3_attn_bk").reshape(P), "l1_cb0": cb[:P], "l1_cb1": cb[P:], "l1_dt0": bdt[:P],
        "l1_dt1": bdt[P:], "l1_d0": dd[:P], "l1_d1": dd[P:], "l1x_b": np.repeat(f("L1_xattn_b"), P),
        "l3_res": f("L3_xattn_g_res"), "iota64": tok % SEQ, "one": np.ones(P), "zero": np.zeros(P),
    }
    z["cols"] = np.stack([c[n] for n in COLS], 1).astype(np.float32)
    r = {
        "l0_v": rep_b(f("L0_attn_bv")), "l0_o": f("L0_attn_bo"), "l0x_v": bsrc[P:], "l0x_o": f("L0_xattn_b_out"),
        "l2_q": f("L2_attn_bq"), "l2_k": f("L2_attn_bk"), "l2_v": f("L2_attn_bv"), "l2_o": f("L2_attn_bo"),
        "l2x_o": f("L2_xattn_b_proj"), "l3_v": f("L3_attn_bv").reshape(P), "l3_o": f("L3_attn_bo"),
        "l3_in": f("L3_xattn_b_in"), "ones": np.ones(P),
    }
    z["rows"] = np.stack([r[n] for n in ROWS])[None].astype(np.float32)
    g = np.zeros((P, 64), np.float32)
    for k, w in enumerate((f("L0_ffn_gate_w").T, f("L1_ffn_gate_w").T, f("L2_ffn_gate_w").T, f("L3_ffn_router_w"))):
        g[:, 16 * k:16 * k + w.shape[1]] = w
    z["gates"] = g
    z["rbias"] = np.tile(f("L3_ffn_router_b"), 4)[None]
    z["rank"] = np.tile(np.arange(16, 0, -1, dtype=np.float32), (P, 1))
    m8 = (tok[:, None] % 32 // 8 == np.arange(4)[None]).astype(np.float64)
    m16 = (tok[:, None] % 32 // 16 == np.arange(2)[None]).astype(np.float64)
    z["headmask"] = np.concatenate([m8, m8 / np.sqrt(8.0), m16, m16 / 4], 1).astype(np.float32)
    z["causal"] = np.where(np.arange(SEQ)[None] <= tok[:, None] % SEQ, 0.0, NEG).astype(np.float32)
    z["rope"] = np.tile(np.stack([cos, sin])[None], (P, 1, 1)).astype(np.float32)
    taps, alog = f("L1_attn_conv_w")[:, 0], f("L1_attn_A_log")
    z["l1w"] = np.concatenate([taps, alog], 1).reshape(2, P, 4 + D_STATE).transpose(1, 0, 2)
    z["bcw"] = win[4 * P:].T
    z["wdt"] = f("L1_attn_W_dt").T.reshape(8, 2, P)
    z["ln_g"], z["ln_b"], z["g_init"] = f("L1_attn_ln_g"), f("L1_attn_ln_b"), f("L3_xattn_g_init")[:P]
    z["maskcol"] = f("mask_BxS2_fk1").reshape(-1, P).T
    z["mask_f"] = f("mask_BxS2_fk1")
    z["mask_i"], z["patch_lens"] = np.asarray(a["mask_BxS2_ik0"]), np.asarray(a["mask_BxS2_if0"])

    def ffn(gate, up, down):
        nf = gate.shape[1]
        t = -(-nf // P)
        o = np.zeros((P, 3, t * P), np.float32)
        o[:, 0, :nf], o[:, 1, :nf] = gate, up
        dp = np.zeros((t * P, P), np.float32)
        dp[:nf] = down
        o[:, 2] = dp.reshape(t, P, P).transpose(1, 0, 2).reshape(P, t * P)
        return o
    efd = lambda n: f(n).transpose(2, 0, 1).reshape(P, -1)
    edf = lambda n: f(n).transpose(0, 2, 1).reshape(-1, P)
    hei = lambda n: f(n).transpose(1, 0, 2).reshape(P, -1)
    z["ffn_l0"] = ffn(efd("L0_ffn_wi_gate"), efd("L0_ffn_wi_up"), edf("L0_ffn_wo"))
    l1 = ffn(np.concatenate([efd("L1_ffn_wg"), f("L1_ffn_sg").T], 1),
             np.concatenate([efd("L1_ffn_wu"), f("L1_ffn_su").T], 1),
             np.concatenate([edf("L1_ffn_wd"), f("L1_ffn_sd").T], 0))
    l2 = ffn(np.concatenate([hei("L2_ffn_wg"), f("L2_ffn_swg")], 1),
             np.concatenate([hei("L2_ffn_wu"), f("L2_ffn_swu")], 1),
             np.concatenate([f("L2_ffn_wd").reshape(-1, P), f("L2_ffn_swd")], 0))
    z["ffn_mid"] = np.concatenate([l1, l2], 2)
    z["ffn_l3"] = ffn(np.concatenate([hei("L3_ffn_w_gate"), f("L3_ffn_sw_gate")], 1),
                      np.concatenate([hei("L3_ffn_w_up"), f("L3_ffn_sw_up")], 1),
                      np.concatenate([f("L3_ffn_w_down").reshape(-1, P), f("L3_ffn_sw_down")], 0))
    for ph, m in MOE.items():
        n = m["e"] * P if ph == L0F else m["nf"]
        per = P if ph == L0F else m["f"]
        z[f"sel{ph}"] = (np.minimum(np.arange(n) // per, m["cols"] - 1)[None] ==
                         np.arange(m["cols"])[:, None]).astype(np.float32)
    z["x"] = f("x").reshape(TOKENS, P)
    z["ctx"] = f("ctx_2048").reshape(TOKENS, CTX)
    return {k: np.ascontiguousarray(v) for k, v in z.items()}


def build(Bacc, arrays, counts):
    nc = Bacc("TRN2", target_bir_lowering=False, num_devices=1)
    d = {n: nc.dram_tensor(f"in_{n}", v.shape, mybir.dt.from_np(v.dtype), kind="ExternalInput").ap()
         for n, v in arrays.items()}
    d["plug"] = nc.dram_tensor("plug", (BATCH, SEQ), F32, kind="Internal").ap()
    out = nc.dram_tensor("out_x", (TOKENS, P), F32, kind="ExternalOutput").ap()
    return nc, decoder(nc, d, out, counts)


COUNTS = {
    "scalar": {L1A: 2},
    "vector": {L0A: 26, L0X: 18, L0F: 30, L1A: 39, L1X: 20, L1F: 19, L2A: 6, L2X: 42, L2F: 24, L3A: 26, L3X: 7, L3F: 33},
}


def kernel(**inputs):
    import concourse.bacc as _bacc
    from concourse.bass_utils import run_bass_kernel_spmd as _run

    arrays = host_arrays(inputs)
    nc = build(_bacc.Bacc, arrays, COUNTS)[0]
    r = _run(nc, [{f"in_{n}": v for n, v in arrays.items()}], core_ids=[0])
    return r.results[0]["out_x"].reshape(BATCH, SEQ, P)
```

```python
from contextlib import ExitStack

import numpy as np

import concourse.bass as bass
from concourse import mybir

F32 = mybir.dt.float32
I32 = mybir.dt.int32
ALU = mybir.AluOpType
ACT = mybir.ActivationFunctionType
AXX = mybir.AxisListType.X

P = 128
BATCH, SEQ, CTX = 128, 64, 256
TOKENS = BATCH * SEQ
TILES = 4
NT = TILES * P
GROUPS = TOKENS // NT
SEQS = NT // SEQ
EPS = 1e-5
NEG = -1e30

L0A, L0X, L0F, L1A, L1X, L1F, L2A, L2X, L2F, L3A, L3X, L3F = range(12)
PHASES = range(12)

MOE = {
    L0F: dict(e=8, f=512, shared=0, cap=int(TOKENS / 8 * 1.25)),
    L1F: dict(e=8, f=64, shared=64, cap=None),
    L2F: dict(e=8, f=176, shared=352, cap=None),
    L3F: dict(e=16, f=176, shared=176, cap=int(np.ceil(1.25 * TOKENS * 2 / 16))),
}
for _m in MOE.values():
    _m["nf"] = _m["e"] * _m["f"] + _m["shared"]
    _m["tiles"] = -(-_m["nf"] // P)
    _m["cols"] = _m["e"] + (1 if _m["shared"] else 0)

ATT = {
    L0A: dict(dh=8, units=4), L0X: dict(dh=16, units=4), L1X: dict(dh=16, units=4),
    L2X: dict(dh=8, units=8), L3A: dict(dh=8, units=4),
}
D_STATE = 16
WOVEN = {**ATT, **MOE}


def slots(ph):
    first = 0 if ph == L1F else 1
    route = [2, 2, 2, 3, 3, 3, 3, 3] if ph == L1F else list(range(3, 11))
    return dict(stats=0, scale=first, turn=first + 1, router=first + 2, route=route, ranks=8,
                weights=4 if ph == L1F else 11)

SQUARES = [
    "l0_q", "l0_qb", "l0_k", "l0_v", "l0_o",
    "l0x_k0", "l0x_k1", "l0x_v0", "l0x_v1", "l0x_q", "l0x_o0", "l0x_o1",
    "l1_x0", "l1_x1", "l1_z0", "l1_z1", "l1_o0", "l1_o1",
    "l2_q", "l2_k", "l2_v", "l2_o", "l2x_q", "l2x_k", "l2x_v", "l2x_o",
    "l3_q", "l3_k", "l3_v", "l3_o", "l3_in",
    "ident", "ones", "before", "block8", "decay", "block64",
]
COLS = [
    "l0_q", "l0_qb", "l0_k", "cos", "sin", "l0x_k", "l0x_q", "l3_q", "l3_k",
    "l1_cb0", "l1_cb1", "l1_dt0", "l1_dt1", "l1_d0", "l1_d1", "l1x_b", "l3_res",
    "iota64", "one", "zero",
]
ROWS = ["l0_v", "l0_o", "l0x_v", "l0x_o", "l2_q", "l2_k", "l2_v", "l2_o", "l2x_o",
        "l3_v", "l3_o", "l3_in", "ones"]
ROUTERS = [L0F, L1F, L2F, L3F]


def per_group():
    units = {ph: a["units"] for ph, a in ATT.items()}
    tiles = {ph: m["tiles"] for ph, m in MOE.items()}
    every = {ph: 1 for ph in range(12)}
    steps = {L1A: 2 * D_STATE}
    states = {L1A: D_STATE}
    return {
        "x_updated": every, "var_ready": {**every, L1A: 2, L3X: 3}, "rstd_ready": {**every, L1A: 2, L3X: 3},
        "xn_ready": every, "xnt_psum": every, "xnt_ready": every,
        "ctx_landed": {L0X: 16, L1X: 16, L2X: 16, L3X: 16}, "ctx_values_landed": {L2X: 16}, "ctx_psum": {L0X: 2, L1X: 1, L2X: 1},
        "ctxt_ready": {L0X: 2, L1X: 1, L2X: 1}, "ctx_used": {L3X: 1},
        "row_landed": {L0X: 16, L1X: 16, L3X: 16}, "row_used": {L1X: 1, L3X: 1},
        "proj_psum": {L0A: 3, L0X: 3, L1A: 7, L2A: 3, L2X: 2, L3A: 3},
        "qt_ready": {ph: 1 for ph in ATT}, "kt_ready": {ph: 1 for ph in ATT},
        "v_ready": {L0A: 1, L0X: 1, L1X: 1, L2A: 1, L2X: 1, L3A: 1},
        "qbd_ready": {ph: 1 for ph in ATT},
        "scores_psum": units, "shifted_ready": units, "exp_ready": units,
        "rsum_ready": units, "probs_ready": units, "probst_psum": units, "probst_ready": units,
        "xn_kept": {L0X: 1}, "xnt_held": {ph: 1 for ph in MOE}, "cwt_held": {ph: 1 for ph in MOE}, "v_held": {L0A: 1, L3A: 1}, "heads_psum": units, "heads_read": units, "out_psum": {**every},
        "logits_psum": {ph: 1 for ph in MOE}, "logits_shifted": {ph: 1 for ph in MOE},
        "logits_exp": {ph: 1 for ph in MOE}, "picks_ready": {L0F: 1, L3F: 1}, "ranks_psum": {L0F: 1, L3F: 1},
        "cw_ready": {ph: 1 for ph in MOE}, "cwt_psum": {ph: 1 for ph in MOE}, "cwt_ready": {ph: 1 for ph in MOE},
        "gate_psum": tiles, "up_psum": tiles, "silu_ready": tiles, "h_ready": tiles, "down_done": tiles,
        "wbc_psum": {**tiles, L0F: 8}, "wbc_read": {**tiles, L0F: 8},
        "yt_ready": {**{ph: 1 for ph in MOE}},
        "conv_ready": {L1A: 1}, "xs_padded": {L1A: 1}, "u_ready": {L1A: 1}, "zs_ready": {L1A: 1},
        "dtr_ready": {L1A: 1}, "soft_exp": {L1A: 1}, "soft_ready": {L1A: 1}, "dt_ready": {L1A: 1}, "du_ready": {L1A: 1},
        "b_psum": states, "c_psum": states, "c_ready": states, "b_read": states,
        "da_ready": steps, "scan_ready": steps, "hc_ready": steps, "hc_used": steps,
        "ym_psum": {L1A: 1}, "ym_ready": {L1A: 1},
        "qk_shifted": {L2A: 2}, "qk_exp": {L2A: 2}, "qkt_psum": {L2A: 1}, "qkt_ready": {L2A: 1},
        "kv_psum": {L2A: 1}, "kv_ready": {L2A: 1}, "den_psum": {L2A: 1}, "y_ready": {L2A: 1},
        "dep_psum": {L3X: 1}, "dep_ready": {L3X: 1}, "u_scaled": {L3X: 1},
    }


class Signal:

    def __init__(self, sem, per):
        self.sem, self.per, self.base = sem, per, {}
        total = 0
        for ph in PHASES:
            self.base[ph] = total
            total += GROUPS * per.get(ph, 0)

    def at(self, ph, i, k):
        return self.base[ph] + i * self.per[ph] + k


class Chain:

    def __init__(self, sem, per):
        self.sem, self.base, self.per = sem, {}, per
        total = 0
        for ph in PHASES:
            self.base[ph] = total
            if ph in WOVEN:
                start, body, last = per.get(ph, (0, 0, 0))
                total += start + (GROUPS - 1) * body + last
            else:
                total += GROUPS * per.get(ph, 0)

    def enter(self, eng, ph, i, start=False):
        self.eng, self.n = eng, 0
        if ph in WOVEN:
            before, body, _ = self.per.get(ph, (0, 0, 0))
            self.from_ = self.base[ph] if start else self.base[ph] + before + i * body
        else:
            self.from_ = self.base[ph] + i * self.per.get(ph, 0)

    def __call__(self, ins):
        self.n += 1
        ins.then_inc(self.sem, 1)
        self.eng.wait_ge(self.sem, self.from_ + self.n)


def decoder(nc, d, out_dram, counts):
    ctx = ExitStack()
    with ctx:
        def sb(name, shape, dt=F32):
            return ctx.enter_context(nc.sbuf_tensor(name, shape, dt))

        xs = sb("xs", [P, TOKENS // P, P])
        square = {n: k for k, n in enumerate(SQUARES)}
        squares = sb("squares", [P, len(SQUARES), P])
        cols = sb("cols", [P, len(COLS)])
        rows = sb("rows", [1, len(ROWS), P])
        gates = sb("gates", [P, 4 * 16])
        rbias = sb("rbias", [1, 64])
        rank = sb("rank", [P, 16])
        headmask = sb("headmask", [P, 12])
        causal = sb("causal", [P, SEQ])
        rope = sb("rope", [P, 2, P])
        l1w = sb("l1w", [P, 2, 4 + D_STATE])
        bcw = sb("bcw", [P, 2 * D_STATE + 8])
        wdt = sb("wdt", [8, 2, P])
        fbc = sb("fbc", [P, 3, P])
        maskcol = sb("maskcol", [P, TOKENS // P])

        big = sb("big", [P, 3, 8 * 512])
        small = sb("small", [P, 3, (MOE[L1F]["tiles"] + MOE[L2F]["tiles"]) * P])
        sel = sb("sel", [17, 24 * P])

        stats = sb("stats", [P, TILES, 6])
        mv = sb("mv", [P, TILES, 2])
        vare = sb("vare", [P, 4])
        rstd = sb("rstd", [P, 4])
        power = sb("power", [P, 4])
        xn = sb("xn", [P, TILES, P])
        xnt = sb("xnt", [P, NT])
        xpad = sb("xpad", [P, 2, SEQS, SEQ + 3])
        work = sb("work", [P, 20 * 512])

        def wk(k, n=1):
            return work[:, k * 512:(k + n) * 512]

        banks = ctx.enter_context(nc.psum_tensor("banks", [P, 8, 512], F32))

        names = per_group()
        S = {n: Signal(ctx.enter_context(nc.semaphore(n)), per) for n, per in names.items()}
        chains = {e: Chain(ctx.enter_context(nc.semaphore(e + "_step")), counts.get(e, {}))
                  for e in ("vector", "scalar", "gpsimd", "tensor")}
        loaded = ctx.enter_context(nc.semaphore("loaded"))
        l0_loaded = ctx.enter_context(nc.semaphore("l0_loaded"))
        l3_loaded = ctx.enter_context(nc.semaphore("l3_loaded"))
        sel_loaded = ctx.enter_context(nc.semaphore("sel_loaded"))
        plug_step = ctx.enter_context(nc.semaphore("plug_step"))
        a_exp = ctx.enter_context(nc.semaphore("a_exp"))
        a_ready = ctx.enter_context(nc.semaphore("a_ready"))
        setup_done = ctx.enter_context(nc.semaphore("setup_done"))
        plug_done = ctx.enter_context(nc.semaphore("plug_done"))
        plug_stored = ctx.enter_context(nc.semaphore("plug_stored"))
        out_stored = ctx.enter_context(nc.semaphore("out_stored"))
        seen = {}

        def sq(n):
            return squares[:, square[n], :]

        def col(n):
            k = COLS.index(n)
            return cols[:, k:k + 1]

        def row(n):
            return rows[0:1, ROWS.index(n), :]

        ones_row = rows[0:1, ROWS.index("ones"), 0:P]
        ident = sq("ident")

        def over(ap, n):
            return ap.unsqueeze(2).broadcast_to([ap.shape[0], ap.shape[1], n])

        def times(ap, n):
            return ap.unsqueeze(1).broadcast_to([ap.shape[0], n, ap.shape[1]])

        def t4(ap):
            return ap.rearrange("p (t f) -> p t f", t=TILES)

        qt, kt, vt = wk(0), wk(1), wk(2)
        qbd = wk(3, 4)
        sc = [wk(7, 2), wk(9, 2)]
        pt = wk(11, 2)
        ht = wk(13)
        ctxn = wk(14, 2).rearrange("p (t f) -> p t f", t=TILES)
        ctxt = wk(16, 2)
        mask_bc = wk(18)
        mask_add = wk(19)
        tmp1, tmp2 = wk(7), wk(8)
        att_small = sb("att_small", [P, 3, 16])
        RT = sb("rt", [P, 24, 4, 17])
        cnt = sb("cnt", [P, 5, 16])
        NB, OB = banks[:, 0, :], banks[:, 1, :]
        TURN = {L0A: banks[:, 4, :], L3A: banks[:, 4, :], L0X: banks[:, 7, :], L1X: banks[:, 7, :], L2X: OB}
        VALUES = {L0A: banks[:, 5, :], L3A: banks[:, 5, :], L0X: banks[:, 7, :]}

        def groups(eng, name, program, woven, before=None):
            chain = chains[name]
            for ph in PHASES:
                if ph in WOVEN:
                    if ph != PHASES[0]:
                        eng.wait_ge(S["x_updated"].sem, S["x_updated"].at(ph, 0, 0))
                    chain.enter(eng, ph, 0, True)
                    if before:
                        before(ph)
                    woven(ph, None, Front(ph, 0, 0))
                    n = [chain.n]
                    with eng.Fori(0, GROUPS - 1) as i:
                        chain.enter(eng, ph, i)
                        woven(ph, i, Front(ph, i, 1))
                    n.append(chain.n)
                    chain.enter(eng, ph, GROUPS - 1)
                    woven(ph, GROUPS - 1, None)
                    seen[name, ph] = (*n, chain.n)
                    continue
                def one(i, first=False):
                    chain.enter(eng, ph, i)
                    if not first:
                        eng.wait_ge(S["x_updated"].sem, S["x_updated"].at(ph, i, 0))
                    program(ph, i)
                    seen[name, ph] = chain.n
                if ph == PHASES[0]:
                    one(0, True)
                    with eng.Fori(1, GROUPS) as i:
                        one(i)
                else:
                    with eng.Fori(0, GROUPS) as i:
                        one(i)

        class Front:

            def __init__(self, ph, i, ahead):
                self.ph, self.i, self.ahead = ph, i, ahead

            def at(self, name, k=1):
                return S[name].sem, S[name].at(self.ph, self.i, k + self.ahead * S[name].per[self.ph])

            def tile(self, t):
                return self.i * TILES + (self.ahead * TILES + t)

        def values_of(ph, i):
            return lambda name, k=1: (S[name].sem, S[name].at(ph, i, k))

        def ffn_weights(ph):
            m = MOE[ph]
            nf = m["nf"]
            if ph in (L0F, L3F):
                r = big
                a = 0
            else:
                r = small
                a = 0 if ph == L1F else MOE[L1F]["tiles"] * P
            n = m["tiles"] * P
            return (r[:, 0, a:a + nf], r[:, 1, a:a + nf],
                    r[:, 2, a:a + n].rearrange("p (t f) -> p t f", f=P))

        def apart(eng):
            eng.wait_ge(loaded, N_LOADED)

        N_LOADED = 16 * 18
        block = ctx.enter_context(nc.Block())

        @block.sync
        def _(sp):
            x_src = d["x"].rearrange("(t p) f -> p t f", p=P)
            sp.dma_start(xs[:, :, :], x_src).then_inc(loaded, 16)
            for dst, name in ((squares[:, :, :], "squares"), (cols[:, :], "cols"), (rows[:, :, :], "rows"),
                              (gates[:, :], "gates"), (rbias[:, :], "rbias"), (rank[:, :], "rank"),
                              (headmask[:, :], "headmask"), (causal[:, :], "causal"), (rope[:, :, :], "rope"),
                              (l1w[:, :, :], "l1w"), (bcw[:, :], "bcw"), (wdt[:, :, :], "wdt"),
                              (maskcol[:, :], "maskcol"), (work[:, 0:SEQ].bitcast(I32), "patch_lens")):
                sp.dma_start(dst, d[name]).then_inc(loaded, 16)
            for k, name in enumerate(("ln_g", "ln_b", "g_init")):
                sp.dma_start(fbc[:, k, :], d[name].partition_broadcast(P)).then_inc(loaded, 16)
            sp.dma_start(big[:, :, :], d["ffn_l0"]).then_inc(l0_loaded, 16)
            sp.dma_start(small[:, :, 0:d["ffn_mid"].shape[2]], d["ffn_mid"]).then_inc(l0_loaded, 16)
            sp.wait_ge(plug_done, 1)
            sp.dma_start(d["plug"], work[:, SEQ:2 * SEQ]).then_inc(plug_stored, 16)
            sp.wait_ge(plug_stored, 16)
            nsel = 0
            for ph in PHASES:
                if ph in MOE:
                    m = MOE[ph]
                    if ph != PHASES[0]:
                        sp.wait_ge(S["x_updated"].sem, S["x_updated"].at(ph, 0, 0))
                    n = m["e"] * P if ph == L0F else m["nf"]
                    sp.dma_start(sel[0:m["cols"], 0:n], d[f"sel{ph}"]).then_inc(sel_loaded, 16)
                if ph == L0F + 1:
                    sp.wait_ge(S["x_updated"].sem, S["x_updated"].at(ph, 0, 0))
                    sp.dma_start(big[:, :, 0:24 * P], d["ffn_l3"]).then_inc(l3_loaded, 16)
                if ph in (L0X, L1X, L2X, L3X):
                    if ph != PHASES[0]:
                        sp.wait_ge(S["x_updated"].sem, S["x_updated"].at(ph, 0, 0))
                    def load(i, first=False):
                        if not first:
                            for name in {L1X: ("ctx_psum", "v_ready"), L3X: ("ctx_used",)}.get(ph, ("ctx_psum",)):
                                sp.wait_ge(S[name].sem, S[name].at(ph, i, 0))
                        src = d["ctx"][bass.ds(i * NT, NT), :]
                        sp.dma_start(ctxn, src.rearrange("(t p) f -> p t f", p=P))\
                            .then_inc(S["ctx_landed"].sem, 16)
                        if ph == L2X:
                            if not first:
                                sp.wait_ge(S["heads_psum"].sem, S["heads_psum"].at(ph, i, 0))
                            sp.dma_start(wk(18, 2).rearrange("p (s f) -> p s f", s=SEQS)[0:SEQ],
                                         src[:, P:CTX].rearrange("(s k) f -> k s f", k=SEQ))\
                                .then_inc(S["ctx_values_landed"].sem, 16)
                        else:
                            if not first:
                                used = S["kt_ready" if ph == L0X else "row_used"]
                                sp.wait_ge(used.sem, used.at(ph, i, 0))
                            name = {L0X: "mask_f", L1X: "mask_i", L3X: "plug"}[ph]
                            dst = mask_bc.bitcast(I32) if ph == L1X else mask_bc
                            per_token = d[name][bass.ds(i * SEQS, SEQS), :].rearrange("b s -> (b s)")
                            sp.dma_start(dst, per_token.partition_broadcast(P)).then_inc(S["row_landed"].sem, 16)
                    load(0, True)
                    with sp.Fori(1, GROUPS) as i:
                        load(i)
            last = S["x_updated"]
            sp.wait_ge(last.sem, last.at(PHASES[-1], GROUPS, 0))
            sp.dma_start(out_dram.rearrange("(t p) f -> p t f", p=P), xs[:, :, :]).then_inc(out_stored, 16)
            sp.wait_ge(out_stored, 16)

        def pool_normalise(ph, u, eng, at):
            n = 8 if ATT[ph]["dh"] == 16 or ph == L2X else 16
            kl = (NT * 2 if ATT[ph]["dh"] == 8 else NT) // n
            e = sc[u % 2][:, 0:n * kl].rearrange("p (r k) -> p r k", k=kl)
            eng.wait_ge(*at("rsum_ready", u + 1))
            eng.tensor_tensor(e, e, over(att_small[:, 2, 0:n], kl), ALU.mult)\
                .then_inc(S["probs_ready"].sem, 1)

        def pool_rstd(at, eng, k):
            eng.wait_ge(*at("var_ready", k))
            eng.tensor_tensor(rstd[:, :], vare[:, :], power[:, :], ALU.pow).then_inc(S["rstd_ready"].sem, 1)

        @block.gpsimd
        def _(eng):
            eng.memset(power[:, :], -0.5).then_inc(setup_done, 1)
            eng.wait_ge(setup_done, 1)

            def program(ph, i):
                at = values_of(ph, i)
                pool_rstd(at, eng, 1)
                if ph == L3X:
                    pool_rstd(at, eng, 2)
                    pool_rstd(at, eng, 3)
                if ph == L1A:
                    eng.wait_ge(*at("dt_ready"))
                    eng.tensor_tensor(wk(6, 2), wk(2, 2), wk(4, 2), ALU.mult).then_inc(S["du_ready"].sem, 1)
                    for s in range(2 * D_STATE):
                        eng.wait_ge(*at("scan_ready", s + 1))
                        eng.wait_ge(*at("c_ready", s // 2 + 1))
                        if s >= 2:
                            eng.wait_ge(*at("hc_used", s - 1))
                        eng.tensor_tensor(wk(16 + s % 2), wk(14 + s % 2), wk(18 + s // 2 % 2), ALU.mult)\
                            .then_inc(S["hc_ready"].sem, 1)
                    pool_rstd(at, eng, 2)

            def woven(ph, i, front):
                if i is None:
                    pool_rstd(front.at, eng, 1)
                    return
                if ph in MOE:
                    if front:
                        pool_rstd(front.at, eng, 1)
                    return
                at = values_of(ph, i)
                units = ATT[ph]["units"]
                for u in range(units):
                    pool_normalise(ph, u, eng, at)
                    if u == units - 4 and front:
                        pool_rstd(front.at, eng, 1)
            groups(eng, "gpsimd", program, woven)

        @block.scalar
        def _(eng):
            link = chains["scalar"]
            eng.wait_ge(loaded, N_LOADED)
            eng.activation(l1w[:, :, 4:], l1w[:, :, 4:], ACT.Exp).then_inc(a_exp, 1)

            def transposed(at):
                eng.wait_ge(*at("xnt_psum"))
                eng.activation(xnt[:, :], NB, ACT.Copy).then_inc(S["xnt_ready"].sem, 1)

            def spread_heads(ph, at):
                a = ATT[ph]
                eng.wait_ge(*at("qt_ready"))
                dst = qbd.rearrange("p (b h s) -> p b h s", h=4, s=SEQ)
                m = 4 if a["dh"] == 8 else 10
                for h in range(32 // a["dh"]):
                    ins = eng.activation(dst[:, :, h, :], qt.rearrange("p (b s) -> p b s", s=SEQ), ACT.Copy,
                                         scale=headmask[:, m + h:m + h + 1])
                ins.then_inc(S["qbd_ready"].sem, 1)

            def xnt_out(ph, at):
                eng.wait_ge(*at("xnt_psum"))
                eng.activation(xnt[:, :], TURN[ph], ACT.Copy)\
                    .then_inc(S["xnt_ready"].sem, 1)

            def ctxt_out(ph, at, k):
                eng.wait_ge(*at("ctx_psum", k + 1))
                eng.activation(ctxt[:, k * 512:(k + 1) * 512], TURN[ph], ACT.Copy)\
                    .then_inc(S["ctxt_ready"].sem, 1)

            def v_hold(at):
                eng.wait_ge(*at("proj_psum", 3))
                eng.activation(wk(14), VALUES[L0A], ACT.Copy).then_inc(S["v_held"].sem, 1)

            def v_out(ph, front):
                at = front.at
                if ph == L1X:
                    eng.wait_ge(*at("ctx_landed", 16))
                    ins = eng.activation(t4(vt), ctxn[:, :, P:CTX], ACT.Copy)
                elif ph == L2X:
                    eng.wait_ge(*at("proj_psum", 2))
                    ins = eng.activation(wk(18, 2)[SEQ:P], banks[SEQ:P, 6:8, :].rearrange("p a n -> p (a n)"),
                                         ACT.Copy)
                elif ph == L0X:
                    eng.wait_ge(*at("proj_psum", 3))
                    for t in range(TILES):
                        ins = eng.activation(t4(vt)[:, t, :], t4(VALUES[ph])[:, t, :], ACT.Copy,
                                             scale=maskcol[:, bass.ds(front.tile(t), 1)])
                else:
                    eng.wait_ge(*at("v_held"))
                    ins = eng.activation(vt, wk(14), ACT.Copy)
                ins.then_inc(S["v_ready"].sem, 1)

            def attend(ph, i, front):
                if i is None:
                    xnt_out(ph, front.at)
                    for k in range({L0X: 2, L1X: 1, L2X: 1}.get(ph, 0)):
                        ctxt_out(ph, front.at, k)
                    spread_heads(ph, front.at)
                    if ph in (L0A, L3A):
                        v_hold(front.at)
                    v_out(ph, front)
                    return
                at = values_of(ph, i)
                a = ATT[ph]
                units = a["units"]
                n = 1024 if a["dh"] == 8 else 512
                for u in range(units + 1):
                    if u < units:
                        eng.wait_ge(*at("shifted_ready", u + 1))
                        eng.activation(sc[u % 2][:, 0:n], sc[u % 2][:, 0:n], ACT.Exp)\
                            .then_inc(S["exp_ready"].sem, 1)
                    if u == 0 and ph == L0X:
                        eng.wait_ge(*at("xnt_ready"))
                        eng.activation(wk(12), xnt[:, :], ACT.Copy).then_inc(S["xn_kept"].sem, 1)
                        eng.wait_ge(*at("xn_kept"))
                    if u >= 1:
                        eng.wait_ge(*at("probst_psum", u))
                        if u >= 2:
                            eng.wait_ge(*at("heads_psum", u - 1))
                        eng.activation(pt[:, 0:n], banks[:, 6:8, :].rearrange("p a n -> p (a n)")[:, 0:n],
                                       ACT.Copy).then_inc(S["probst_ready"].sem, 1)
                    if front and u == units - 2 and ph not in (L0A, L3A):
                        xnt_out(ph, front.at)
                        if ph != L2X:
                            ctxt_out(ph, front.at, 0)
                    if front and u == units - 1:
                        if ph in (L0A, L3A):
                            xnt_out(ph, front.at)
                        if ph == L0X:
                            ctxt_out(ph, front.at, 1)
                        if ph == L2X:
                            ctxt_out(ph, front.at, 0)
                        spread_heads(ph, front.at)
                        if ph in (L0A, L3A):
                            v_hold(front.at)
                if front:
                    eng.wait_ge(*at("heads_psum", units))
                    v_out(ph, front)

            def feed_forward(ph, i, front):
                m = MOE[ph]
                tiles = m["tiles"]
                z = slots(ph)
                at = None if i is None else values_of(ph, i)

                def hold_tokens():
                    eng.wait_ge(*front.at("xnt_psum"))
                    eng.activation(wk(8), NB, ACT.Copy).then_inc(S["xnt_held"].sem, 1)

                def logits():
                    eng.wait_ge(*front.at("logits_shifted"))
                    eng.activation(RT[:, 1, :, 0:m["e"]], RT[:, 0, :, 0:m["e"]], ACT.Exp)\
                        .then_inc(S["logits_exp"].sem, 1)

                def hold_weights():
                    eng.wait_ge(*front.at("cwt_psum"))
                    eng.activation(wk(9)[0:m["cols"], :], NB[0:m["cols"], :], ACT.Copy)\
                        .then_inc(S["cwt_held"].sem, 1)

                def hand_over():
                    eng.wait_ge(*front.at("xnt_held"))
                    eng.activation(xnt[:, :], wk(8), ACT.Copy).then_inc(S["xnt_ready"].sem, 1)
                    eng.wait_ge(*front.at("cwt_held"))
                    eng.activation(wk(0)[0:m["cols"], :], wk(9)[0:m["cols"], :], ACT.Copy)\
                        .then_inc(S["cwt_ready"].sem, 1)
                    silu(0, front.at)

                def silu(f, at):
                    r = min(P, m["nf"] - f * P)
                    eng.wait_ge(*at("gate_psum", f + 1))
                    if f >= 2:
                        eng.wait_ge(*at("h_ready", f - 1))
                    eng.activation(wk(1 + f % 2)[0:r], banks[0:r, 2 + f % 2, :], ACT.Silu)\
                        .then_inc(S["silu_ready"].sem, 1)

                if i is None:
                    hold_tokens()
                    logits()
                    hold_weights()
                    hand_over()
                    return
                for f in range(1, tiles):
                    silu(f, at)
                    if front:
                        if f == z["turn"]:
                            hold_tokens()
                        if f == z["route"][0]:
                            logits()
                        if f == z["weights"]:
                            hold_weights()
                if front:
                    eng.wait_ge(*at("up_psum", tiles))
                    hand_over()
                eng.wait_ge(*at("down_done", tiles))
                eng.activation(wk(7), banks[:, 7, :], ACT.Copy).then_inc(S["yt_ready"].sem, 1)

            def woven(ph, i, front):
                (attend if ph in ATT else feed_forward)(ph, i, front)

            def program(ph, i):
                at = values_of(ph, i)
                if ph != L3X:
                    transposed(at)
                if ph == L2A:
                    for k in range(2):
                        eng.wait_ge(*at("qk_shifted", k + 1))
                        eng.activation(wk(k), wk(k), ACT.Exp).then_inc(S["qk_exp"].sem, 1)
                    eng.wait_ge(*at("proj_psum", 3))
                    eng.activation(wk(2), banks[:, 4, :], ACT.Copy).then_inc(S["v_ready"].sem, 1)
                    eng.wait_ge(*at("qkt_psum"))
                    eng.activation(wk(3), banks[:, 5, :], ACT.Copy).then_inc(S["qkt_ready"].sem, 1)
                if ph == L1A:
                    mamba(at)
                if ph == L3X:
                    eng.wait_ge(*at("xnt_psum"))
                    eng.activation(xnt[:, :], NB, ACT.Copy, scale=col("l3_res"))\
                        .then_inc(S["xnt_ready"].sem, 1)
                    eng.wait_ge(*at("dep_psum"))
                    eng.activation(wk(2), banks[:, 2, :], ACT.Copy).then_inc(S["dep_ready"].sem, 1)

            def mamba(at):
                for h in range(2):
                    eng.wait_ge(*at("proj_psum", h + 1))
                    ins = eng.activation(xpad[:, h, :, 3:], banks[:, 2 + h, :].rearrange("p (b s) -> p b s", s=SEQ),
                                         ACT.Copy)
                ins.then_inc(S["xs_padded"].sem, 1)
                eng.wait_ge(*at("proj_psum", 5))
                eng.activation(wk(12)[0:8], banks[0:8, 6, :], ACT.Copy).then_inc(S["dtr_ready"].sem, 1)
                for h in range(2):
                    eng.wait_ge(*at("proj_psum", 3 + h))
                    ins = eng.activation(wk(10 + h), banks[:, 4 + h, :], ACT.Silu)
                ins.then_inc(S["zs_ready"].sem, 1)
                eng.wait_ge(*at("conv_ready"))
                for h in range(2):
                    ins = eng.activation(wk(4 + h), wk(h), ACT.Silu, bias=col(f"l1_cb{h}"))
                ins.then_inc(S["u_ready"].sem, 1)
                for h in range(2):
                    eng.wait_ge(*at("proj_psum", 6 + h))
                    link(eng.activation(wk(8 + h), banks[:, (7, 1)[h], :], ACT.Abs, bias=col(f"l1_dt{h}")))
                for h in range(2):
                    ins = eng.activation(wk(8 + h), wk(8 + h), ACT.Exp, scale=-1.0)
                ins.then_inc(S["soft_exp"].sem, 1)
                eng.wait_ge(*at("soft_exp"))
                for h in range(2):
                    ins = eng.activation(wk(12 + h), wk(8 + h), ACT.Ln, bias=col("one"))
                ins.then_inc(S["soft_ready"].sem, 1)
                eng.wait_ge(*at("dt_ready"))
                for n in range(D_STATE):
                    eng.wait_ge(*at("c_psum", n + 1))
                    if n >= 2:
                        eng.wait_ge(*at("hc_ready", 2 * n - 2))
                    eng.activation(wk(18 + n % 2), banks[:, 4 + n % 2, :], ACT.Copy)\
                        .then_inc(S["c_ready"].sem, 1)
                    for h in range(2):
                        s = 2 * n + h
                        if s >= 2:
                            eng.wait_ge(*at("scan_ready", s - 1))
                        eng.activation(wk(h), wk(8 + h), ACT.Exp, scale=l1w[:, h, 4 + n:5 + n])\
                            .then_inc(S["da_ready"].sem, 1)
            groups(eng, "scalar", program, woven)

        @block.tensor
        def _(eng):
            eng.wait_ge(loaded, N_LOADED)
            mm = eng.matmul

            def transposes(dst, src_tiles):
                for t, src in enumerate(src_tiles):
                    ins = eng.transpose(dst[:, t * P:(t + 1) * P], src, ident)
                return ins

            def token_major(out, bias, *products):
                for t in range(TILES):
                    c = slice(t * P, (t + 1) * P)
                    dst = out[:, c]
                    mm(dst, ones_row, row(bias), start=True, stop=False)
                    for k, (src, weight) in enumerate(products):
                        ins = mm(dst, src[:, c], weight if weight.shape[1] == P else weight[:, c],
                                 start=False, stop=k == len(products) - 1)
                return ins

            def turn_context(ph, at, k):
                if k == 0:
                    eng.wait_ge(*at("ctx_landed", 16))
                    eng.wait_ge(*at("xnt_ready"))
                else:
                    eng.wait_ge(*at("ctxt_ready", k))
                transposes(TURN[ph], [ctxn[:, t, k * P:(k + 1) * P] for t in range(TILES)])\
                    .then_inc(S["ctx_psum"].sem, 1)

            def turn_tokens(ph, at):
                eng.wait_ge(*at("xn_ready"))
                transposes(TURN[ph], [xn[:, t, :] for t in range(TILES)]).then_inc(S["xnt_psum"].sem, 1)

            def projections(ph, at):
                if ph == L1X:
                    return
                eng.wait_ge(*at("xnt_ready"))
                if ph == L0X:
                    eng.wait_ge(*at("ctxt_ready", 2))
                    project("l0x_q", banks[:, 2, :]).then_inc(S["proj_psum"].sem, 1)
                    mm(banks[:, 3, :], sq("l0x_k0"), ctxt[:, 0:NT], start=True, stop=False)
                    mm(banks[:, 3, :], sq("l0x_k1"), ctxt[:, NT:2 * NT], start=False, stop=True)\
                        .then_inc(S["proj_psum"].sem, 1)
                    token_major(VALUES[ph], "l0x_v", (ctxt[:, 0:NT], sq("l0x_v0")),
                                (ctxt[:, NT:], sq("l0x_v1"))).then_inc(S["proj_psum"].sem, 1)
                elif ph == L2X:
                    project("l2x_q", banks[:, 2, :])
                    project("l2x_k", banks[:, 3, :]).then_inc(S["proj_psum"].sem, 1)
                else:
                    n = "l0" if ph == L0A else "l3"
                    project(n + "_q", banks[:, 2, :]).then_inc(S["proj_psum"].sem, 1)
                    project(n + "_k", banks[:, 3, :]).then_inc(S["proj_psum"].sem, 1)
                    token_major(VALUES[ph], n + "_v", (xnt, sq(n + "_v")))\
                        .then_inc(S["proj_psum"].sem, 1)

            def own_values():
                own = banks[SEQ:P, 6:8, :].rearrange("p a n -> p (a n)")
                for s in range(SEQS):
                    ins = mm(own[:, s * P:(s + 1) * P], xnt[:, s * SEQ:(s + 1) * SEQ], sq("l2x_v"),
                             start=True, stop=True, tile_position=(0, SEQ))
                ins.then_inc(S["proj_psum"].sem, 1)

            def attend(ph, i, front):
                at = None if i is None else values_of(ph, i)
                a = ATT[ph]
                dh = a["dh"]
                hg, units = 32 // dh, a["units"]
                pairs = hg // 2
                J = 4 * pairs
                q = qbd.rearrange("p (b n) -> p b n", b=SEQS)
                probs_bank = banks[:, 6:8, :].rearrange("p a n -> p (a n)")

                def scores(u):
                    if u == 0:
                        eng.wait_ge(*front.at("qbd_ready"))
                        eng.wait_ge(*front.at("kt_ready"))
                    else:
                        eng.wait_ge(*at("shifted_ready", u))
                    for j in range(J):
                        g, jj = divmod(j, pairs)
                        part = slice(32 * g, 32 * g + 32)
                        for b in range(2):
                            if ph == L2X:
                                seq, keys = u, (ctxt[part, u * SEQ:(u + 1) * SEQ] if b == 0 else
                                                kt[part, u * SEQ:(u + 1) * SEQ])
                            else:
                                seq = 2 * u + b
                                keys = kt[part, seq * SEQ:(seq + 1) * SEQ]
                            c = (jj * 2 + b) * SEQ
                            ins = mm(banks[:, 2 + g, c:c + SEQ], q[part, seq, jj * P:(jj + 1) * P], keys,
                                     start=True, stop=True, tile_position=(32 * g, 0))
                    ins.then_inc(S["scores_psum"].sem, 1)

                def turn(u):
                    if u == 0:
                        eng.wait_ge(*at("v_ready"))
                    eng.wait_ge(*at("probs_ready", u + 1))
                    if u >= 1:
                        eng.wait_ge(*at("probst_ready", u))
                    for j in range(J):
                        ins = eng.transpose(probs_bank[:, j * P:(j + 1) * P], sc[u % 2][:, j * P:(j + 1) * P],
                                            ident)
                    ins.then_inc(S["probst_psum"].sem, 1)

                def values(u):
                    apart(eng)
                    if u == 0:
                        eng.wait_ge(*at("v_ready"))
                        if ph == L2X:
                            eng.wait_ge(*at("ctx_values_landed", 16))
                    eng.wait_ge(*at("probst_ready", u + 1))
                    if u >= 1:
                        eng.wait_ge(*at("heads_read", u))
                    n = hg * SEQ
                    for g in range(4):
                        if ph == L2X:
                            v = wk(18, 2).rearrange("p (s f) -> p s f", s=SEQS)[:, u, 32 * g:32 * g + 32]
                            ins = mm(banks[32 * g:32 * g + 32, 0, 0:n], v, pt[:, g * n:(g + 1) * n],
                                     start=True, stop=True, tile_position=(0, 32 * g))
                        else:
                            for b in range(2):
                                part = slice(b * SEQ, (b + 1) * SEQ)
                                v = t4(vt)[part, u, 32 * g:32 * g + 32]
                                ins = mm(banks[32 * g:32 * g + 32, b, 0:n], v,
                                         pt[part, g * n:(g + 1) * n], start=True, stop=True,
                                         tile_position=(b * SEQ, 32 * g))
                    ins.then_inc(S["heads_psum"].sem, 1)

                if i is None:
                    turn_tokens(ph, front.at)
                    for k in range({L0X: 2, L1X: 1, L2X: 1}.get(ph, 0)):
                        turn_context(ph, front.at, k)
                    projections(ph, front.at)
                    if ph == L2X:
                        own_values()
                    if ph in (L0A, L3A):
                        eng.wait_ge(*front.at("v_held"))
                    scores(0)
                    return
                for u in range(units):
                    if u + 1 < units:
                        scores(u + 1)
                    if u >= 1:
                        values(u - 1)
                    if front and u == units - 2 and ph not in (L0A, L3A):
                        turn_tokens(ph, front.at)
                        if ph in (L0X, L1X):
                            turn_context(ph, front.at, 0)
                    if front and u == units - 1:
                        if ph == L0X:
                            turn_context(ph, front.at, 1)
                        eng.wait_ge(*at("shifted_ready", units))
                        if ph in (L0A, L3A):
                            turn_tokens(ph, front.at)
                        projections(ph, front.at)
                        if ph == L2X:
                            turn_context(ph, front.at, 0)
                    turn(u)
                if front:
                    if ph in (L0A, L3A):
                        eng.wait_ge(*front.at("v_held"))
                    scores(0)
                values(units - 1)
                if front and ph == L2X:
                    own_values()
                    eng.wait_ge(*front.at("ctxt_ready"))
                eng.wait_ge(*at("heads_read", units))
                if ph == L0X:
                    eng.wait_ge(*at("xn_kept"))
                    ins = token_major(OB, "l0x_o", (wk(12), sq("l0x_o0")), (ht, sq("l0x_o1")))
                elif ph == L1X:
                    ins = transposes(OB, [ht[:, t * P:(t + 1) * P] for t in range(TILES)])
                else:
                    name = {L0A: "l0_o", L2X: "l2x_o", L3A: "l3_o"}[ph]
                    ins = token_major(OB, name, (ht, sq(name)))
                ins.then_inc(S["out_psum"].sem, 1)

            def feed_forward(ph, i, front):
                m = MOE[ph]
                e, ncol, tiles = m["e"], m["cols"], m["tiles"]
                z = slots(ph)
                at = None if i is None else values_of(ph, i)
                wg, wu, wd = ffn_weights(ph)
                gate_w = gates[:, 16 * ROUTERS.index(ph):16 * ROUTERS.index(ph) + e]
                cwt = wk(0)[0:ncol, :]
                WB = banks[:, 6, :]
                per = m["f"] // P

                def turn_tokens():
                    eng.wait_ge(*front.at("xn_ready"))
                    transposes(NB, [xn[:, t, :] for t in range(TILES)]).then_inc(S["xnt_psum"].sem, 1)

                def router():
                    eng.wait_ge(*front.at("xnt_held"))
                    for t in range(TILES):
                        if ph == L3F:
                            mm(OB[:, t * e:(t + 1) * e], ones_row, rbias[0:1, 0:e], start=True, stop=False)
                        ins = mm(OB[:, t * e:(t + 1) * e], wk(8)[:, t * P:(t + 1) * P], gate_w,
                                 start=ph != L3F, stop=True)
                    ins.then_inc(S["logits_psum"].sem, 1)

                def ranks():
                    eng.wait_ge(*front.at("picks_ready"))
                    picks = RT[:, 8, :, 0:16]
                    mm(OB[:, 64:128].rearrange("p (t e) -> p t e", t=4), sq("before"), picks,
                       start=True, stop=True)
                    mm(OB[:, 128:192].rearrange("p (t e) -> p t e", t=4), sq("ones"), picks,
                       start=True, stop=True).then_inc(S["ranks_psum"].sem, 1)

                def turn_weights():
                    eng.wait_ge(*front.at("cw_ready"))
                    for t in range(TILES):
                        ins = eng.transpose(NB[0:ncol, t * P:(t + 1) * P], RT[:, 16, t, 0:ncol], ident)
                    ins.then_inc(S["cwt_psum"].sem, 1)

                def down(f):
                    r = min(P, m["nf"] - f * P)
                    eng.wait_ge(*at("h_ready", f + 1))
                    mm(banks[:, 7, :], wd[0:r, f, :], wk(3 + f % 2)[0:r], start=f == 0,
                       stop=f == tiles - 1).then_inc(S["down_done"].sem, 1)

                def tile(f, at):
                    r = min(P, m["nf"] - f * P)
                    if f == 0:
                        eng.wait_ge(*at("xnt_ready"))
                        eng.wait_ge(*at("cwt_ready"))
                    if f >= 2:
                        eng.wait_ge(*at("silu_ready", f - 1))
                    if ph == L0F and f % per == 0:
                        x = f // per
                        if x >= 1:
                            eng.wait_ge(*at("wbc_read", x))
                        mm(WB, sel[0:ncol, x * P:(x + 1) * P], cwt, start=True, stop=True)\
                            .then_inc(S["wbc_psum"].sem, 1)
                    mm(banks[0:r, 2 + f % 2, :], wg[:, f * P:f * P + r], xnt[:, :], start=True, stop=True)\
                        .then_inc(S["gate_psum"].sem, 1)
                    if ph != L0F:
                        if f >= 1:
                            eng.wait_ge(*at("wbc_read", f))
                        mm(WB[0:r], sel[0:ncol, f * P:f * P + r], cwt, start=True, stop=True)\
                            .then_inc(S["wbc_psum"].sem, 1)
                    if f >= 2:
                        eng.wait_ge(*at("h_ready", f - 1))
                    if ph == L0F:
                        if f % per == 0:
                            eng.wait_ge(*at("wbc_read", f // per + 1))
                        up_in = wk(5 + f // per % 2)
                    else:
                        up_in = xnt[:, :]
                    mm(banks[0:r, 4 + f % 2, :], wu[:, f * P:f * P + r], up_in, start=True, stop=True)\
                        .then_inc(S["up_psum"].sem, 1)

                if i is None:
                    eng.wait_ge(sel_loaded, 16 * (1 + [p for p in PHASES if p in MOE].index(ph)))
                    eng.wait_ge(l0_loaded, 32)
                    if ph == L3F and L1A in PHASES:
                        eng.wait_ge(l3_loaded, 16)
                    turn_tokens()
                    router()
                    if m["cap"] is not None:
                        ranks()
                    turn_weights()
                    tile(0, front.at)
                    tile(1, front.at)
                    return
                for f in range(1, tiles):
                    if f >= 2:
                        tile(f, at)
                    down(f - 1)
                    if front:
                        if f == z["turn"]:
                            turn_tokens()
                        if f == z["router"]:
                            router()
                        if f == z["ranks"] and m["cap"] is not None:
                            ranks()
                        if f == z["weights"]:
                            turn_weights()
                if tiles % 2:
                    down(tiles - 1)
                if front:
                    if ph != L0F:
                        eng.wait_ge(*at("wbc_read", tiles))
                    tile(0, front.at)
                if tiles % 2 == 0:
                    down(tiles - 1)
                if front:
                    tile(1, front.at)
                eng.wait_ge(*at("yt_ready"))
                transposes(OB, [wk(7)[:, t * P:(t + 1) * P] for t in range(TILES)])\
                    .then_inc(S["out_psum"].sem, 1)

            def woven(ph, i, front):
                (attend if ph in ATT else feed_forward)(ph, i, front)

            def mamba(at):
                for h in range(2):
                    mm(banks[:, 2 + h, :], sq(f"l1_x{h}"), xnt[:, :], start=True, stop=True)\
                        .then_inc(S["proj_psum"].sem, 1)
                for h in range(2):
                    mm(banks[:, 4 + h, :], sq(f"l1_z{h}"), xnt[:, :], start=True, stop=True)\
                        .then_inc(S["proj_psum"].sem, 1)
                mm(banks[0:8, 6, :], bcw[:, 2 * D_STATE:2 * D_STATE + 8], xnt[:, :], start=True, stop=True)\
                    .then_inc(S["proj_psum"].sem, 1)
                eng.wait_ge(*at("dtr_ready"))
                for h in range(2):
                    mm(banks[:, (7, 1)[h], :], wdt[0:8, h, :], wk(12)[0:8, :], start=True, stop=True)\
                        .then_inc(S["proj_psum"].sem, 1)
                eng.wait_ge(*at("xs_padded"))
                eng.wait_ge(*at("zs_ready"))
                eng.wait_ge(*at("dt_ready"))

                def spread(n):
                    if n >= 2:
                        eng.wait_ge(*at("b_read", n - 1))
                        eng.wait_ge(*at("c_ready", n - 1))
                    mm(banks[:, 2 + n % 2, :], bcw[:, n:n + 1].broadcast_to([P, P]), xnt[:, :],
                       start=True, stop=True).then_inc(S["b_psum"].sem, 1)
                    mm(banks[:, 4 + n % 2, :], bcw[:, D_STATE + n:D_STATE + n + 1].broadcast_to([P, P]),
                       xnt[:, :], start=True, stop=True).then_inc(S["c_psum"].sem, 1)

                spread(0)
                for n in range(D_STATE):
                    if n + 1 < D_STATE:
                        spread(n + 1)
                    for h in range(2):
                        eng.wait_ge(*at("hc_ready", 2 * n + h + 1))
                        ins = mm(banks[:, 6 + h, :], ident, wk(16 + h), start=n == 0, stop=n == D_STATE - 1)
                        ins.then_inc(S["hc_used"].sem, 1)
                eng.wait_ge(*at("ym_ready"))
                for t in range(TILES):
                    for h in range(2):
                        ins = mm(OB[:, t * P:(t + 1) * P], wk(6 + h)[:, t * P:(t + 1) * P], sq(f"l1_o{h}"),
                                 start=h == 0, stop=h == 1)
                ins.then_inc(S["out_psum"].sem, 1)

            def linear_attention(at):
                for k, w in enumerate(("l2_q", "l2_k", "l2_v")):
                    ins = token_major(banks[:, 2 + k, :], w, (xnt, sq(w)))
                    ins.then_inc(S["proj_psum"].sem, 1)
                eng.wait_ge(*at("qk_exp", 1))
                transposes(banks[:, 5, :], [wk(0)[:, t * P:(t + 1) * P] for t in range(TILES)])\
                    .then_inc(S["qkt_psum"].sem, 1)
                eng.wait_ge(*at("qk_exp", 2))
                eng.wait_ge(*at("v_ready"))
                for s in range(SEQS):
                    part = slice(s % 2 * SEQ, s % 2 * SEQ + SEQ)
                    c = slice((s // 2) * P, (s // 2 + 1) * P)
                    tp = (s % 2 * SEQ, 0)
                    mm(banks[:, 2 + s % 2, c], wk(1)[part, c], wk(2)[part, c], start=True, stop=True,
                       tile_position=tp)
                    ins = mm(banks[:, 6 + s % 2, c], wk(1)[part, c], sq("ones")[part, :], start=True,
                             stop=True, tile_position=tp)
                ins.then_inc(S["kv_psum"].sem, 1)
                eng.wait_ge(*at("kv_ready"))
                eng.wait_ge(*at("qkt_ready"))
                for s in range(SEQS):
                    c = slice(s * SEQ, (s + 1) * SEQ)
                    k = slice((s % 2 * 4 + s // 2) * P, (s % 2 * 4 + s // 2 + 1) * P)
                    mm(banks[:, 4, c], wk(4, 2)[:, k], wk(3)[:, c], start=True, stop=True)
                    ins = mm(banks[:, 5, c], wk(6, 2)[:, k], wk(3)[:, c], start=True, stop=True)
                ins.then_inc(S["den_psum"].sem, 1)
                eng.wait_ge(*at("y_ready"))
                token_major(OB, "l2_o", (wk(10), sq("l2_o"))).then_inc(S["out_psum"].sem, 1)

            def project(name, bank, src=None):
                return mm(bank, sq(name), xnt[:, :] if src is None else src, start=True, stop=True)

            def program(ph, i):
                at = values_of(ph, i)
                if ph != L3X:
                    eng.wait_ge(*at("xn_ready"))
                    transposes(NB, [xn[:, t, :] for t in range(TILES)]).then_inc(S["xnt_psum"].sem, 1)
                    eng.wait_ge(*at("xnt_ready"))
                if ph == L1A:
                    mamba(at)
                if ph == L2A:
                    linear_attention(at)
                if ph == L3X:
                    eng.wait_ge(*at("u_scaled"))
                    for t in range(TILES):
                        ins = mm(banks[:, 2, t * P:(t + 1) * P], sq("decay"), wk(0)[:, t * P:(t + 1) * P],
                                 start=True, stop=True)
                    ins.then_inc(S["dep_psum"].sem, 1)
                    eng.wait_ge(*at("xn_ready"))
                    transposes(NB, [wk(3)[:, t * P:(t + 1) * P] for t in range(TILES)])\
                        .then_inc(S["xnt_psum"].sem, 1)
                    eng.wait_ge(*at("xnt_ready"))
                    eng.wait_ge(*at("dep_ready"))
                    eng.wait_ge(*at("row_used"))
                    ins = token_major(OB, "l3_in", (xnt, sq("l3_in")), (wk(4), wk(2)))
                    ins.then_inc(S["out_psum"].sem, 1)
            groups(eng, "tensor", program, woven)

        @block.vector
        def _(eng):
            link = chains["vector"]
            eng.wait_ge(loaded, N_LOADED)
            n = [0]

            def step(ins):
                n[0] += 1
                ins.then_inc(plug_step, 1)
                eng.wait_ge(plug_step, n[0])

            TT, TS, STT = eng.tensor_tensor, eng.tensor_scalar, eng.scalar_tensor_tensor
            step(eng.memset(xpad[:, :, :, :], 0.0))
            step(eng.memset(cnt[:, :, :], 0.0))
            step(eng.memset(RT[:, :, :, :], 1.0))
            step(eng.memset(work[:, 3 * SEQ:4 * SEQ], 1.0))
            lens, plug = work[:, 2 * SEQ:3 * SEQ], work[:, SEQ:2 * SEQ]
            onesw, wrap = work[:, 3 * SEQ:4 * SEQ], work[:, 4 * SEQ:5 * SEQ]
            hits = work[:, 512:512 + SEQ * SEQ].rearrange("p (t i) -> p t i", i=SEQ)
            bound = work[:, 5 * SEQ:6 * SEQ]
            step(eng.tensor_copy(lens, work[:, 0:SEQ].bitcast(I32)))
            step(eng.tensor_tensor_scan(bound, onesw, lens, 0.0, ALU.mult, ALU.add))
            step(TS(bound, bound, 1.0, None, ALU.subtract))
            step(TS(wrap, bound, 0.0, float(SEQ), ALU.is_lt, ALU.mult))
            step(TT(bound, bound, wrap, ALU.add))
            step(eng.tensor_tensor_scan(wrap, onesw, onesw, -1.0, ALU.mult, ALU.add))
            step(TT(hits, over(wrap, SEQ), times(bound, SEQ), ALU.is_equal))
            step(eng.tensor_reduce(lens, hits, AXX, ALU.max))
            step(eng.tensor_tensor_scan(plug, onesw, lens, -1.0, ALU.mult, ALU.add))
            TS(plug, plug, 0.0, None, ALU.max).then_inc(plug_done, 1)
            eng.wait_ge(a_exp, 1)
            TS(l1w[:, :, 4:], l1w[:, :, 4:], -1.0, None, ALU.mult).then_inc(a_ready, 1)
            eng.wait_ge(a_ready, 1)
            step(TT(sq("l0_q"), sq("l0_q"), rope[:, 0, :], ALU.mult))
            step(TT(sq("l0_qb"), sq("l0_qb"), rope[:, 1, :], ALU.mult))
            step(TT(sq("l0_q"), sq("l0_q"), sq("l0_qb"), ALU.add))
            step(TT(col("l0_q"), col("l0_q"), col("cos"), ALU.mult))
            step(STT(col("l0_q"), col("l0_qb"), col("sin"), col("l0_q"), ALU.mult, ALU.add))
            eng.wait_ge(plug_stored, 16)

            def norm(group):
                norm_stats(group)
                return norm_scale(group)

            def norm_stats(group):
                for t in range(TILES):
                    ins = eng.bn_stats(stats[:, t, :], xs[:, bass.ds(group.tile(t), 1), :])
                link(ins)
                eng.memset(att_small[0:1, 0, 15:16], 0.0)
                for t in range(TILES):
                    ins = eng.bn_aggr(mv[:, t, :], stats[:, t, :])
                link(ins)
                TS(vare[:, :], mv[:, :, 1], EPS, None, ALU.add).then_inc(S["var_ready"].sem, 1)

            def norm_scale(group):
                eng.wait_ge(*group.at("rstd_ready", 1))
                for t in range(TILES):
                    ins = TS(xn[:, t, :], xs[:, bass.ds(group.tile(t), 1), :].rearrange("p a f -> p (a f)"),
                             mv[:, t, 0:1], rstd[:, t:t + 1], ALU.subtract, ALU.mult)
                return ins

            def add_out(i, at):
                eng.wait_ge(*at("out_psum"))
                x4 = xs[:, bass.ds(i * TILES, TILES), :]
                TT(x4, x4, t4(OB), ALU.add).then_inc(S["x_updated"].sem, 1)

            def heads_in(ph, at):
                if ph == L0X:
                    eng.wait_ge(*at("row_landed", 16))
                    TS(mask_add, mask_bc, 0.0, NEG, ALU.is_equal, ALU.mult)
                    eng.wait_ge(*at("proj_psum", 1))
                    STT(qt, banks[:, 2, :], col("l0x_q"), mask_bc, ALU.add, ALU.mult)\
                        .then_inc(S["qt_ready"].sem, 1)
                    eng.wait_ge(*at("proj_psum", 2))
                    STT(kt, banks[:, 3, :], col("l0x_k"), mask_bc, ALU.add, ALU.mult)\
                        .then_inc(S["kt_ready"].sem, 1)
                elif ph == L1X:
                    eng.wait_ge(*at("xnt_ready"))
                    eng.tensor_copy(qt, xnt[:, :]).then_inc(S["qt_ready"].sem, 1)
                    eng.wait_ge(*at("ctxt_ready"))
                    eng.tensor_copy(kt, ctxt[:, 0:NT]).then_inc(S["kt_ready"].sem, 1)
                    eng.wait_ge(*at("row_landed", 16))
                    link(eng.tensor_copy(mask_add, mask_bc.bitcast(I32)))
                    link(TS(mask_add, mask_add, -1.0, 1.0, ALU.mult, ALU.add))
                    TS(mask_add, mask_add, NEG, None, ALU.mult).then_inc(S["row_used"].sem, 1)
                    eng.wait_ge(*at("row_used"))
                elif ph == L2X:
                    eng.wait_ge(*at("proj_psum", 1))
                    eng.tensor_copy(qt, banks[:, 2, :]).then_inc(S["qt_ready"].sem, 1)
                    eng.tensor_copy(kt, banks[:, 3, :]).then_inc(S["kt_ready"].sem, 1)
                else:
                    n = "l0" if ph == L0A else "l3"
                    eng.wait_ge(*at("proj_psum", 1))
                    TS(qt, banks[:, 2, :], col(n + "_q"), None, ALU.add).then_inc(S["qt_ready"].sem, 1)
                    eng.wait_ge(*at("proj_psum", 2))
                    TS(kt, banks[:, 3, :], col(n + "_k"), None, ALU.add).then_inc(S["kt_ready"].sem, 1)

            def attend(ph, i, front):
                if i is None:
                    norm(front).then_inc(S["xn_ready"].sem, 1)
                    heads_in(ph, front.at)
                    return
                at = values_of(ph, i)
                a = ATT[ph]
                dh, units = a["dh"], a["units"]
                n = 1024 if dh == 8 else 512
                kl = P if ph == L2X else SEQ
                r = n // kl
                hg = 32 // dh
                bank = banks[:, 2:6, 0:n // 4].rearrange("p g (r k) -> p g r k", k=kl)
                mx, sm, rc = (att_small[:, k, 0:r] for k in range(3))

                def rk(ap):
                    return ap.rearrange("p (r k) -> p r k", k=kl)

                for u in range(units + 2):
                    if u < units:
                        s = sc[u % 2][:, 0:n].rearrange("p (g r k) -> p g r k", g=4, k=kl)
                        eng.wait_ge(*at("scores_psum", u + 1))
                        if u >= 2:
                            eng.wait_ge(*at("probst_psum", u - 1))
                        src = s
                        if ph in (L0A, L3A):
                            m = causal[:, :].unsqueeze(1).unsqueeze(1).broadcast_to([P, 4, r // 4, SEQ])
                            link(TT(s, bank, m, ALU.add))
                        elif ph in (L0X, L1X):
                            s2 = sc[u % 2][:, 0:n].rearrange("p (g k) -> p g k", g=4)
                            b2 = banks[:, 2:6, 0:P]
                            m = times(mask_add[:, u * P:(u + 1) * P], 4)
                            if ph == L0X:
                                link(TT(s2, b2, m, ALU.add))
                            else:
                                link(STT(s2, b2, col("l1x_b"), m, ALU.add, ALU.add))
                        else:
                            src = bank
                        link(eng.tensor_reduce(mx, src, AXX, ALU.max))
                        mx4 = mx.rearrange("p (g r) -> p g r", g=4).unsqueeze(3).broadcast_to([P, 4, r // 4, kl])
                        TT(s, src, mx4, ALU.subtract).then_inc(S["shifted_ready"].sem, 1)
                    if u < units:
                        eng.wait_ge(*at("exp_ready", u + 1))
                        if u >= 1:
                            eng.wait_ge(*at("probs_ready", u))
                        link(eng.tensor_reduce(sm, rk(sc[u % 2][:, 0:n]), AXX, ALU.add))
                        eng.reciprocal(rc, sm).then_inc(S["rsum_ready"].sem, 1)
                    if front and u == units - 4:
                        norm_stats(front)
                    if front and u == units - 3:
                        norm_scale(front).then_inc(S["xn_ready"].sem, 1)
                    if u >= 2:
                        v = u - 2
                        eng.wait_ge(*at("heads_psum", v + 1))
                        nb = 1 if ph == L2X else 2
                        dst = ht[:, v * nb * SEQ:(v + 1) * nb * SEQ].rearrange("p (b s) -> p b s", b=nb)
                        src = banks[:, 0:nb, 0:hg * SEQ].rearrange("p b (h s) -> p b h s", h=hg)
                        m = 0 if dh == 8 else 8
                        for h in range(hg):
                            hm = headmask[:, m + h:m + h + 1]
                            if h == 0:
                                ins = TS(dst, src[:, :, h, :], hm, None, ALU.mult)
                            else:
                                ins = STT(dst, src[:, :, h, :], hm, dst, ALU.mult, ALU.add)
                            if h < hg - 1:
                                link(ins)
                        ins.then_inc(S["heads_read"].sem, 1)
                    if front and u == units - 1:
                        heads_in(ph, front.at)
                add_out(i, at)

            def route(ph, at):
                m = MOE[ph]
                e = m["e"]
                R = lambda k: RT[:, k, :, 0:e]
                sm = lambda k: RT[:, 20, :, k]
                bc = lambda k: over(sm(k), e)
                lg = OB[:, 0:4 * e].rearrange("p (t e) -> p t e", t=4)
                eng.wait_ge(*at("logits_psum"))
                link(eng.tensor_reduce(sm(0), lg, AXX, ALU.max))
                TT(R(0), lg, bc(0), ALU.subtract).then_inc(S["logits_shifted"].sem, 1)
                yield
                eng.wait_ge(*at("logits_exp"))
                link(eng.tensor_reduce(sm(1), R(1), AXX, ALU.add))
                link(eng.reciprocal(sm(2), sm(1)))
                link(TT(R(2), R(1), bc(2), ALU.mult))
                yield

                def best(probs, k, out, signal=None):
                    link(eng.tensor_reduce(sm(k), probs, AXX, ALU.max))
                    link(TT(R(3), probs, bc(k), ALU.is_equal))
                    link(TT(R(3), R(3), times(rank[:, 16 - e:16], 4), ALU.mult))
                    link(eng.tensor_reduce(sm(5), R(3), AXX, ALU.max))
                    ins = TT(out, R(3), bc(5), ALU.is_equal)
                    if signal is None:
                        link(ins)
                    else:
                        ins.then_inc(S[signal].sem, 1)
                        eng.wait_ge(*at(signal))
                oh1, oh2 = (RT[:, 8, :, 0:8], RT[:, 8, :, 8:16]) if ph == L0F else (R(9), R(10))
                best(R(2), 3, oh1)
                yield
                link(STT(R(4), oh1, -2.0, R(2), ALU.mult, ALU.add))
                best(R(4), 4, oh2, "picks_ready" if ph == L0F else None)
                yield
                if ph != L1F:
                    eps = {L0F: 0.0, L2F: 1e-20, L3F: 1e-9}[ph]
                    link(TT(sm(6), sm(3), sm(4), ALU.add))
                    if eps:
                        link(TS(sm(6), sm(6), eps, None, ALU.add))
                    link(eng.reciprocal(sm(7), sm(6)))
                    link(TT(sm(3), sm(3), sm(7), ALU.mult))
                    link(TT(sm(4), sm(4), sm(7), ALU.mult))
                if ph == L3F:
                    TT(RT[:, 8, :, 0:16], oh1, oh2, ALU.add).then_inc(S["picks_ready"].sem, 1)
                    eng.wait_ge(*at("picks_ready"))
                yield
                if m["cap"] is not None:
                    eng.wait_ge(*at("ranks_psum"))
                    tot = OB[:, 128:192].rearrange("p (t e) -> p t e", t=4)
                    for t in range(TILES):
                        link(TT(cnt[:, t + 1, :], cnt[:, t, :], tot[:, t, :], ALU.add))
                    link(TT(RT[:, 11, :, 0:16], OB[:, 64:128].rearrange("p (t e) -> p t e", t=4),
                            cnt[:, 0:4, :], ALU.add))
                    yield
                    link(eng.tensor_copy(cnt[:, 0, :], cnt[:, 4, :]))
                    link(TS(RT[:, 12, :, 0:16], RT[:, 11, :, 0:16], float(m["cap"]), None, ALU.is_lt))
                if ph == L0F:
                    link(TT(RT[:, 8, :, 0:16], RT[:, 8, :, 0:16], RT[:, 12, :, 0:16], ALU.mult))
                link(TT(R(5), oh1, bc(3), ALU.mult))
                link(TT(R(6), oh2, bc(4), ALU.mult))
                if ph == L3F:
                    link(TT(R(5), R(5), R(6), ALU.add))
                    TT(R(16), R(5), R(12), ALU.mult).then_inc(S["cw_ready"].sem, 1)
                else:
                    TT(R(16), R(5), R(6), ALU.add).then_inc(S["cw_ready"].sem, 1)
                yield

            def feed_forward(ph, i, front):
                m = MOE[ph]
                per, tiles = m["f"] // P, m["tiles"]
                z = slots(ph)
                at = None if i is None else values_of(ph, i)

                def scale():
                    norm_scale(front).then_inc(S["xn_ready"].sem, 1)
                    if ph == L3F:
                        eng.wait_ge(*front.at("xn_ready"))
                        x4 = xs[:, bass.ds(front.tile(0), TILES), :]
                        TT(x4, x4, xn[:, :, :], ALU.add)

                def hidden(f, at):
                    r = min(P, m["nf"] - f * P)
                    if ph == L0F and f % per == 0:
                        x = f // per
                        eng.wait_ge(*at("wbc_psum", x + 1))
                        if x >= 2:
                            eng.wait_ge(*at("up_psum", (x - 1) * per))
                        TT(wk(5 + x % 2), xnt[:, :], banks[:, 6, :], ALU.mult).then_inc(S["wbc_read"].sem, 1)
                    sg = wk(1 + f % 2)[0:r]
                    eng.wait_ge(*at("silu_ready", f + 1))
                    if ph != L0F:
                        eng.wait_ge(*at("wbc_psum", f + 1))
                        TT(sg, sg, banks[0:r, 6, :], ALU.mult).then_inc(S["wbc_read"].sem, 1)
                        eng.wait_ge(*at("wbc_read", f + 1))
                    eng.wait_ge(*at("up_psum", f + 1))
                    if f >= 2:
                        eng.wait_ge(*at("down_done", f - 1))
                    TT(wk(3 + f % 2)[0:r], sg, banks[0:r, 4 + f % 2, :], ALU.mult)\
                        .then_inc(S["h_ready"].sem, 1)

                if i is None:
                    norm_stats(front)
                    scale()
                    for _ in route(ph, front.at):
                        pass
                    hidden(0, front.at)
                    return
                if front:
                    routing = route(ph, front.at)
                for f in range(tiles):
                    if f >= 1:
                        hidden(f, at)
                    if front:
                        if f == z["stats"]:
                            norm_stats(front)
                        if f == z["scale"]:
                            scale()
                        for _ in range(z["route"].count(f)):
                            next(routing, None)
                if front:
                    assert next(routing, "done") == "done"
                    hidden(0, front.at)
                add_out(i, at)

            def woven(ph, i, front):
                (attend if ph in ATT else feed_forward)(ph, i, front)

            def mamba(at):
                eng.wait_ge(*at("xs_padded"))
                for k in range(4):
                    for h in range(2):
                        o = wk(h).rearrange("p (b s) -> p b s", s=SEQ)
                        src = xpad[:, h, :, k:k + SEQ]
                        if k == 0:
                            ins = TS(o, src, l1w[:, h, 0:1], None, ALU.mult)
                        else:
                            ins = STT(o, src, l1w[:, h, k:k + 1], o, ALU.mult, ALU.add)
                    if k < 3:
                        link(ins)
                ins.then_inc(S["conv_ready"].sem, 1)
                eng.wait_ge(*at("soft_exp"))
                e1, w1, z1 = wk(8, 2), wk(14, 2), wk(16, 2)
                link(TS(w1, e1, 1.0, None, ALU.add))
                link(TS(w1, w1, 1.0, None, ALU.subtract))
                link(TS(z1, w1, 0.0, None, ALU.is_equal))
                link(TT(w1, w1, z1, ALU.add))
                link(eng.reciprocal(w1, w1))
                eng.wait_ge(*at("soft_ready"))
                link(TT(e1, e1, w1, ALU.mult))
                link(TT(z1, z1, wk(12, 2), ALU.add))
                link(TT(e1, e1, z1, ALU.mult))
                for h in range(2):
                    ins = TS(wk(2 + h), banks[:, (7, 1)[h], :], col(f"l1_dt{h}"), 0.0, ALU.add, ALU.max)
                link(ins)
                link(TT(wk(2, 2), wk(2, 2), wk(8, 2), ALU.add))
                link(eng.tensor_copy(wk(8, 2), wk(2, 2)))
                eng.wait_ge(*at("u_ready"))
                eng.memset(wk(8, 2).rearrange("p (b s) -> p b s", s=SEQ)[:, :, 0:1], 1e25)\
                    .then_inc(S["dt_ready"].sem, 1)
                eng.wait_ge(*at("du_ready"))
                for s in range(2 * D_STATE):
                    st, h = divmod(s, 2)
                    eng.wait_ge(*at("b_psum", st + 1))
                    db = wk(12 + h)
                    ins = TT(db, wk(6 + h), banks[:, 2 + st % 2, :], ALU.mult)
                    if h == 1:
                        ins.then_inc(S["b_read"].sem, 1)
                        eng.wait_ge(*at("b_read", st + 1))
                    else:
                        link(ins)
                    eng.wait_ge(*at("da_ready", s + 1))
                    if s >= 2:
                        eng.wait_ge(*at("hc_ready", s - 1))
                    eng.tensor_tensor_scan(wk(14 + h), wk(h), db, 0.0, ALU.mult, ALU.add)\
                        .then_inc(S["scan_ready"].sem, 1)
                eng.wait_ge(*at("hc_used", 2 * D_STATE))
                eng.wait_ge(*at("zs_ready"))
                for h in range(2):
                    ins = STT(wk(12 + h), wk(4 + h), col(f"l1_d{h}"), banks[:, 6 + h, :], ALU.mult, ALU.add)
                link(ins)
                TT(wk(6, 2), wk(12, 2), wk(10, 2), ALU.mult).then_inc(S["ym_ready"].sem, 1)
                eng.wait_ge(*at("out_psum"))
                res = t4(wk(12))
                link(TT(res, xn[:, :, :], t4(OB), ALU.add))
                for t in range(TILES):
                    ins = eng.bn_stats(stats[:, t, :], res[:, t, :])
                link(ins)
                eng.memset(att_small[0:1, 0, 15:16], 0.0)
                for t in range(TILES):
                    ins = eng.bn_aggr(mv[:, t, :], stats[:, t, :])
                link(ins)
                TS(vare[:, :], mv[:, :, 1], EPS, None, ALU.add).then_inc(S["var_ready"].sem, 1)
                eng.wait_ge(*at("rstd_ready", 2))
                for t in range(TILES):
                    ins = TS(res[:, t, :], res[:, t, :], mv[:, t, 0:1], rstd[:, t:t + 1],
                             ALU.subtract, ALU.mult)
                link(ins)
                link(TT(res, res, times(fbc[:, 0, :], TILES), ALU.mult))
                link(TT(res, res, times(fbc[:, 1, :], TILES), ALU.add))
                return res

            def program(ph, i):
                at = values_of(ph, i)
                group = Front(ph, i, 0)
                if ph == L3X:
                    link(norm(group))
                else:
                    norm(group).then_inc(S["xn_ready"].sem, 1)
                if ph == L1A:
                    res = mamba(at)
                    x4 = xs[:, bass.ds(i * TILES, TILES), :]
                    TT(x4, x4, res, ALU.add).then_inc(S["x_updated"].sem, 1)
                    return
                if ph == L2A:
                    for k in range(2):
                        eng.wait_ge(*at("proj_psum", k + 1))
                        b = banks[:, 2 + k, :].rearrange("p (r d) -> p r d", d=8)
                        link(eng.tensor_reduce(wk(9)[:, 0:SEQ], b, AXX, ALU.max))
                        TT(wk(k).rearrange("p (r d) -> p r d", d=8), b, over(wk(9)[:, 0:SEQ], 8),
                           ALU.subtract).then_inc(S["qk_shifted"].sem, 1)
                        eng.wait_ge(*at("qk_shifted", k + 1))
                    eng.wait_ge(*at("kv_psum"))
                    kv = banks[:, 2:4, :].rearrange("p a (s f) -> p (a s) f", f=P)
                    ks = banks[:, 6:8, :].rearrange("p a (s f) -> p (a s) f", f=P)
                    m = times(sq("block8"), SEQS)
                    TT(wk(4, 2).rearrange("p (s f) -> p s f", f=P), kv, m, ALU.mult)
                    TT(wk(6, 2).rearrange("p (s f) -> p s f", f=P), ks, m, ALU.mult)\
                        .then_inc(S["kv_ready"].sem, 1)
                    eng.wait_ge(*at("den_psum"))
                    link(TS(wk(8), banks[:, 5, :], 1e-6, None, ALU.add))
                    link(eng.reciprocal(wk(9), wk(8)))
                    TT(wk(10), wk(9), banks[:, 4, :], ALU.mult).then_inc(S["y_ready"].sem, 1)
                if ph == L3X:
                    link(TT(t4(wk(5)), xn[:, :, :], xn[:, :, :], ALU.mult))
                    link(eng.tensor_reduce(vare[:, :], t4(wk(5)), AXX, ALU.add))
                    TS(vare[:, :], vare[:, :], 1.0 / P, EPS, ALU.mult, ALU.add)\
                        .then_inc(S["var_ready"].sem, 1)
                    eng.wait_ge(*at("rstd_ready", 2))
                    for t in range(TILES):
                        ins = TS(wk(3)[:, t * P:(t + 1) * P], xn[:, t, :], rstd[:, t:t + 1], None, ALU.mult)
                    ins.then_inc(S["xn_ready"].sem, 1)
                    eng.wait_ge(*at("ctx_landed", 16))
                    link(TT(wk(5, 2).rearrange("p (t f) -> p t f", t=TILES), ctxn, ctxn, ALU.mult))
                    link(eng.tensor_reduce(vare[:, :], wk(5, 2).rearrange("p (t f) -> p t f", t=TILES),
                                           AXX, ALU.add))
                    TS(vare[:, :], vare[:, :], 1.0 / CTX, EPS, ALU.mult, ALU.add)\
                        .then_inc(S["var_ready"].sem, 1)
                    eng.wait_ge(*at("rstd_ready", 3))
                    for t in range(TILES):
                        ins = TS(wk(7)[:, t * P:(t + 1) * P], ctxn[:, t, 0:P], rstd[:, t:t + 1], None, ALU.mult)
                    ins.then_inc(S["ctx_used"].sem, 1)
                    eng.wait_ge(*at("ctx_used"))
                    TT(t4(wk(0)), t4(wk(7)), times(fbc[:, 2, :], TILES), ALU.mult)\
                        .then_inc(S["u_scaled"].sem, 1)
                    eng.wait_ge(*at("row_landed", 16))
                    STT(t4(wk(4)), t4(mask_bc), col("iota64"), times(sq("block64"), TILES),
                        ALU.is_equal, ALU.mult).then_inc(S["row_used"].sem, 1)
                add_out(i, at)

            def before(ph):
                if ph == L3F:
                    link(eng.memset(cnt[:, :, :], 0.0))
            groups(eng, "vector", program, woven, before)
    return seen


def host_arrays(a):
    f = lambda n: np.asarray(a[n], np.float32)
    z = {}
    perm_a, perm_b = [0, 2, 1, 3, 4, 6, 5, 7], [1, 3, 0, 2, 5, 7, 4, 6]
    heads = lambda w, p: w.reshape(P, 16, 8)[:, :, p].reshape(P, P)
    heads1 = lambda b, p: b.reshape(16, 8)[:, p].reshape(P)
    rep16 = lambda w: np.tile(w, (1, 16))
    wsrc, wtgt, wout = f("L0_xattn_W_src"), f("L0_xattn_W_tgt"), f("L0_xattn_W_out")
    win, w_out1 = f("L1_attn_W_in"), f("L1_attn_W_out")
    qkv = f("L2_xattn_w_qkv")
    h3 = lambda n: f(n).transpose(1, 0, 2).reshape(P, P)
    tok = np.arange(P)
    step_ = np.exp(-0.001)
    dt = -np.log(-np.expm1(-0.001))
    lag = tok[None, :] % SEQ - tok[:, None] % SEQ
    same = tok[None, :] // SEQ == tok[:, None] // SEQ
    decay = np.where(same & (lag >= 0), step_ * np.exp(-dt * np.maximum(lag, 0)), 0.0)
    q = {
        "l0_q": heads(f("L0_attn_Wq"), perm_a), "l0_qb": heads(f("L0_attn_Wq"), perm_b),
        "l0_k": rep16(f("L0_attn_Wk")[:, perm_a]),
        "l0_v": rep16(f("L0_attn_Wv")), "l0_o": f("L0_attn_Wo"),
        "l0x_k0": wsrc[:P, :P].T, "l0x_k1": wsrc[:P, P:].T, "l0x_v0": wsrc[P:, :P].T, "l0x_v1": wsrc[P:, P:].T,
        "l0x_q": wtgt.T, "l0x_o0": wout[:, :P].T, "l0x_o1": wout[:, P:].T,
        "l1_x0": win[0:P].T, "l1_x1": win[P:2 * P].T, "l1_z0": win[2 * P:3 * P].T, "l1_z1": win[3 * P:4 * P].T,
        "l1_o0": w_out1[:, :P].T, "l1_o1": w_out1[:, P:].T,
        "l2_q": f("L2_attn_Wq").T, "l2_k": f("L2_attn_Wk").T, "l2_v": f("L2_attn_Wv").T, "l2_o": f("L2_attn_Wo").T,
        "l2x_q": qkv[:P].T, "l2x_k": qkv[P:2 * P].T, "l2x_v": qkv[2 * P:].T, "l2x_o": f("L2_xattn_w_proj").T,
        "l3_q": h3("L3_attn_Wq"), "l3_k": h3("L3_attn_Wk"), "l3_v": h3("L3_attn_Wv"), "l3_o": f("L3_attn_Wo"),
        "l3_in": f("L3_xattn_W_in").T,
        "ident": np.eye(P), "ones": np.ones((P, P)), "before": tok[:, None] < tok[None, :],
        "block8": tok[:, None] // 8 == tok[None, :] // 8, "decay": decay, "block64": same,
    }
    theta = (1.0 / 10000.0 ** (np.arange(0, 4, 2, dtype=np.float32) / 4)).astype(np.float32)
    ang = (tok // 8).astype(np.float32) * theta[np.array([0, 1, 0, 1])[tok % 4]]
    cos, sin = np.cos(ang), np.sin(ang) * np.where(tok % 4 < 2, -1, 1)
    z["squares"] = np.stack([q[n] for n in SQUARES], 1).astype(np.float32)
    bsrc = f("L0_xattn_b_src")
    rep_b = lambda b: np.tile(b, 16)
    cb, bdt, dd = f("L1_attn_conv_b"), f("L1_attn_b_dt"), f("L1_attn_D")
    c = {
        "cos": cos, "sin": sin, "l0_q": heads1(f("L0_attn_bq"), perm_a), "l0_qb": heads1(f("L0_attn_bq"), perm_b),
        "l0_k": rep_b(f("L0_attn_bk")[perm_a]),
        "l0x_k": bsrc[:P], "l0x_q": f("L0_xattn_b_tgt"), "l3_q": f("L3_attn_bq").reshape(P),
        "l3_k": f("L3_attn_bk").reshape(P), "l1_cb0": cb[:P], "l1_cb1": cb[P:], "l1_dt0": bdt[:P],
        "l1_dt1": bdt[P:], "l1_d0": dd[:P], "l1_d1": dd[P:], "l1x_b": np.repeat(f("L1_xattn_b"), P),
        "l3_res": f("L3_xattn_g_res"), "iota64": tok % SEQ, "one": np.ones(P), "zero": np.zeros(P),
    }
    z["cols"] = np.stack([c[n] for n in COLS], 1).astype(np.float32)
    r = {
        "l0_v": rep_b(f("L0_attn_bv")), "l0_o": f("L0_attn_bo"), "l0x_v": bsrc[P:], "l0x_o": f("L0_xattn_b_out"),
        "l2_q": f("L2_attn_bq"), "l2_k": f("L2_attn_bk"), "l2_v": f("L2_attn_bv"), "l2_o": f("L2_attn_bo"),
        "l2x_o": f("L2_xattn_b_proj"), "l3_v": f("L3_attn_bv").reshape(P), "l3_o": f("L3_attn_bo"),
        "l3_in": f("L3_xattn_b_in"), "ones": np.ones(P),
    }
    z["rows"] = np.stack([r[n] for n in ROWS])[None].astype(np.float32)
    g = np.zeros((P, 64), np.float32)
    for k, w in enumerate((f("L0_ffn_gate_w").T, f("L1_ffn_gate_w").T, f("L2_ffn_gate_w").T, f("L3_ffn_router_w"))):
        g[:, 16 * k:16 * k + w.shape[1]] = w
    z["gates"] = g
    z["rbias"] = np.tile(f("L3_ffn_router_b"), 4)[None]
    z["rank"] = np.tile(np.arange(16, 0, -1, dtype=np.float32), (P, 1))
    m8 = (tok[:, None] % 32 // 8 == np.arange(4)[None]).astype(np.float64)
    m16 = (tok[:, None] % 32 // 16 == np.arange(2)[None]).astype(np.float64)
    z["headmask"] = np.concatenate([m8, m8 / np.sqrt(8.0), m16, m16 / 4], 1).astype(np.float32)
    z["causal"] = np.where(np.arange(SEQ)[None] <= tok[:, None] % SEQ, 0.0, NEG).astype(np.float32)
    z["rope"] = np.tile(np.stack([cos, sin])[None], (P, 1, 1)).astype(np.float32)
    taps, alog = f("L1_attn_conv_w")[:, 0], f("L1_attn_A_log")
    z["l1w"] = np.concatenate([taps, alog], 1).reshape(2, P, 4 + D_STATE).transpose(1, 0, 2)
    z["bcw"] = win[4 * P:].T
    z["wdt"] = f("L1_attn_W_dt").T.reshape(8, 2, P)
    z["ln_g"], z["ln_b"], z["g_init"] = f("L1_attn_ln_g"), f("L1_attn_ln_b"), f("L3_xattn_g_init")[:P]
    z["maskcol"] = f("mask_BxS2_fk1").reshape(-1, P).T
    z["mask_f"] = f("mask_BxS2_fk1")
    z["mask_i"], z["patch_lens"] = np.asarray(a["mask_BxS2_ik0"]), np.asarray(a["mask_BxS2_if0"])

    def ffn(gate, up, down):
        nf = gate.shape[1]
        t = -(-nf // P)
        o = np.zeros((P, 3, t * P), np.float32)
        o[:, 0, :nf], o[:, 1, :nf] = gate, up
        dp = np.zeros((t * P, P), np.float32)
        dp[:nf] = down
        o[:, 2] = dp.reshape(t, P, P).transpose(1, 0, 2).reshape(P, t * P)
        return o
    efd = lambda n: f(n).transpose(2, 0, 1).reshape(P, -1)
    edf = lambda n: f(n).transpose(0, 2, 1).reshape(-1, P)
    hei = lambda n: f(n).transpose(1, 0, 2).reshape(P, -1)
    z["ffn_l0"] = ffn(efd("L0_ffn_wi_gate"), efd("L0_ffn_wi_up"), edf("L0_ffn_wo"))
    l1 = ffn(np.concatenate([efd("L1_ffn_wg"), f("L1_ffn_sg").T], 1),
             np.concatenate([efd("L1_ffn_wu"), f("L1_ffn_su").T], 1),
             np.concatenate([edf("L1_ffn_wd"), f("L1_ffn_sd").T], 0))
    l2 = ffn(np.concatenate([hei("L2_ffn_wg"), f("L2_ffn_swg")], 1),
             np.concatenate([hei("L2_ffn_wu"), f("L2_ffn_swu")], 1),
             np.concatenate([f("L2_ffn_wd").reshape(-1, P), f("L2_ffn_swd")], 0))
    z["ffn_mid"] = np.concatenate([l1, l2], 2)
    z["ffn_l3"] = ffn(np.concatenate([hei("L3_ffn_w_gate"), f("L3_ffn_sw_gate")], 1),
                      np.concatenate([hei("L3_ffn_w_up"), f("L3_ffn_sw_up")], 1),
                      np.concatenate([f("L3_ffn_w_down").reshape(-1, P), f("L3_ffn_sw_down")], 0))
    for ph, m in MOE.items():
        n = m["e"] * P if ph == L0F else m["nf"]
        per = P if ph == L0F else m["f"]
        z[f"sel{ph}"] = (np.minimum(np.arange(n) // per, m["cols"] - 1)[None] ==
                         np.arange(m["cols"])[:, None]).astype(np.float32)
    z["x"] = f("x").reshape(TOKENS, P)
    z["ctx"] = f("ctx_2048").reshape(TOKENS, CTX)
    return {k: np.ascontiguousarray(v) for k, v in z.items()}


def build(Bacc, arrays, counts):
    nc = Bacc("TRN2", target_bir_lowering=False, num_devices=1)
    d = {n: nc.dram_tensor(f"in_{n}", v.shape, mybir.dt.from_np(v.dtype), kind="ExternalInput").ap()
         for n, v in arrays.items()}
    d["plug"] = nc.dram_tensor("plug", (BATCH, SEQ), F32, kind="Internal").ap()
    out = nc.dram_tensor("out_x", (TOKENS, P), F32, kind="ExternalOutput").ap()
    return nc, decoder(nc, d, out, counts)


COUNTS = {
    "gpsimd": {L0A: (0, 0, 0), L0X: (0, 0, 0), L0F: (0, 0, 0), L1X: (0, 0, 0), L1F: (0, 0, 0), L2X: (0, 0, 0), L2F: (0, 0, 0), L3A: (0, 0, 0), L3F: (0, 0, 0)},
    "scalar": {L0A: (0, 0, 0), L0X: (0, 0, 0), L0F: (0, 0, 0), L1A: 2, L1X: (0, 0, 0), L1F: (0, 0, 0), L2X: (0, 0, 0), L2F: (0, 0, 0), L3A: (0, 0, 0), L3F: (0, 0, 0)},
    "tensor": {L0A: (0, 0, 0), L0X: (0, 0, 0), L0F: (0, 0, 0), L1X: (0, 0, 0), L1F: (0, 0, 0), L2X: (0, 0, 0), L2F: (0, 0, 0), L3A: (0, 0, 0), L3F: (0, 0, 0)},
    "vector": {L0A: (2, 26, 24), L0X: (2, 18, 16), L0F: (30, 30, 0), L1A: 39, L1X: (4, 20, 16), L1F: (19, 19, 0), L2A: 6, L2X: (2, 42, 40), L2F: (24, 24, 0), L3A: (2, 26, 24), L3X: 7, L3F: (33, 32, 0)},
}


def kernel(**inputs):
    import concourse.bacc as _bacc
    from concourse.bass_utils import run_bass_kernel_spmd as _run

    arrays = host_arrays(inputs)
    nc = build(_bacc.Bacc, arrays, COUNTS)[0]
    r = _run(nc, [{f"in_{n}": v for n, v in arrays.items()}], core_ids=[0])
    return r.results[0]["out_x"].reshape(BATCH, SEQ, P)
```

```python
from contextlib import ExitStack

import numpy as np

import concourse.bass as bass
from concourse import mybir

F32 = mybir.dt.float32
BF16 = mybir.dt.bfloat16
U16 = mybir.dt.uint16
I32 = mybir.dt.int32
ALU = mybir.AluOpType
ACT = mybir.ActivationFunctionType
AXX = mybir.AxisListType.X

P = 128
BATCH, SEQ, CTX = 128, 64, 256
TOKENS = BATCH * SEQ
TILES = 4
NT = TILES * P
GROUPS = TOKENS // NT
SEQS = NT // SEQ
EPS = 1e-5
NEG = -1e30

L0A, L0X, L0F, L1A, L1X, L1F, L2A, L2X, L2F, L3A, L3X, L3F = range(12)
PHASES = range(12)

MOE = {
    L0F: dict(e=8, f=512, shared=0, cap=int(TOKENS / 8 * 1.25)),
    L1F: dict(e=8, f=64, shared=64, cap=None),
    L2F: dict(e=8, f=176, shared=352, cap=None),
    L3F: dict(e=16, f=176, shared=176, cap=int(np.ceil(1.25 * TOKENS * 2 / 16))),
}
for _m in MOE.values():
    _m["nf"] = _m["e"] * _m["f"] + _m["shared"]
    _m["tiles"] = -(-_m["nf"] // P)
    _m["cols"] = _m["e"] + (1 if _m["shared"] else 0)

ATT = {
    L0A: dict(dh=8, units=4), L0X: dict(dh=16, units=4), L1X: dict(dh=16, units=4),
    L2X: dict(dh=8, units=8), L3A: dict(dh=8, units=4),
}
D_STATE = 16
WOVEN = {*ATT, *MOE, L1A, L2A}


def slots(ph):
    first = 0 if ph == L1F else 1
    route = [2, 2, 2, 3, 3, 3, 3, 3, 3] if ph == L1F else list(range(3, 12))
    return dict(stats=0, scale=first, turn=first + 1, router=first + 2, route=route, ranks=8,
                weights=4 if ph == L1F else 12)

SQUARES = [
    "l0_q", "l0_qb", "l0_k", "l0_v", "l0_o",
    "l0x_k0", "l0x_k1", "l0x_v0", "l0x_v1", "l0x_q", "l0x_o0", "l0x_o1",
    "l1_x0", "l1_x1", "l1_z0", "l1_z1", "l1_o0", "l1_o1",
    "l2_q", "l2_k", "l2_v", "l2_o", "l2x_q", "l2x_k", "l2x_v", "l2x_o",
    "l3_q", "l3_k", "l3_v", "l3_o", "l3_in",
    "ident", "ones", "before", "block8", "decay", "block64",
]
COLS = [
    "l0_q", "l0_qb", "l0_k", "cos", "sin", "l0x_k", "l0x_q", "l3_q", "l3_k",
    "l1_cb0", "l1_cb1", "l1_dt0", "l1_dt1", "l1_d0", "l1_d1", "l1x_b", "l3_res",
    "iota64", "one", "zero",
]
ROWS = ["l0_v", "l0_o", "l0x_v", "l0x_o", "l2_q", "l2_k", "l2_v", "l2_o", "l2x_o",
        "l3_v", "l3_o", "l3_in", "ones"]
ROUTERS = [L0F, L1F, L2F, L3F]


def per_group():
    units = {ph: a["units"] for ph, a in ATT.items()}
    tiles = {ph: m["tiles"] for ph, m in MOE.items()}
    every = {ph: 1 for ph in range(12)}
    steps = {L1A: 2 * D_STATE}
    states = {L1A: D_STATE}
    return {
        "x_updated": every, "var_ready": {**every, L3X: 3}, "rstd_ready": {**every, L3X: 3},
        "xn_ready": every, "xnt_psum": every, "xnt_ready": every,
        "ctx_landed": {L0X: 16, L1X: 16, L2X: 16, L3X: 16}, "ctx_values_landed": {L2X: 16}, "ctx_psum": {L0X: 2, L1X: 1, L2X: 1},
        "ctxt_ready": {L0X: 2, L1X: 1, L2X: 1}, "ctx_used": {L3X: 1},
        "row_landed": {L0X: 16, L1X: 16, L3X: 16}, "row_used": {L1X: 1, L3X: 1},
        "proj_psum": {L0A: 3, L0X: 3, L1A: 8, L2A: 3, L2X: 2, L3A: 3},
        "qt_ready": {ph: 1 for ph in ATT}, "kt_ready": {ph: 1 for ph in ATT},
        "v_ready": {L0A: 1, L0X: 1, L1X: 1, L2A: 1, L2X: 1, L3A: 1},
        "qbd_ready": {ph: 1 for ph in ATT},
        "scores_psum": {ph: 2 * n for ph, n in units.items()}, "scores_read": {ph: 2 * n for ph, n in units.items()},
        "shifted_ready": {ph: n for ph, n in units.items() if ph != L2X}, "exp_ready": units,
        "rsum_ready": units, "probs_ready": units, "probst_psum": units, "probst_ready": units,
        "xn_kept": {L0X: 1}, "xnt_held": {ph: 1 for ph in MOE}, "cwt_held": {ph: 1 for ph in MOE}, "v_held": {L0A: 1, L3A: 1}, "heads_psum": units, "heads_read": units, "out_psum": {**every},
        "logits_psum": {ph: 1 for ph in MOE}, "logits_shifted": {ph: 1 for ph in MOE},
        "logits_exp": {ph: 1 for ph in MOE}, "picks_ready": {L0F: 1, L3F: 1}, "ranks_psum": {L0F: 1, L3F: 1},
        "cw_ready": {ph: 1 for ph in MOE}, "cwt_psum": {ph: 1 for ph in MOE}, "cwt_ready": {ph: 1 for ph in MOE},
        "gate_psum": tiles, "up_psum": tiles, "silu_ready": tiles, "h_ready": tiles, "down_done": tiles,
        "wbc_psum": {**tiles, L0F: 8}, "wbc_read": {**tiles, L0F: 8},
        "yt_ready": {**{ph: 1 for ph in MOE}},
        **{name: {L1A: 1} for name in (
            "res_var_ready", "res_rstd_ready", "bc_high", "bc_rest", "bc_middle", "bc_held", "bc_ready", "held_moved",
            "dt_raw")},
        "conv_ready": {L1A: 1}, "xs_padded": {L1A: 2}, "u_ready": {L1A: 1}, "zs_ready": {L1A: 1},
        "dtr_ready": {L1A: 1}, "soft_exp": {L1A: 1}, "soft_ready": {L1A: 1}, "dt_ready": {L1A: 1},
        "b_psum": states, "c_psum": states, "c_ready": states, "b_read": states,
        "da_ready": steps, "scan_ready": steps, "hc_ready": steps, "hc_used": steps,
        "ym_psum": {L1A: 1}, "ym_ready": {L1A: 1},
        "qk_shifted": {L2A: 2}, "qk_exp": {L2A: 2}, "qkt_psum": {L2A: 1}, "qkt_ready": {L2A: 1},
        "kv_psum": {L2A: 1}, "kv_ready": {L2A: 1}, "den_psum": {L2A: 1}, "y_ready": {L2A: 1},
        "dep_psum": {L3X: 1}, "dep_ready": {L3X: 1}, "u_scaled": {L3X: 1},
    }


class Signal:

    def __init__(self, sem, per):
        self.sem, self.per, self.base = sem, per, {}
        total = 0
        for ph in PHASES:
            self.base[ph] = total
            total += GROUPS * per.get(ph, 0)

    def at(self, ph, i, k):
        return self.base[ph] + i * self.per[ph] + k


class Chain:

    def __init__(self, sem, per):
        self.sem, self.base, self.per = sem, {}, per
        total = 0
        for ph in PHASES:
            self.base[ph] = total
            if ph in WOVEN:
                start, body, last = per.get(ph, (0, 0, 0))
                total += start + (GROUPS - 1) * body + last
            else:
                total += GROUPS * per.get(ph, 0)

    def enter(self, eng, ph, i, start=False):
        self.eng, self.n = eng, 0
        if ph in WOVEN:
            before, body, _ = self.per.get(ph, (0, 0, 0))
            self.from_ = self.base[ph] if start else self.base[ph] + before + i * body
        else:
            self.from_ = self.base[ph] + i * self.per.get(ph, 0)

    def __call__(self, ins):
        self.n += 1
        ins.then_inc(self.sem, 1)
        self.eng.wait_ge(self.sem, self.from_ + self.n)


def decoder(nc, d, out_dram, counts):
    ctx = ExitStack()
    with ctx:
        def sb(name, shape, dt=F32):
            return ctx.enter_context(nc.sbuf_tensor(name, shape, dt))

        xs = sb("xs", [P, TOKENS // P, P])
        square = {n: k for k, n in enumerate(SQUARES)}
        squares = sb("squares", [P, len(SQUARES), P])
        cols = sb("cols", [P, len(COLS)])
        rows = sb("rows", [1, len(ROWS), P])
        gates = sb("gates", [P, 4 * 16])
        rbias = sb("rbias", [1, 64])
        rank = sb("rank", [P, 16])
        headmask = sb("headmask", [P, 12])
        causal = sb("causal", [P, SEQ])
        rope = sb("rope", [P, 2, P])
        l1w = sb("l1w", [P, 2, 4 + D_STATE])
        bcw = sb("bcw", [P, 6 * D_STATE + 8])
        pick = sb("pick", [6 * D_STATE, 2 * D_STATE], BF16)
        wdt = sb("wdt", [8, 2, P])
        fbc = sb("fbc", [P, 3, P])
        maskcol = sb("maskcol", [P, TOKENS // P])

        big = sb("big", [P, 3, 8 * 512])
        small = sb("small", [P, 3, (MOE[L1F]["tiles"] + MOE[L2F]["tiles"]) * P])
        sel = sb("sel", [P, 24 * P])

        sel16 = sel[:, :].bitcast(BF16)
        ident16 = sb("ident16", [P, P], BF16)
        parts = sb("parts", [P, TILES, 96], BF16)

        stats = sb("stats", [P, TILES, 6])
        mv = sb("mv", [P, TILES, 2])
        vare = sb("vare", [P, 4])
        rstd = sb("rstd", [P, 4])
        power = sb("power", [P, 4])
        xn = sb("xn", [P, TILES, P])
        xnt = sb("xnt", [P, NT])
        xpad = sb("xpad", [P, 2, SEQS, SEQ + 3])
        work = sb("work", [P, 20 * 512])

        def wk(k, n=1):
            return work[:, k * 512:(k + n) * 512]

        banks = ctx.enter_context(nc.psum_tensor("banks", [P, 8, 512], F32))

        names = per_group()
        S = {n: Signal(ctx.enter_context(nc.semaphore(n)), per) for n, per in names.items()}
        chains = {e: Chain(ctx.enter_context(nc.semaphore(e + "_step")), counts.get(e, {}))
                  for e in ("vector", "scalar", "gpsimd", "tensor")}
        loaded = ctx.enter_context(nc.semaphore("loaded"))
        l0_loaded = ctx.enter_context(nc.semaphore("l0_loaded"))
        l3_loaded = ctx.enter_context(nc.semaphore("l3_loaded"))
        sel_loaded = ctx.enter_context(nc.semaphore("sel_loaded"))
        plug_step = ctx.enter_context(nc.semaphore("plug_step"))
        a_exp = ctx.enter_context(nc.semaphore("a_exp"))
        a_ready = ctx.enter_context(nc.semaphore("a_ready"))
        setup_done = ctx.enter_context(nc.semaphore("setup_done"))
        plug_done = ctx.enter_context(nc.semaphore("plug_done"))
        plug_stored = ctx.enter_context(nc.semaphore("plug_stored"))
        out_stored = ctx.enter_context(nc.semaphore("out_stored"))
        seen = {}

        def sq(n):
            return squares[:, square[n], :]

        def col(n):
            k = COLS.index(n)
            return cols[:, k:k + 1]

        def row(n):
            return rows[0:1, ROWS.index(n), :]

        ones_row = rows[0:1, ROWS.index("ones"), 0:P]
        ident = sq("ident")

        def over(ap, n):
            return ap.unsqueeze(2).broadcast_to([ap.shape[0], ap.shape[1], n])

        def times(ap, n):
            return ap.unsqueeze(1).broadcast_to([ap.shape[0], n, ap.shape[1]])

        def t4(ap):
            return ap.rearrange("p (t f) -> p t f", t=TILES)

        qt, kt, vt = wk(0), wk(1), wk(2)
        qbd = wk(3, 4)
        sc = [wk(7, 2), wk(9, 2)]
        pt = wk(11, 2)
        ht = wk(13)
        ctxn = wk(14, 2).rearrange("p (t f) -> p t f", t=TILES)
        ctxt = wk(16, 2)
        mask_bc = wk(18)
        mask_add = wk(19)
        tmp1, tmp2 = wk(7), wk(8)
        att_small = sb("att_small", [P, 3, 16])
        RT = sb("rt", [P, 24, 4, 17])
        cnt = sb("cnt", [P, 5, 16])
        NB, OB = banks[:, 0, :], banks[:, 1, :]
        NBC = 6 * D_STATE
        pair = [big[:, k, 6 * 512:8 * 512] for k in range(3)] + [sel[:, k * 1024:(k + 1) * 1024] for k in range(3)]
        u_held, zs_held, soft_e, soft_d, soft_l, soft_r = pair
        dt_held = wk(2, 2)
        rt_flat = RT[:, :, :, :].rearrange("p a b c -> p (a b c)")
        xn_held = rt_flat[:, 0:512]
        bc_next = rt_flat[0:NBC, 512:768].bitcast(BF16)
        bc_now = rt_flat[0:NBC, 768:1024].bitcast(BF16)
        bc_rest = soft_e[0:NBC, 0:512]
        bc_mid = soft_d[0:NBC, 0:256].bitcast(BF16)
        dtr = soft_r[0:8, 0:512]
        TURN = {L0A: banks[:, 4, :], L3A: banks[:, 4, :], L0X: banks[:, 7, :], L1X: banks[:, 7, :], L2X: OB}
        VALUES = {L0A: banks[:, 5, :], L3A: banks[:, 5, :], L0X: banks[:, 7, :]}

        def cw_now(m):
            return wk(0)[0:64 + m["cols"], 0:256].bitcast(BF16)

        def cw_next(m):
            return wk(9)[0:64 + m["cols"], 0:256].bitcast(BF16)

        def groups(eng, name, program, woven, before=None):
            chain = chains[name]
            for ph in PHASES:
                if ph in WOVEN:
                    if ph != PHASES[0]:
                        eng.wait_ge(S["x_updated"].sem, S["x_updated"].at(ph, 0, 0))
                    chain.enter(eng, ph, 0, True)
                    if before:
                        before(ph)
                    woven(ph, None, Front(ph, 0, 0))
                    n = [chain.n]
                    with eng.Fori(0, GROUPS - 1) as i:
                        chain.enter(eng, ph, i)
                        woven(ph, i, Front(ph, i, 1))
                    n.append(chain.n)
                    chain.enter(eng, ph, GROUPS - 1)
                    woven(ph, GROUPS - 1, None)
                    seen[name, ph] = (*n, chain.n)
                    continue
                def one(i, first=False):
                    chain.enter(eng, ph, i)
                    if not first:
                        eng.wait_ge(S["x_updated"].sem, S["x_updated"].at(ph, i, 0))
                    program(ph, i)
                    seen[name, ph] = chain.n
                if ph == PHASES[0]:
                    one(0, True)
                    with eng.Fori(1, GROUPS) as i:
                        one(i)
                else:
                    with eng.Fori(0, GROUPS) as i:
                        one(i)

        class Front:

            def __init__(self, ph, i, ahead):
                self.ph, self.i, self.ahead = ph, i, ahead

            def at(self, name, k=1):
                return S[name].sem, S[name].at(self.ph, self.i, k + self.ahead * S[name].per[self.ph])

            def tile(self, t):
                return self.i * TILES + (self.ahead * TILES + t)

        def values_of(ph, i):
            return lambda name, k=1: (S[name].sem, S[name].at(ph, i, k))

        def ffn_weights(ph):
            m = MOE[ph]
            nf = m["nf"]
            if ph in (L0F, L3F):
                r = big
                a = 0
            else:
                r = small
                a = 0 if ph == L1F else MOE[L1F]["tiles"] * P
            n = m["tiles"] * P
            return (r[:, 0, a:a + nf], r[:, 1, a:a + nf],
                    r[:, 2, a:a + n].rearrange("p (t f) -> p t f", f=P))

        def apart(eng):
            eng.wait_ge(loaded, N_LOADED)

        N_LOADED = 16 * 20
        block = ctx.enter_context(nc.Block())

        @block.sync
        def _(sp):
            x_src = d["x"].rearrange("(t p) f -> p t f", p=P)
            sp.dma_start(xs[:, :, :], x_src).then_inc(loaded, 16)
            for dst, name in ((squares[:, :, :], "squares"), (cols[:, :], "cols"), (rows[:, :, :], "rows"),
                              (gates[:, :], "gates"), (rbias[:, :], "rbias"), (rank[:, :], "rank"),
                              (headmask[:, :], "headmask"), (causal[:, :], "causal"), (rope[:, :, :], "rope"),
                              (l1w[:, :, :], "l1w"), (bcw[:, :], "bcw"), (wdt[:, :, :], "wdt"),
                              (maskcol[:, :], "maskcol"), (pick[:, :].bitcast(U16), "pick"), (ident16[:, :].bitcast(U16), "ident16"), (work[:, 0:SEQ].bitcast(I32), "patch_lens")):
                sp.dma_start(dst, d[name]).then_inc(loaded, 16)
            for k, name in enumerate(("ln_g", "ln_b", "g_init")):
                sp.dma_start(fbc[:, k, :], d[name].partition_broadcast(P)).then_inc(loaded, 16)
            sp.dma_start(big[:, :, :], d["ffn_l0"]).then_inc(l0_loaded, 16)
            sp.dma_start(small[:, :, 0:d["ffn_mid"].shape[2]], d["ffn_mid"]).then_inc(l0_loaded, 16)
            sp.wait_ge(plug_done, 1)
            sp.dma_start(d["plug"], work[:, SEQ:2 * SEQ]).then_inc(plug_stored, 16)
            sp.wait_ge(plug_stored, 16)
            for ph in PHASES:
                if ph in MOE:
                    m = MOE[ph]
                    if ph != PHASES[0]:
                        sp.wait_ge(S["x_updated"].sem, S["x_updated"].at(ph, 0, 0))
                    n = m["e"] * P if ph == L0F else m["nf"]
                    sp.dma_start(sel16[0:64 + m["cols"], 0:n].bitcast(U16), d[f"sel{ph}"]).then_inc(sel_loaded, 16)
                if ph == L0F + 1:
                    sp.wait_ge(S["x_updated"].sem, S["x_updated"].at(ph, 0, 0))
                    sp.dma_start(big[:, :, 0:24 * P], d["ffn_l3"]).then_inc(l3_loaded, 16)
                if ph in (L0X, L1X, L2X, L3X):
                    if ph != PHASES[0]:
                        sp.wait_ge(S["x_updated"].sem, S["x_updated"].at(ph, 0, 0))
                    def load(i, first=False):
                        if not first:
                            for name in {L1X: ("ctx_psum", "v_ready"), L3X: ("ctx_used",)}.get(ph, ("ctx_psum",)):
                                sp.wait_ge(S[name].sem, S[name].at(ph, i, 0))
                        src = d["ctx"][bass.ds(i * NT, NT), :]
                        sp.dma_start(ctxn, src.rearrange("(t p) f -> p t f", p=P))\
                            .then_inc(S["ctx_landed"].sem, 16)
                        if ph == L2X:
                            if not first:
                                sp.wait_ge(S["heads_psum"].sem, S["heads_psum"].at(ph, i, 0))
                            sp.dma_start(wk(18, 2).rearrange("p (s f) -> p s f", s=SEQS)[0:SEQ],
                                         src[:, P:CTX].rearrange("(s k) f -> k s f", k=SEQ))\
                                .then_inc(S["ctx_values_landed"].sem, 16)
                        else:
                            if not first:
                                used = S["kt_ready" if ph == L0X else "row_used"]
                                sp.wait_ge(used.sem, used.at(ph, i, 0))
                            name = {L0X: "mask_f", L1X: "mask_i", L3X: "plug"}[ph]
                            dst = mask_bc.bitcast(I32) if ph == L1X else mask_bc
                            per_token = d[name][bass.ds(i * SEQS, SEQS), :].rearrange("b s -> (b s)")
                            sp.dma_start(dst, per_token.partition_broadcast(P)).then_inc(S["row_landed"].sem, 16)
                    load(0, True)
                    with sp.Fori(1, GROUPS) as i:
                        load(i)
            last = S["x_updated"]
            sp.wait_ge(last.sem, last.at(PHASES[-1], GROUPS, 0))
            sp.dma_start(out_dram.rearrange("(t p) f -> p t f", p=P), xs[:, :, :]).then_inc(out_stored, 16)
            sp.wait_ge(out_stored, 16)

        def pool_normalise(ph, u, eng, at):
            n = 8 if ATT[ph]["dh"] == 16 or ph == L2X else 16
            kl = (NT * 2 if ATT[ph]["dh"] == 8 else NT) // n
            e = sc[u % 2][:, 0:n * kl].rearrange("p (r k) -> p r k", k=kl)
            eng.wait_ge(*at("rsum_ready", u + 1))
            eng.tensor_tensor(e, e, over(att_small[:, 2, 0:n], kl), ALU.mult)\
                .then_inc(S["probs_ready"].sem, 1)

        def pool_rstd(at, eng, k):
            eng.wait_ge(*at("var_ready", k))
            eng.tensor_tensor(rstd[:, :], vare[:, :], power[:, :], ALU.pow).then_inc(S["rstd_ready"].sem, 1)

        @block.gpsimd
        def _(eng):
            eng.memset(power[:, :], -0.5).then_inc(setup_done, 1)
            eng.wait_ge(setup_done, 1)

            def program(ph, i):
                at = values_of(ph, i)
                pool_rstd(at, eng, 1)
                if ph == L3X:
                    pool_rstd(at, eng, 2)
                    pool_rstd(at, eng, 3)

            def woven(ph, i, front):
                if i is None:
                    pool_rstd(front.at, eng, 1)
                    return
                if ph in MOE or ph == L2A:
                    if front:
                        pool_rstd(front.at, eng, 1)
                    return
                at = values_of(ph, i)
                if ph == L1A:
                    for s in range(2 * D_STATE):
                        eng.wait_ge(*at("scan_ready", s + 1))
                        eng.wait_ge(*at("c_ready", s // 2 + 1))
                        if s >= 2:
                            eng.wait_ge(*at("hc_used", s - 1))
                        eng.tensor_tensor(wk(16 + s % 2), wk(14 + s % 2), wk(18 + s // 2 % 2), ALU.mult)\
                            .then_inc(S["hc_ready"].sem, 1)
                        if s == 1 and front:
                            pool_rstd(front.at, eng, 1)
                    eng.wait_ge(*at("res_var_ready"))
                    eng.tensor_tensor(rstd[:, :], vare[:, :], power[:, :], ALU.pow)\
                        .then_inc(S["res_rstd_ready"].sem, 1)
                    return
                units = ATT[ph]["units"]
                for u in range(units):
                    pool_normalise(ph, u, eng, at)
                    if u == units - 4 and front:
                        pool_rstd(front.at, eng, 1)
            groups(eng, "gpsimd", program, woven)

        @block.scalar
        def _(eng):
            link = chains["scalar"]
            eng.wait_ge(loaded, N_LOADED)
            eng.activation(l1w[:, :, 4:], l1w[:, :, 4:], ACT.Exp).then_inc(a_exp, 1)

            def transposed(at):
                eng.wait_ge(*at("xnt_psum"))
                eng.activation(xnt[:, :], NB, ACT.Copy).then_inc(S["xnt_ready"].sem, 1)

            def spread_heads(ph, at):
                a = ATT[ph]
                eng.wait_ge(*at("qt_ready"))
                dst = qbd.rearrange("p (b h s) -> p b h s", h=4, s=SEQ)
                m = 4 if a["dh"] == 8 else 10
                for h in range(32 // a["dh"]):
                    ins = eng.activation(dst[:, :, h, :], qt.rearrange("p (b s) -> p b s", s=SEQ), ACT.Copy,
                                         scale=headmask[:, m + h:m + h + 1])
                ins.then_inc(S["qbd_ready"].sem, 1)

            def xnt_out(ph, at):
                eng.wait_ge(*at("xnt_psum"))
                eng.activation(xnt[:, :], TURN[ph], ACT.Copy)\
                    .then_inc(S["xnt_ready"].sem, 1)

            def ctxt_out(ph, at, k):
                eng.wait_ge(*at("ctx_psum", k + 1))
                eng.activation(ctxt[:, k * 512:(k + 1) * 512], TURN[ph], ACT.Copy)\
                    .then_inc(S["ctxt_ready"].sem, 1)

            def v_hold(at):
                eng.wait_ge(*at("proj_psum", 3))
                eng.activation(wk(14), VALUES[L0A], ACT.Copy).then_inc(S["v_held"].sem, 1)

            def v_out(ph, front):
                at = front.at
                if ph == L1X:
                    eng.wait_ge(*at("ctx_landed", 16))
                    ins = eng.activation(t4(vt), ctxn[:, :, P:CTX], ACT.Copy)
                elif ph == L2X:
                    eng.wait_ge(*at("proj_psum", 2))
                    ins = eng.activation(wk(18, 2)[SEQ:P], banks[SEQ:P, 6:8, :].rearrange("p a n -> p (a n)"),
                                         ACT.Copy)
                elif ph == L0X:
                    eng.wait_ge(*at("proj_psum", 3))
                    for t in range(TILES):
                        ins = eng.activation(t4(vt)[:, t, :], t4(VALUES[ph])[:, t, :], ACT.Copy,
                                             scale=maskcol[:, bass.ds(front.tile(t), 1)])
                else:
                    eng.wait_ge(*at("v_held"))
                    ins = eng.activation(vt, wk(14), ACT.Copy)
                ins.then_inc(S["v_ready"].sem, 1)

            def attend(ph, i, front):
                if i is None:
                    xnt_out(ph, front.at)
                    for k in range({L0X: 2, L1X: 1, L2X: 1}.get(ph, 0)):
                        ctxt_out(ph, front.at, k)
                    spread_heads(ph, front.at)
                    if ph in (L0A, L3A):
                        v_hold(front.at)
                    v_out(ph, front)
                    return
                at = values_of(ph, i)
                a = ATT[ph]
                units = a["units"]
                n = 1024 if a["dh"] == 8 else 512
                for u in range(units + 1):
                    if u < units:
                        if ph == L2X:
                            eng.wait_ge(*at("scores_read", 2 * u + 2))
                        else:
                            eng.wait_ge(*at("shifted_ready", u + 1))
                        eng.activation(sc[u % 2][:, 0:n], sc[u % 2][:, 0:n], ACT.Exp)\
                            .then_inc(S["exp_ready"].sem, 1)
                    if u == 0 and ph == L0X:
                        eng.wait_ge(*at("xnt_ready"))
                        eng.activation(wk(12), xnt[:, :], ACT.Copy).then_inc(S["xn_kept"].sem, 1)
                        eng.wait_ge(*at("xn_kept"))
                    if u >= 1:
                        eng.wait_ge(*at("probst_psum", u))
                        if u >= 2:
                            eng.wait_ge(*at("heads_psum", u - 1))
                        eng.activation(pt[:, 0:n], banks[:, 6:8, :].rearrange("p a n -> p (a n)")[:, 0:n],
                                       ACT.Copy).then_inc(S["probst_ready"].sem, 1)
                    if front and u == units - 2 and ph not in (L0A, L3A):
                        xnt_out(ph, front.at)
                        if ph != L2X:
                            ctxt_out(ph, front.at, 0)
                    if front and u == units - 1:
                        if ph in (L0A, L3A):
                            xnt_out(ph, front.at)
                        if ph == L0X:
                            ctxt_out(ph, front.at, 1)
                        if ph == L2X:
                            ctxt_out(ph, front.at, 0)
                        spread_heads(ph, front.at)
                        if ph in (L0A, L3A):
                            v_hold(front.at)
                if front:
                    eng.wait_ge(*at("heads_psum", units))
                    v_out(ph, front)

            def feed_forward(ph, i, front):
                m = MOE[ph]
                tiles = m["tiles"]
                z = slots(ph)
                at = None if i is None else values_of(ph, i)

                def hold_tokens():
                    eng.wait_ge(*front.at("xnt_psum"))
                    eng.activation(wk(8), NB, ACT.Copy).then_inc(S["xnt_held"].sem, 1)

                def logits():
                    eng.wait_ge(*front.at("logits_shifted"))
                    eng.activation(RT[:, 1, :, 0:m["e"]], RT[:, 0, :, 0:m["e"]], ACT.Exp)\
                        .then_inc(S["logits_exp"].sem, 1)

                def hold_weights():
                    eng.wait_ge(*front.at("cwt_psum"))
                    eng.activation(cw_next(m), NB[0:64 + m["cols"], :], ACT.Copy)\
                        .then_inc(S["cwt_held"].sem, 1)

                def hand_over():
                    eng.wait_ge(*front.at("xnt_held"))
                    eng.activation(xnt[:, :], wk(8), ACT.Copy).then_inc(S["xnt_ready"].sem, 1)
                    eng.wait_ge(*front.at("cwt_held"))
                    eng.activation(cw_now(m), cw_next(m), ACT.Copy)\
                        .then_inc(S["cwt_ready"].sem, 1)
                    silu(0, front.at)

                def silu(f, at):
                    r = min(P, m["nf"] - f * P)
                    eng.wait_ge(*at("gate_psum", f + 1))
                    if f >= 2:
                        eng.wait_ge(*at("h_ready", f - 1))
                    eng.activation(wk(1 + f % 2)[0:r], banks[0:r, 2 + f % 2, :], ACT.Silu)\
                        .then_inc(S["silu_ready"].sem, 1)

                if i is None:
                    hold_tokens()
                    logits()
                    hold_weights()
                    hand_over()
                    return
                for f in range(1, tiles):
                    silu(f, at)
                    if front:
                        if f == z["turn"]:
                            hold_tokens()
                        if f == z["route"][0]:
                            logits()
                        if f == z["weights"]:
                            hold_weights()
                if front:
                    eng.wait_ge(*at("up_psum", tiles))
                    hand_over()
                eng.wait_ge(*at("down_done", tiles))
                eng.activation(wk(7), banks[:, 7, :], ACT.Copy).then_inc(S["yt_ready"].sem, 1)

            def woven(ph, i, front):
                if ph in ATT:
                    attend(ph, i, front)
                elif ph in MOE:
                    feed_forward(ph, i, front)
                elif ph == L1A:
                    mamba(ph, i, front)
                else:
                    linear_attention(ph, i, front)

            def program(ph, i):
                at = values_of(ph, i)
                if ph != L3X:
                    transposed(at)
                if ph == L3X:
                    eng.wait_ge(*at("xnt_psum"))
                    eng.activation(xnt[:, :], NB, ACT.Copy, scale=col("l3_res"))\
                        .then_inc(S["xnt_ready"].sem, 1)
                    eng.wait_ge(*at("dep_psum"))
                    eng.activation(wk(2), banks[:, 2, :], ACT.Copy).then_inc(S["dep_ready"].sem, 1)

            def linear_attention(ph, i, front):
                if i is not None:
                    at = values_of(ph, i)
                    eng.wait_ge(*at("qkt_psum"))
                    eng.activation(wk(3), banks[:, 5, :], ACT.Copy).then_inc(S["qkt_ready"].sem, 1)
                if front:
                    at = front.at
                    transposed(at)
                    for k in range(2):
                        eng.wait_ge(*at("qk_shifted", k + 1))
                        eng.activation(wk(k), wk(k), ACT.Exp).then_inc(S["qk_exp"].sem, 1)
                    eng.wait_ge(*at("proj_psum", 3))
                    eng.activation(wk(2), banks[:, 4, :], ACT.Copy).then_inc(S["v_ready"].sem, 1)

            def mamba(ph, i, front):
                at = None if i is None else values_of(ph, i)

                def start(slot):
                    at = front.at
                    if slot == 2:
                        eng.wait_ge(*at("xnt_psum"))
                        eng.activation(xnt[:, :], NB, ACT.Copy).then_inc(S["xnt_ready"].sem, 1)
                    if slot == 3:
                        eng.wait_ge(*at("proj_psum", 1))
                        eng.activation(bc_next, OB[0:NBC, :], ACT.Copy).then_inc(S["bc_high"].sem, 1)
                    if slot == 4:
                        eng.wait_ge(*at("proj_psum", 2))
                        eng.activation(xpad[:, 0, :, 3:], NB.rearrange("p (b s) -> p b s", s=SEQ), ACT.Copy)\
                            .then_inc(S["xs_padded"].sem, 1)
                        eng.wait_ge(*at("bc_rest"))
                        eng.activation(bc_mid[64:96], bc_rest[64:96], ACT.Copy)
                        eng.activation(bc_next[32:64], bc_rest[32:64], ACT.Copy).then_inc(S["bc_middle"].sem, 1)
                    if slot == 5:
                        eng.wait_ge(*at("proj_psum", 3))
                        eng.activation(xpad[:, 1, :, 3:], OB.rearrange("p (b s) -> p b s", s=SEQ), ACT.Copy)\
                            .then_inc(S["xs_padded"].sem, 1)
                    if slot == 8:
                        for h in range(2):
                            eng.wait_ge(*at("proj_psum", 4 + h))
                            ins = eng.activation(zs_held[:, h * 512:(h + 1) * 512], banks[:, h, :], ACT.Silu)
                        ins.then_inc(S["zs_ready"].sem, 1)
                        eng.wait_ge(*at("conv_ready"))
                        for h in range(2):
                            half = u_held[:, h * 512:(h + 1) * 512]
                            ins = eng.activation(half, half, ACT.Silu, bias=col(f"l1_cb{h}"))
                        ins.then_inc(S["u_ready"].sem, 1)
                    if slot == 9:
                        eng.wait_ge(*at("proj_psum", 6))
                        eng.activation(dtr, NB[0:8, :], ACT.Copy).then_inc(S["dtr_ready"].sem, 1)
                    if slot == 12:
                        eng.wait_ge(*at("dt_raw"))
                        link(eng.activation(soft_e, dt_held, ACT.Abs))
                        eng.activation(soft_e, soft_e, ACT.Exp, scale=-1.0).then_inc(S["soft_exp"].sem, 1)
                    if slot == 12:
                        eng.wait_ge(*at("soft_exp"))
                        eng.activation(soft_l, soft_e, ACT.Ln, bias=col("one")).then_inc(S["soft_ready"].sem, 1)

                def hand_over():
                    eng.wait_ge(*front.at("bc_middle"))
                    eng.wait_ge(*front.at("bc_held"))
                    eng.activation(bc_now, bc_next, ACT.Copy).then_inc(S["bc_ready"].sem, 1)

                if i is None:
                    for slot in range(D_STATE):
                        start(slot)
                    hand_over()
                    return
                eng.wait_ge(*at("dt_ready"))
                for n in range(D_STATE):
                    eng.wait_ge(*at("c_psum", n + 1))
                    if n >= 2:
                        eng.wait_ge(*at("hc_ready", 2 * n - 2))
                    eng.activation(wk(18 + n % 2), banks[:, 4 + n % 2, :], ACT.Copy)\
                        .then_inc(S["c_ready"].sem, 1)
                    for h in range(2):
                        s = 2 * n + h
                        if s >= 2:
                            eng.wait_ge(*at("scan_ready", s - 1))
                        eng.activation(wk(h), wk(8 + h), ACT.Exp, scale=l1w[:, h, 4 + n:5 + n])\
                            .then_inc(S["da_ready"].sem, 1)
                    if n == 0:
                        eng.activation(wk(4, 2), u_held, ACT.Copy)
                    if n == 1:
                        eng.activation(wk(10, 2), zs_held, ACT.Copy).then_inc(S["held_moved"].sem, 1)
                        eng.wait_ge(*at("held_moved"))
                    if front:
                        start(n)
                if front:
                    hand_over()

            groups(eng, "scalar", program, woven)

        @block.tensor
        def _(eng):
            eng.wait_ge(loaded, N_LOADED)
            mm = eng.matmul

            def transposes(dst, src_tiles):
                for t, src in enumerate(src_tiles):
                    ins = eng.transpose(dst[:, t * P:(t + 1) * P], src, ident)
                return ins

            def token_major(out, bias, *products):
                for t in range(TILES):
                    c = slice(t * P, (t + 1) * P)
                    dst = out[:, c]
                    mm(dst, ones_row, row(bias), start=True, stop=False)
                    for k, (src, weight) in enumerate(products):
                        ins = mm(dst, src[:, c], weight if weight.shape[1] == P else weight[:, c],
                                 start=False, stop=k == len(products) - 1)
                return ins

            def turn_context(ph, at, k):
                if k == 0:
                    eng.wait_ge(*at("ctx_landed", 16))
                    eng.wait_ge(*at("xnt_ready"))
                else:
                    eng.wait_ge(*at("ctxt_ready", k))
                transposes(TURN[ph], [ctxn[:, t, k * P:(k + 1) * P] for t in range(TILES)])\
                    .then_inc(S["ctx_psum"].sem, 1)

            def turn_tokens(ph, at):
                eng.wait_ge(*at("xn_ready"))
                transposes(TURN[ph], [xn[:, t, :] for t in range(TILES)]).then_inc(S["xnt_psum"].sem, 1)

            def projections(ph, at):
                if ph == L1X:
                    return
                eng.wait_ge(*at("xnt_ready"))
                if ph == L0X:
                    eng.wait_ge(*at("ctxt_ready", 2))
                    project("l0x_q", banks[:, 2, :]).then_inc(S["proj_psum"].sem, 1)
                    mm(banks[:, 3, :], sq("l0x_k0"), ctxt[:, 0:NT], start=True, stop=False)
                    mm(banks[:, 3, :], sq("l0x_k1"), ctxt[:, NT:2 * NT], start=False, stop=True)\
                        .then_inc(S["proj_psum"].sem, 1)
                    token_major(VALUES[ph], "l0x_v", (ctxt[:, 0:NT], sq("l0x_v0")),
                                (ctxt[:, NT:], sq("l0x_v1"))).then_inc(S["proj_psum"].sem, 1)
                elif ph == L2X:
                    project("l2x_q", banks[:, 2, :])
                    project("l2x_k", banks[:, 3, :]).then_inc(S["proj_psum"].sem, 1)
                else:
                    n = "l0" if ph == L0A else "l3"
                    project(n + "_q", banks[:, 2, :]).then_inc(S["proj_psum"].sem, 1)
                    project(n + "_k", banks[:, 3, :]).then_inc(S["proj_psum"].sem, 1)
                    token_major(VALUES[ph], n + "_v", (xnt, sq(n + "_v")))\
                        .then_inc(S["proj_psum"].sem, 1)

            def own_values():
                own = banks[SEQ:P, 6:8, :].rearrange("p a n -> p (a n)")
                for s in range(SEQS):
                    ins = mm(own[:, s * P:(s + 1) * P], xnt[:, s * SEQ:(s + 1) * SEQ], sq("l2x_v"),
                             start=True, stop=True, tile_position=(0, SEQ))
                ins.then_inc(S["proj_psum"].sem, 1)

            def attend(ph, i, front):
                at = None if i is None else values_of(ph, i)
                a = ATT[ph]
                dh = a["dh"]
                hg, units = 32 // dh, a["units"]
                pairs = hg // 2
                J = 4 * pairs
                q = qbd.rearrange("p (b n) -> p b n", b=SEQS)
                probs_bank = banks[:, 6:8, :].rearrange("p a n -> p (a n)")

                def scores(u):
                    if u == 0:
                        eng.wait_ge(*front.at("qbd_ready"))
                        eng.wait_ge(*front.at("kt_ready"))
                    for half in range(2):
                        if u >= 1:
                            eng.wait_ge(*at("scores_read", 2 * (u - 1) + half + 1))
                        for j in range(2 * half * pairs, 2 * (half + 1) * pairs):
                            g, jj = divmod(j, pairs)
                            part = slice(32 * g, 32 * g + 32)
                            for b in range(2):
                                if ph == L2X:
                                    seq, keys = u, (ctxt[part, u * SEQ:(u + 1) * SEQ] if b == 0 else
                                                    kt[part, u * SEQ:(u + 1) * SEQ])
                                else:
                                    seq = 2 * u + b
                                    keys = kt[part, seq * SEQ:(seq + 1) * SEQ]
                                c = (jj * 2 + b) * SEQ
                                ins = mm(banks[:, 2 + g, c:c + SEQ], q[part, seq, jj * P:(jj + 1) * P], keys,
                                         start=True, stop=True, tile_position=(32 * g, 0))
                        ins.then_inc(S["scores_psum"].sem, 1)

                def turn(u):
                    if u == 0:
                        eng.wait_ge(*at("v_ready"))
                    eng.wait_ge(*at("probs_ready", u + 1))
                    if u >= 1:
                        eng.wait_ge(*at("probst_ready", u))
                    for j in range(J):
                        ins = eng.transpose(probs_bank[:, j * P:(j + 1) * P], sc[u % 2][:, j * P:(j + 1) * P],
                                            ident)
                    ins.then_inc(S["probst_psum"].sem, 1)

                def values(u):
                    apart(eng)
                    if u == 0:
                        eng.wait_ge(*at("v_ready"))
                        if ph == L2X:
                            eng.wait_ge(*at("ctx_values_landed", 16))
                    eng.wait_ge(*at("probst_ready", u + 1))
                    if u >= 1:
                        eng.wait_ge(*at("heads_read", u))
                    n = hg * SEQ
                    for g in range(4):
                        if ph == L2X:
                            v = wk(18, 2).rearrange("p (s f) -> p s f", s=SEQS)[:, u, 32 * g:32 * g + 32]
                            ins = mm(banks[32 * g:32 * g + 32, 0, 0:n], v, pt[:, g * n:(g + 1) * n],
                                     start=True, stop=True, tile_position=(0, 32 * g))
                        else:
                            for b in range(2):
                                part = slice(b * SEQ, (b + 1) * SEQ)
                                v = t4(vt)[part, u, 32 * g:32 * g + 32]
                                ins = mm(banks[32 * g:32 * g + 32, b, 0:n], v,
                                         pt[part, g * n:(g + 1) * n], start=True, stop=True,
                                         tile_position=(b * SEQ, 32 * g))
                    ins.then_inc(S["heads_psum"].sem, 1)

                if i is None:
                    turn_tokens(ph, front.at)
                    for k in range({L0X: 2, L1X: 1, L2X: 1}.get(ph, 0)):
                        turn_context(ph, front.at, k)
                    projections(ph, front.at)
                    if ph == L2X:
                        own_values()
                    if ph in (L0A, L3A):
                        eng.wait_ge(*front.at("v_held"))
                    scores(0)
                    return
                for u in range(units):
                    if u + 1 < units:
                        scores(u + 1)
                    if u >= 1:
                        values(u - 1)
                    if front and u == units - 2 and ph not in (L0A, L3A):
                        turn_tokens(ph, front.at)
                        if ph in (L0X, L1X):
                            turn_context(ph, front.at, 0)
                    if front and u == units - 1:
                        if ph == L0X:
                            turn_context(ph, front.at, 1)
                        eng.wait_ge(*at("scores_read", 2 * units))
                        if ph in (L0A, L3A):
                            turn_tokens(ph, front.at)
                        projections(ph, front.at)
                        if ph == L2X:
                            turn_context(ph, front.at, 0)
                    turn(u)
                if front:
                    if ph in (L0A, L3A):
                        eng.wait_ge(*front.at("v_held"))
                    scores(0)
                values(units - 1)
                if front and ph == L2X:
                    own_values()
                    eng.wait_ge(*front.at("ctxt_ready"))
                eng.wait_ge(*at("heads_read", units))
                if ph == L0X:
                    eng.wait_ge(*at("xn_kept"))
                    ins = token_major(OB, "l0x_o", (wk(12), sq("l0x_o0")), (ht, sq("l0x_o1")))
                elif ph == L1X:
                    ins = transposes(OB, [ht[:, t * P:(t + 1) * P] for t in range(TILES)])
                else:
                    name = {L0A: "l0_o", L2X: "l2x_o", L3A: "l3_o"}[ph]
                    ins = token_major(OB, name, (ht, sq(name)))
                ins.then_inc(S["out_psum"].sem, 1)

            def feed_forward(ph, i, front):
                m = MOE[ph]
                e, ncol, tiles = m["e"], 64 + m["cols"], m["tiles"]
                z = slots(ph)
                at = None if i is None else values_of(ph, i)
                wg, wu, wd = ffn_weights(ph)
                gate_w = gates[:, 16 * ROUTERS.index(ph):16 * ROUTERS.index(ph) + e]
                cwt = cw_now(m)
                WB = banks[:, 6, :]
                per = m["f"] // P

                def turn_tokens():
                    eng.wait_ge(*front.at("xn_ready"))
                    transposes(NB, [xn[:, t, :] for t in range(TILES)]).then_inc(S["xnt_psum"].sem, 1)

                def router():
                    eng.wait_ge(*front.at("xnt_held"))
                    for t in range(TILES):
                        if ph == L3F:
                            mm(OB[:, t * e:(t + 1) * e], ones_row, rbias[0:1, 0:e], start=True, stop=False)
                        ins = mm(OB[:, t * e:(t + 1) * e], wk(8)[:, t * P:(t + 1) * P], gate_w,
                                 start=ph != L3F, stop=True)
                    ins.then_inc(S["logits_psum"].sem, 1)

                def ranks():
                    eng.wait_ge(*front.at("picks_ready"))
                    picks = RT[:, 8, :, 0:16]
                    mm(OB[:, 64:128].rearrange("p (t e) -> p t e", t=4), sq("before"), picks,
                       start=True, stop=True)
                    mm(OB[:, 128:192].rearrange("p (t e) -> p t e", t=4), sq("ones"), picks,
                       start=True, stop=True).then_inc(S["ranks_psum"].sem, 1)

                def turn_weights():
                    eng.wait_ge(*front.at("cw_ready"))
                    for t in range(TILES):
                        ins = mm(NB[0:ncol, t * P:(t + 1) * P], parts[:, t, 0:ncol], ident16[:, :],
                                 start=True, stop=True)
                    ins.then_inc(S["cwt_psum"].sem, 1)

                def down(f):
                    r = min(P, m["nf"] - f * P)
                    eng.wait_ge(*at("h_ready", f + 1))
                    mm(banks[:, 7, :], wd[0:r, f, :], wk(3 + f % 2)[0:r], start=f == 0,
                       stop=f == tiles - 1).then_inc(S["down_done"].sem, 1)

                def tile(f, at):
                    r = min(P, m["nf"] - f * P)
                    if f == 0:
                        eng.wait_ge(*at("xnt_ready"))
                        eng.wait_ge(*at("cwt_ready"))
                    if f >= 2:
                        eng.wait_ge(*at("silu_ready", f - 1))
                    if ph == L0F and f % per == 0:
                        x = f // per
                        if x >= 1:
                            eng.wait_ge(*at("wbc_read", x))
                        mm(WB, sel16[0:ncol, x * P:(x + 1) * P], cwt, start=True, stop=True)\
                            .then_inc(S["wbc_psum"].sem, 1)
                    mm(banks[0:r, 2 + f % 2, :], wg[:, f * P:f * P + r], xnt[:, :], start=True, stop=True)\
                        .then_inc(S["gate_psum"].sem, 1)
                    if ph != L0F:
                        if f >= 1:
                            eng.wait_ge(*at("wbc_read", f))
                        mm(WB[0:r], sel16[0:ncol, f * P:f * P + r], cwt, start=True, stop=True)\
                            .then_inc(S["wbc_psum"].sem, 1)
                    if f >= 2:
                        eng.wait_ge(*at("h_ready", f - 1))
                    if ph == L0F:
                        if f % per == 0:
                            eng.wait_ge(*at("wbc_read", f // per + 1))
                        up_in = wk(5 + f // per % 2)
                    else:
                        up_in = xnt[:, :]
                    mm(banks[0:r, 4 + f % 2, :], wu[:, f * P:f * P + r], up_in, start=True, stop=True)\
                        .then_inc(S["up_psum"].sem, 1)

                if i is None:
                    eng.wait_ge(sel_loaded, 16 * (1 + [p for p in PHASES if p in MOE].index(ph)))
                    eng.wait_ge(l0_loaded, 32)
                    if ph == L3F and L1A in PHASES:
                        eng.wait_ge(l3_loaded, 16)
                    turn_tokens()
                    router()
                    if m["cap"] is not None:
                        ranks()
                    turn_weights()
                    tile(0, front.at)
                    tile(1, front.at)
                    return
                for f in range(1, tiles):
                    if f >= 2:
                        tile(f, at)
                    down(f - 1)
                    if front:
                        if f == z["turn"]:
                            turn_tokens()
                        if f == z["router"]:
                            router()
                        if f == z["ranks"] and m["cap"] is not None:
                            ranks()
                        if f == z["weights"]:
                            turn_weights()
                if tiles % 2:
                    down(tiles - 1)
                if front:
                    if ph != L0F:
                        eng.wait_ge(*at("wbc_read", tiles))
                    tile(0, front.at)
                if tiles % 2 == 0:
                    down(tiles - 1)
                if front:
                    tile(1, front.at)
                eng.wait_ge(*at("yt_ready"))
                transposes(OB, [wk(7)[:, t * P:(t + 1) * P] for t in range(TILES)])\
                    .then_inc(S["out_psum"].sem, 1)

            def woven(ph, i, front):
                if ph in ATT:
                    attend(ph, i, front)
                elif ph in MOE:
                    feed_forward(ph, i, front)
                elif ph == L1A:
                    mamba(ph, i, front)
                else:
                    linear_attention(ph, i, front)

            def mamba(ph, i, front):
                at = None if i is None else values_of(ph, i)

                def start(slot):
                    at = front.at
                    if slot == 1:
                        eng.wait_ge(*at("xn_ready"))
                        transposes(NB, [xn_held[:, t * P:(t + 1) * P] for t in range(TILES)])\
                            .then_inc(S["xnt_psum"].sem, 1)
                    if slot == 2:
                        eng.wait_ge(*at("xnt_ready"))
                        mm(OB[0:NBC, :], bcw[:, 0:NBC], xnt[:, :], start=True, stop=True)\
                            .then_inc(S["proj_psum"].sem, 1)
                    if slot == 3:
                        project("l1_x0", NB).then_inc(S["proj_psum"].sem, 1)
                    if slot == 4:
                        eng.wait_ge(*at("bc_rest"))
                        project("l1_x1", OB).then_inc(S["proj_psum"].sem, 1)
                    if slot in (5, 6):
                        h = slot - 5
                        eng.wait_ge(*at("xs_padded", h + 1))
                        project(f"l1_z{h}", banks[:, h, :]).then_inc(S["proj_psum"].sem, 1)
                    if slot == 8:
                        eng.wait_ge(*at("zs_ready"))
                        mm(NB[0:8, :], bcw[:, NBC:NBC + 8], xnt[:, :], start=True, stop=True)\
                            .then_inc(S["proj_psum"].sem, 1)
                    if slot in (9, 10):
                        h = slot - 9
                        eng.wait_ge(*at("dtr_ready"))
                        mm(banks[:, 1 - h, :], wdt[0:8, h, :], dtr, start=True, stop=True)\
                            .then_inc(S["proj_psum"].sem, 1)

                def spread(n, at):
                    if n >= 2:
                        eng.wait_ge(*at("b_read", n - 1))
                        eng.wait_ge(*at("c_ready", n - 1))
                    mm(banks[:, 2 + n % 2, :], pick[:, n:n + 1].broadcast_to([NBC, P]), bc_now,
                       start=True, stop=True).then_inc(S["b_psum"].sem, 1)
                    mm(banks[:, 4 + n % 2, :], pick[:, D_STATE + n:D_STATE + n + 1].broadcast_to([NBC, P]),
                       bc_now, start=True, stop=True).then_inc(S["c_psum"].sem, 1)

                if i is None:
                    for slot in range(D_STATE):
                        start(slot)
                    eng.wait_ge(*front.at("bc_ready"))
                    spread(0, front.at)
                    spread(1, front.at)
                    return
                for n in range(D_STATE):
                    for h in range(2):
                        eng.wait_ge(*at("hc_ready", 2 * n + h + 1))
                        ins = mm(banks[:, 6 + h, :], ident, wk(16 + h), start=n == 0, stop=n == D_STATE - 1)
                        ins.then_inc(S["hc_used"].sem, 1)
                    if n + 2 < D_STATE:
                        spread(n + 2, at)
                    if front:
                        start(n)
                if front:
                    eng.wait_ge(*front.at("bc_ready"))
                    spread(0, front.at)
                    spread(1, front.at)
                eng.wait_ge(*at("ym_ready"))
                for t in range(TILES):
                    for h in range(2):
                        ins = mm(OB[:, t * P:(t + 1) * P], wk(14 + h)[:, t * P:(t + 1) * P], sq(f"l1_o{h}"),
                                 start=h == 0, stop=h == 1)
                ins.then_inc(S["out_psum"].sem, 1)

            def linear_attention(ph, i, front):
                def turn_tokens():
                    eng.wait_ge(*front.at("xn_ready"))
                    transposes(NB, [xn[:, t, :] for t in range(TILES)]).then_inc(S["xnt_psum"].sem, 1)
                    eng.wait_ge(*front.at("xnt_ready"))

                def made(k, w):
                    token_major(banks[:, 2 + k, :], w, (xnt, sq(w))).then_inc(S["proj_psum"].sem, 1)

                if i is None:
                    turn_tokens()
                    for k, w in enumerate(("l2_q", "l2_k", "l2_v")):
                        made(k, w)
                    return
                at = values_of(ph, i)
                eng.wait_ge(*at("qk_exp", 1))
                transposes(banks[:, 5, :], [wk(0)[:, t * P:(t + 1) * P] for t in range(TILES)])\
                    .then_inc(S["qkt_psum"].sem, 1)
                eng.wait_ge(*at("qk_exp", 2))
                eng.wait_ge(*at("v_ready"))
                for s in range(SEQS):
                    part = slice(s % 2 * SEQ, s % 2 * SEQ + SEQ)
                    c = slice((s // 2) * P, (s // 2 + 1) * P)
                    tp = (s % 2 * SEQ, 0)
                    mm(banks[:, 2 + s % 2, c], wk(1)[part, c], wk(2)[part, c], start=True, stop=True,
                       tile_position=tp)
                    ins = mm(banks[:, 6 + s % 2, c], wk(1)[part, c], sq("ones")[part, :], start=True,
                             stop=True, tile_position=tp)
                ins.then_inc(S["kv_psum"].sem, 1)
                if front:
                    turn_tokens()
                eng.wait_ge(*at("kv_ready"))
                eng.wait_ge(*at("qkt_ready"))
                for s in range(SEQS):
                    c = slice(s * SEQ, (s + 1) * SEQ)
                    k = slice((s % 2 * 4 + s // 2) * P, (s % 2 * 4 + s // 2 + 1) * P)
                    mm(banks[:, 4, c], wk(4, 2)[:, k], wk(3)[:, c], start=True, stop=True)
                    ins = mm(banks[:, 5, c], wk(6, 2)[:, k], wk(3)[:, c], start=True, stop=True)
                ins.then_inc(S["den_psum"].sem, 1)
                if front:
                    made(0, "l2_q")
                    made(1, "l2_k")
                eng.wait_ge(*at("y_ready"))
                token_major(OB, "l2_o", (wk(10), sq("l2_o"))).then_inc(S["out_psum"].sem, 1)
                if front:
                    made(2, "l2_v")

            def project(name, bank, src=None):
                return mm(bank, sq(name), xnt[:, :] if src is None else src, start=True, stop=True)

            def program(ph, i):
                at = values_of(ph, i)
                if ph != L3X:
                    eng.wait_ge(*at("xn_ready"))
                    transposes(NB, [xn[:, t, :] for t in range(TILES)]).then_inc(S["xnt_psum"].sem, 1)
                    eng.wait_ge(*at("xnt_ready"))
                if ph == L3X:
                    eng.wait_ge(*at("u_scaled"))
                    for t in range(TILES):
                        ins = mm(banks[:, 2, t * P:(t + 1) * P], sq("decay"), wk(0)[:, t * P:(t + 1) * P],
                                 start=True, stop=True)
                    ins.then_inc(S["dep_psum"].sem, 1)
                    eng.wait_ge(*at("xn_ready"))
                    transposes(NB, [wk(3)[:, t * P:(t + 1) * P] for t in range(TILES)])\
                        .then_inc(S["xnt_psum"].sem, 1)
                    eng.wait_ge(*at("xnt_ready"))
                    eng.wait_ge(*at("dep_ready"))
                    eng.wait_ge(*at("row_used"))
                    ins = token_major(OB, "l3_in", (xnt, sq("l3_in")), (wk(4), wk(2)))
                    ins.then_inc(S["out_psum"].sem, 1)
            groups(eng, "tensor", program, woven)

        @block.vector
        def _(eng):
            link = chains["vector"]
            eng.wait_ge(loaded, N_LOADED)
            n = [0]

            def step(ins):
                n[0] += 1
                ins.then_inc(plug_step, 1)
                eng.wait_ge(plug_step, n[0])

            TT, TS, STT = eng.tensor_tensor, eng.tensor_scalar, eng.scalar_tensor_tensor
            step(eng.memset(xpad[:, :, :, :], 0.0))
            step(eng.memset(cnt[:, :, :], 0.0))
            step(eng.memset(RT[:, :, :, :], 1.0))
            step(eng.memset(parts[:, :, :], 0.0))
            step(eng.memset(work[:, 3 * SEQ:4 * SEQ], 1.0))
            lens, plug = work[:, 2 * SEQ:3 * SEQ], work[:, SEQ:2 * SEQ]
            onesw, wrap = work[:, 3 * SEQ:4 * SEQ], work[:, 4 * SEQ:5 * SEQ]
            hits = work[:, 512:512 + SEQ * SEQ].rearrange("p (t i) -> p t i", i=SEQ)
            bound = work[:, 5 * SEQ:6 * SEQ]
            step(eng.tensor_copy(lens, work[:, 0:SEQ].bitcast(I32)))
            step(eng.tensor_tensor_scan(bound, onesw, lens, 0.0, ALU.mult, ALU.add))
            step(TS(bound, bound, 1.0, None, ALU.subtract))
            step(TS(wrap, bound, 0.0, float(SEQ), ALU.is_lt, ALU.mult))
            step(TT(bound, bound, wrap, ALU.add))
            step(eng.tensor_tensor_scan(wrap, onesw, onesw, -1.0, ALU.mult, ALU.add))
            step(TT(hits, over(wrap, SEQ), times(bound, SEQ), ALU.is_equal))
            step(eng.tensor_reduce(lens, hits, AXX, ALU.max))
            step(eng.tensor_tensor_scan(plug, onesw, lens, -1.0, ALU.mult, ALU.add))
            TS(plug, plug, 0.0, None, ALU.max).then_inc(plug_done, 1)
            eng.wait_ge(a_exp, 1)
            TS(l1w[:, :, 4:], l1w[:, :, 4:], -1.0, None, ALU.mult).then_inc(a_ready, 1)
            eng.wait_ge(a_ready, 1)
            step(TT(sq("l0_q"), sq("l0_q"), rope[:, 0, :], ALU.mult))
            step(TT(sq("l0_qb"), sq("l0_qb"), rope[:, 1, :], ALU.mult))
            step(TT(sq("l0_q"), sq("l0_q"), sq("l0_qb"), ALU.add))
            step(TT(col("l0_q"), col("l0_q"), col("cos"), ALU.mult))
            step(STT(col("l0_q"), col("l0_qb"), col("sin"), col("l0_q"), ALU.mult, ALU.add))
            eng.wait_ge(plug_stored, 16)

            def norm(group):
                norm_stats(group)
                return norm_scale(group)

            def norm_stats(group):
                for t in range(TILES):
                    ins = eng.bn_stats(stats[:, t, :], xs[:, bass.ds(group.tile(t), 1), :])
                link(ins)
                eng.memset(att_small[0:1, 0, 15:16], 0.0)
                for t in range(TILES):
                    ins = eng.bn_aggr(mv[:, t, :], stats[:, t, :])
                link(ins)
                TS(vare[:, :], mv[:, :, 1], EPS, None, ALU.add).then_inc(S["var_ready"].sem, 1)

            def norm_scale(group, dst=xn):
                eng.wait_ge(*group.at("rstd_ready", 1))
                for t in range(TILES):
                    ins = TS(dst[:, t, :], xs[:, bass.ds(group.tile(t), 1), :].rearrange("p a f -> p (a f)"),
                             mv[:, t, 0:1], rstd[:, t:t + 1], ALU.subtract, ALU.mult)
                return ins

            def add_out(i, at):
                eng.wait_ge(*at("out_psum"))
                x4 = xs[:, bass.ds(i * TILES, TILES), :]
                TT(x4, x4, t4(OB), ALU.add).then_inc(S["x_updated"].sem, 1)

            def heads_in(ph, at):
                if ph == L0X:
                    eng.wait_ge(*at("row_landed", 16))
                    TS(mask_add, mask_bc, 0.0, NEG, ALU.is_equal, ALU.mult)
                    eng.wait_ge(*at("proj_psum", 1))
                    STT(qt, banks[:, 2, :], col("l0x_q"), mask_bc, ALU.add, ALU.mult)\
                        .then_inc(S["qt_ready"].sem, 1)
                    eng.wait_ge(*at("proj_psum", 2))
                    STT(kt, banks[:, 3, :], col("l0x_k"), mask_bc, ALU.add, ALU.mult)\
                        .then_inc(S["kt_ready"].sem, 1)
                elif ph == L1X:
                    eng.wait_ge(*at("xnt_ready"))
                    eng.tensor_copy(qt, xnt[:, :]).then_inc(S["qt_ready"].sem, 1)
                    eng.wait_ge(*at("ctxt_ready"))
                    eng.tensor_copy(kt, ctxt[:, 0:NT]).then_inc(S["kt_ready"].sem, 1)
                    eng.wait_ge(*at("row_landed", 16))
                    link(eng.tensor_copy(mask_add, mask_bc.bitcast(I32)))
                    link(TS(mask_add, mask_add, -1.0, 1.0, ALU.mult, ALU.add))
                    TS(mask_add, mask_add, NEG, None, ALU.mult).then_inc(S["row_used"].sem, 1)
                    eng.wait_ge(*at("row_used"))
                elif ph == L2X:
                    eng.wait_ge(*at("proj_psum", 1))
                    eng.tensor_copy(qt, banks[:, 2, :]).then_inc(S["qt_ready"].sem, 1)
                    eng.tensor_copy(kt, banks[:, 3, :]).then_inc(S["kt_ready"].sem, 1)
                else:
                    n = "l0" if ph == L0A else "l3"
                    eng.wait_ge(*at("proj_psum", 1))
                    TS(qt, banks[:, 2, :], col(n + "_q"), None, ALU.add).then_inc(S["qt_ready"].sem, 1)
                    eng.wait_ge(*at("proj_psum", 2))
                    TS(kt, banks[:, 3, :], col(n + "_k"), None, ALU.add).then_inc(S["kt_ready"].sem, 1)

            def attend(ph, i, front):
                if i is None:
                    norm(front).then_inc(S["xn_ready"].sem, 1)
                    heads_in(ph, front.at)
                    return
                at = values_of(ph, i)
                a = ATT[ph]
                dh, units = a["dh"], a["units"]
                n = 1024 if dh == 8 else 512
                kl = P if ph == L2X else SEQ
                r = n // kl
                hg = 32 // dh
                bank = banks[:, 2:6, 0:n // 4].rearrange("p g (r k) -> p g r k", k=kl)
                mx, sm, rc = (att_small[:, k, 0:r] for k in range(3))

                def rk(ap):
                    return ap.rearrange("p (r k) -> p r k", k=kl)

                for u in range(units + 2):
                    if u < units:
                        s = sc[u % 2][:, 0:n].rearrange("p (g r k) -> p g r k", g=4, k=kl)
                        if u >= 2:
                            eng.wait_ge(*at("probst_psum", u - 1))
                        for half in range(2):
                            eng.wait_ge(*at("scores_psum", 2 * u + half + 1))
                            gs = slice(2 * half, 2 * half + 2)
                            if ph in (L0A, L3A):
                                m = causal[:, :].unsqueeze(1).unsqueeze(1).broadcast_to([P, 2, r // 4, SEQ])
                                ins = TT(s[:, gs], bank[:, gs], m, ALU.add)
                            elif ph in (L0X, L1X):
                                s2 = sc[u % 2][:, 0:n].rearrange("p (g k) -> p g k", g=4)[:, gs]
                                b2 = banks[:, 2 + 2 * half:4 + 2 * half, 0:P]
                                m = times(mask_add[:, u * P:(u + 1) * P], 2)
                                if ph == L0X:
                                    ins = TT(s2, b2, m, ALU.add)
                                else:
                                    ins = STT(s2, b2, col("l1x_b"), m, ALU.add, ALU.add)
                            else:
                                mh = mx[:, half * r // 2:(half + 1) * r // 2]
                                link(eng.tensor_reduce(mh, bank[:, gs], AXX, ALU.max))
                                mh = mh.rearrange("p (g r) -> p g r", g=2).unsqueeze(3)\
                                    .broadcast_to([P, 2, r // 4, kl])
                                ins = TT(s[:, gs], bank[:, gs], mh, ALU.subtract)
                            ins.then_inc(S["scores_read"].sem, 1)
                        if ph != L2X:
                            eng.wait_ge(*at("scores_read", 2 * u + 2))
                            link(eng.tensor_reduce(mx, s, AXX, ALU.max))
                            mx4 = mx.rearrange("p (g r) -> p g r", g=4).unsqueeze(3)\
                                .broadcast_to([P, 4, r // 4, kl])
                            TT(s, s, mx4, ALU.subtract).then_inc(S["shifted_ready"].sem, 1)
                    if u < units:
                        eng.wait_ge(*at("exp_ready", u + 1))
                        if u >= 1:
                            eng.wait_ge(*at("probs_ready", u))
                        link(eng.tensor_reduce(sm, rk(sc[u % 2][:, 0:n]), AXX, ALU.add))
                        eng.reciprocal(rc, sm).then_inc(S["rsum_ready"].sem, 1)
                    if front and u == units - 4:
                        norm_stats(front)
                    if front and u == units - 3:
                        norm_scale(front).then_inc(S["xn_ready"].sem, 1)
                    if u >= 2:
                        v = u - 2
                        eng.wait_ge(*at("heads_psum", v + 1))
                        nb = 1 if ph == L2X else 2
                        dst = ht[:, v * nb * SEQ:(v + 1) * nb * SEQ].rearrange("p (b s) -> p b s", b=nb)
                        src = banks[:, 0:nb, 0:hg * SEQ].rearrange("p b (h s) -> p b h s", h=hg)
                        m = 0 if dh == 8 else 8
                        for h in range(hg):
                            hm = headmask[:, m + h:m + h + 1]
                            if h == 0:
                                ins = TS(dst, src[:, :, h, :], hm, None, ALU.mult)
                            else:
                                ins = STT(dst, src[:, :, h, :], hm, dst, ALU.mult, ALU.add)
                            if h < hg - 1:
                                link(ins)
                        ins.then_inc(S["heads_read"].sem, 1)
                    if front and u == units - 1:
                        heads_in(ph, front.at)
                add_out(i, at)

            def route(ph, at):
                m = MOE[ph]
                e = m["e"]
                R = lambda k: RT[:, k, :, 0:e]
                sm = lambda k: RT[:, 20, :, k]
                bc = lambda k: over(sm(k), e)
                lg = OB[:, 0:4 * e].rearrange("p (t e) -> p t e", t=4)
                eng.wait_ge(*at("logits_psum"))
                link(eng.tensor_reduce(sm(0), lg, AXX, ALU.max))
                TT(R(0), lg, bc(0), ALU.subtract).then_inc(S["logits_shifted"].sem, 1)
                yield
                eng.wait_ge(*at("logits_exp"))
                link(eng.tensor_reduce(sm(1), R(1), AXX, ALU.add))
                link(eng.reciprocal(sm(2), sm(1)))
                link(TT(R(2), R(1), bc(2), ALU.mult))
                yield

                def best(probs, k, out, signal=None):
                    link(eng.tensor_reduce(sm(k), probs, AXX, ALU.max))
                    link(TT(R(3), probs, bc(k), ALU.is_equal))
                    link(TT(R(3), R(3), times(rank[:, 16 - e:16], 4), ALU.mult))
                    link(eng.tensor_reduce(sm(5), R(3), AXX, ALU.max))
                    ins = TT(out, R(3), bc(5), ALU.is_equal)
                    if signal is None:
                        link(ins)
                    else:
                        ins.then_inc(S[signal].sem, 1)
                        eng.wait_ge(*at(signal))
                oh1, oh2 = (RT[:, 8, :, 0:8], RT[:, 8, :, 8:16]) if ph == L0F else (R(9), R(10))
                best(R(2), 3, oh1)
                yield
                link(STT(R(4), oh1, -2.0, R(2), ALU.mult, ALU.add))
                best(R(4), 4, oh2, "picks_ready" if ph == L0F else None)
                yield
                if ph != L1F:
                    eps = {L0F: 0.0, L2F: 1e-20, L3F: 1e-9}[ph]
                    link(TT(sm(6), sm(3), sm(4), ALU.add))
                    if eps:
                        link(TS(sm(6), sm(6), eps, None, ALU.add))
                    link(eng.reciprocal(sm(7), sm(6)))
                    link(TT(sm(3), sm(3), sm(7), ALU.mult))
                    link(TT(sm(4), sm(4), sm(7), ALU.mult))
                if ph == L3F:
                    TT(RT[:, 8, :, 0:16], oh1, oh2, ALU.add).then_inc(S["picks_ready"].sem, 1)
                    eng.wait_ge(*at("picks_ready"))
                yield
                if m["cap"] is not None:
                    eng.wait_ge(*at("ranks_psum"))
                    tot = OB[:, 128:192].rearrange("p (t e) -> p t e", t=4)
                    for t in range(TILES):
                        link(TT(cnt[:, t + 1, :], cnt[:, t, :], tot[:, t, :], ALU.add))
                    link(TT(RT[:, 11, :, 0:16], OB[:, 64:128].rearrange("p (t e) -> p t e", t=4),
                            cnt[:, 0:4, :], ALU.add))
                    yield
                    link(eng.tensor_copy(cnt[:, 0, :], cnt[:, 4, :]))
                    link(TS(RT[:, 12, :, 0:16], RT[:, 11, :, 0:16], float(m["cap"]), None, ALU.is_lt))
                if ph == L0F:
                    link(TT(RT[:, 8, :, 0:16], RT[:, 8, :, 0:16], RT[:, 12, :, 0:16], ALU.mult))
                link(TT(R(5), oh1, bc(3), ALU.mult))
                link(TT(R(6), oh2, bc(4), ALU.mult))
                if ph == L3F:
                    link(TT(R(5), R(5), R(6), ALU.add))
                    link(TT(R(16), R(5), R(12), ALU.mult))
                else:
                    link(TT(R(16), R(5), R(6), ALU.add))
                yield
                w, rest, rest2 = (RT[:, k, :, 0:m["cols"]] for k in (16, 17, 18))
                high, middle, low = (parts[:, :, k:k + m["cols"]] for k in (0, 32, 64))
                link(eng.tensor_copy(high, w))
                link(TT(rest, w, high, ALU.subtract))
                link(eng.tensor_copy(middle, rest))
                link(TT(rest2, rest, middle, ALU.subtract))
                eng.tensor_copy(low, rest2).then_inc(S["cw_ready"].sem, 1)
                yield

            def feed_forward(ph, i, front):
                m = MOE[ph]
                per, tiles = m["f"] // P, m["tiles"]
                z = slots(ph)
                at = None if i is None else values_of(ph, i)

                def scale():
                    norm_scale(front).then_inc(S["xn_ready"].sem, 1)
                    if ph == L3F:
                        eng.wait_ge(*front.at("xn_ready"))
                        x4 = xs[:, bass.ds(front.tile(0), TILES), :]
                        TT(x4, x4, xn[:, :, :], ALU.add)

                def hidden(f, at):
                    r = min(P, m["nf"] - f * P)
                    if ph == L0F and f % per == 0:
                        x = f // per
                        eng.wait_ge(*at("wbc_psum", x + 1))
                        if x >= 2:
                            eng.wait_ge(*at("up_psum", (x - 1) * per))
                        TT(wk(5 + x % 2), xnt[:, :], banks[:, 6, :], ALU.mult).then_inc(S["wbc_read"].sem, 1)
                    sg = wk(1 + f % 2)[0:r]
                    eng.wait_ge(*at("silu_ready", f + 1))
                    if ph != L0F:
                        eng.wait_ge(*at("wbc_psum", f + 1))
                        TT(sg, sg, banks[0:r, 6, :], ALU.mult).then_inc(S["wbc_read"].sem, 1)
                        eng.wait_ge(*at("wbc_read", f + 1))
                    eng.wait_ge(*at("up_psum", f + 1))
                    if f >= 2:
                        eng.wait_ge(*at("down_done", f - 1))
                    TT(wk(3 + f % 2)[0:r], sg, banks[0:r, 4 + f % 2, :], ALU.mult)\
                        .then_inc(S["h_ready"].sem, 1)

                if i is None:
                    norm_stats(front)
                    scale()
                    for _ in route(ph, front.at):
                        pass
                    hidden(0, front.at)
                    return
                if front:
                    routing = route(ph, front.at)
                for f in range(tiles):
                    if f >= 1:
                        hidden(f, at)
                    if front:
                        if f == z["stats"]:
                            norm_stats(front)
                        if f == z["scale"]:
                            scale()
                        for _ in range(z["route"].count(f)):
                            next(routing, None)
                if front:
                    assert next(routing, "done") == "done"
                    hidden(0, front.at)
                add_out(i, at)

            def woven(ph, i, front):
                if ph in ATT:
                    attend(ph, i, front)
                elif ph in MOE:
                    feed_forward(ph, i, front)
                elif ph == L1A:
                    mamba(ph, i, front)
                else:
                    linear_attention(ph, i, front)

            def linear_attention(ph, i, front):
                def shifted():
                    for k in range(2):
                        eng.wait_ge(*front.at("proj_psum", k + 1))
                        b = banks[:, 2 + k, :].rearrange("p (r d) -> p r d", d=8)
                        link(eng.tensor_reduce(wk(9)[:, 0:SEQ], b, AXX, ALU.max))
                        TT(wk(k).rearrange("p (r d) -> p r d", d=8), b, over(wk(9)[:, 0:SEQ], 8),
                           ALU.subtract).then_inc(S["qk_shifted"].sem, 1)
                        eng.wait_ge(*front.at("qk_shifted", k + 1))

                if front:
                    norm(front).then_inc(S["xn_ready"].sem, 1)
                if i is None:
                    shifted()
                    return
                at = values_of(ph, i)
                eng.wait_ge(*at("kv_psum"))
                kv = banks[:, 2:4, :].rearrange("p a (s f) -> p (a s) f", f=P)
                ks = banks[:, 6:8, :].rearrange("p a (s f) -> p (a s) f", f=P)
                m = times(sq("block8"), SEQS)
                TT(wk(4, 2).rearrange("p (s f) -> p s f", f=P), kv, m, ALU.mult)
                TT(wk(6, 2).rearrange("p (s f) -> p s f", f=P), ks, m, ALU.mult)\
                    .then_inc(S["kv_ready"].sem, 1)
                eng.wait_ge(*at("den_psum"))
                link(TS(wk(8), banks[:, 5, :], 1e-6, None, ALU.add))
                link(eng.reciprocal(wk(9), wk(8)))
                TT(wk(10), wk(9), banks[:, 4, :], ALU.mult).then_inc(S["y_ready"].sem, 1)
                if front:
                    eng.wait_ge(*at("y_ready"))
                    shifted()
                add_out(i, at)

            def mamba(ph, i, front):
                at = None if i is None else values_of(ph, i)

                def conv(taps):
                    for k in taps:
                        for h in range(2):
                            o = u_held[:, h * 512:(h + 1) * 512].rearrange("p (b s) -> p b s", s=SEQ)
                            src = xpad[:, h, :, k:k + SEQ]
                            if k == 0:
                                ins = TS(o, src, l1w[:, h, 0:1], None, ALU.mult)
                            else:
                                ins = STT(o, src, l1w[:, h, k:k + 1], o, ALU.mult, ALU.add)
                        if k < 3:
                            link(ins)
                    return ins

                def start(slot):
                    if slot == 0:
                        norm_stats(front)
                    if slot == 1:
                        norm_scale(front, t4(xn_held)).then_inc(S["xn_ready"].sem, 1)
                    if slot == 3:
                        eng.wait_ge(*front.at("bc_high"))
                        TT(bc_rest, OB[0:NBC, :], bc_next, ALU.subtract).then_inc(S["bc_rest"].sem, 1)
                        eng.wait_ge(*front.at("bc_rest"))
                    if slot == 5:
                        eng.wait_ge(*front.at("bc_middle"))
                        TT(bc_next[64:96], bc_rest[64:96], bc_mid[64:96], ALU.subtract)\
                            .then_inc(S["bc_held"].sem, 1)
                    if slot == 6:
                        if i is not None:
                            eng.wait_ge(*at("held_moved"))
                        eng.wait_ge(*front.at("xs_padded", 2))
                        conv((0, 1))
                    if slot == 7:
                        conv((2, 3)).then_inc(S["conv_ready"].sem, 1)
                    if slot == 11:
                        for h in range(2):
                            eng.wait_ge(*front.at("proj_psum", 7 + h))
                            ins = TS(dt_held[:, h * 512:(h + 1) * 512], banks[:, 1 - h, :], col(f"l1_dt{h}"),
                                     None, ALU.add)
                        ins.then_inc(S["dt_raw"].sem, 1)
                    if slot == 13:
                        eng.wait_ge(*front.at("soft_exp"))
                        link(TS(soft_d, soft_e, 1.0, None, ALU.add))
                        link(TS(soft_d, soft_d, 1.0, None, ALU.subtract))
                        link(TS(soft_r, soft_d, 0.0, None, ALU.is_equal))
                        link(TT(soft_d, soft_d, soft_r, ALU.add))
                    if slot == 14:
                        link(eng.reciprocal(soft_d, soft_d))
                    if slot == 15:
                        eng.wait_ge(*front.at("soft_ready"))
                        link(TT(soft_d, soft_d, soft_e, ALU.mult))
                        link(TT(soft_l, soft_r, soft_l, ALU.add))
                        link(TT(soft_d, soft_d, soft_l, ALU.mult))
                        link(STT(dt_held, dt_held, 0.0, soft_d, ALU.max, ALU.add))

                def hand_over():
                    TT(wk(6, 2), dt_held, u_held, ALU.mult)
                    link(eng.tensor_copy(wk(8, 2), dt_held))
                    eng.memset(wk(8, 2).rearrange("p (b s) -> p b s", s=SEQ)[:, :, 0:1], 1e25)\
                        .then_inc(S["dt_ready"].sem, 1)
                    eng.wait_ge(*front.at("dt_ready"))

                if i is None:
                    for slot in range(D_STATE):
                        start(slot)
                    link(eng.tensor_copy(xn[:, :, :], t4(xn_held)))
                    eng.wait_ge(*front.at("u_ready"))
                    hand_over()
                    return
                for s in range(2 * D_STATE):
                    st, h = divmod(s, 2)
                    eng.wait_ge(*at("b_psum", st + 1))
                    db = wk(12 + h)
                    ins = TT(db, wk(6 + h), banks[:, 2 + st % 2, :], ALU.mult)
                    if h == 1:
                        ins.then_inc(S["b_read"].sem, 1)
                        eng.wait_ge(*at("b_read", st + 1))
                    else:
                        link(ins)
                    eng.wait_ge(*at("da_ready", s + 1))
                    if s >= 2:
                        eng.wait_ge(*at("hc_ready", s - 1))
                    eng.tensor_tensor_scan(wk(14 + h), wk(h), db, 0.0, ALU.mult, ALU.add)\
                        .then_inc(S["scan_ready"].sem, 1)
                    if h == 1 and front:
                        start(st)
                eng.wait_ge(*at("hc_used", 2 * D_STATE))
                eng.wait_ge(*at("held_moved"))
                for h in range(2):
                    ins = STT(wk(12 + h), wk(4 + h), col(f"l1_d{h}"), banks[:, 6 + h, :], ALU.mult, ALU.add)
                link(ins)
                TT(wk(14, 2), wk(12, 2), wk(10, 2), ALU.mult).then_inc(S["ym_ready"].sem, 1)
                if front:
                    eng.wait_ge(*front.at("u_ready"))
                    hand_over()
                eng.wait_ge(*at("out_psum"))
                res = t4(wk(12))
                link(TT(res, xn[:, :, :], t4(OB), ALU.add))
                for t in range(TILES):
                    ins = eng.bn_stats(stats[:, t, :], res[:, t, :])
                link(ins)
                eng.memset(att_small[0:1, 0, 15:16], 0.0)
                for t in range(TILES):
                    ins = eng.bn_aggr(mv[:, t, :], stats[:, t, :])
                link(ins)
                TS(vare[:, :], mv[:, :, 1], EPS, None, ALU.add).then_inc(S["res_var_ready"].sem, 1)
                if front:
                    eng.tensor_copy(xn[:, :, :], t4(xn_held))
                eng.wait_ge(*at("res_rstd_ready"))
                for t in range(TILES):
                    ins = TS(res[:, t, :], res[:, t, :], mv[:, t, 0:1], rstd[:, t:t + 1],
                             ALU.subtract, ALU.mult)
                link(ins)
                link(TT(res, res, times(fbc[:, 0, :], TILES), ALU.mult))
                link(TT(res, res, times(fbc[:, 1, :], TILES), ALU.add))
                x4 = xs[:, bass.ds(i * TILES, TILES), :]
                TT(x4, x4, res, ALU.add).then_inc(S["x_updated"].sem, 1)
                if front:
                    eng.wait_ge(*at("x_updated"))

            def program(ph, i):
                at = values_of(ph, i)
                group = Front(ph, i, 0)
                if ph == L3X:
                    link(norm(group))
                else:
                    norm(group).then_inc(S["xn_ready"].sem, 1)
                if ph == L3X:
                    link(TT(t4(wk(5)), xn[:, :, :], xn[:, :, :], ALU.mult))
                    link(eng.tensor_reduce(vare[:, :], t4(wk(5)), AXX, ALU.add))
                    TS(vare[:, :], vare[:, :], 1.0 / P, EPS, ALU.mult, ALU.add)\
                        .then_inc(S["var_ready"].sem, 1)
                    eng.wait_ge(*at("rstd_ready", 2))
                    for t in range(TILES):
                        ins = TS(wk(3)[:, t * P:(t + 1) * P], xn[:, t, :], rstd[:, t:t + 1], None, ALU.mult)
                    ins.then_inc(S["xn_ready"].sem, 1)
                    eng.wait_ge(*at("ctx_landed", 16))
                    link(TT(wk(5, 2).rearrange("p (t f) -> p t f", t=TILES), ctxn, ctxn, ALU.mult))
                    link(eng.tensor_reduce(vare[:, :], wk(5, 2).rearrange("p (t f) -> p t f", t=TILES),
                                           AXX, ALU.add))
                    TS(vare[:, :], vare[:, :], 1.0 / CTX, EPS, ALU.mult, ALU.add)\
                        .then_inc(S["var_ready"].sem, 1)
                    eng.wait_ge(*at("rstd_ready", 3))
                    for t in range(TILES):
                        ins = TS(wk(7)[:, t * P:(t + 1) * P], ctxn[:, t, 0:P], rstd[:, t:t + 1], None, ALU.mult)
                    ins.then_inc(S["ctx_used"].sem, 1)
                    eng.wait_ge(*at("ctx_used"))
                    TT(t4(wk(0)), t4(wk(7)), times(fbc[:, 2, :], TILES), ALU.mult)\
                        .then_inc(S["u_scaled"].sem, 1)
                    eng.wait_ge(*at("row_landed", 16))
                    STT(t4(wk(4)), t4(mask_bc), col("iota64"), times(sq("block64"), TILES),
                        ALU.is_equal, ALU.mult).then_inc(S["row_used"].sem, 1)
                add_out(i, at)

            def before(ph):
                if ph == L3F:
                    link(eng.memset(cnt[:, :, :], 0.0))
            groups(eng, "vector", program, woven, before)
    return seen


def host_arrays(a):
    f = lambda n: np.asarray(a[n], np.float32)
    z = {}
    perm_a, perm_b = [0, 2, 1, 3, 4, 6, 5, 7], [1, 3, 0, 2, 5, 7, 4, 6]
    heads = lambda w, p: w.reshape(P, 16, 8)[:, :, p].reshape(P, P)
    heads1 = lambda b, p: b.reshape(16, 8)[:, p].reshape(P)
    rep16 = lambda w: np.tile(w, (1, 16))
    wsrc, wtgt, wout = f("L0_xattn_W_src"), f("L0_xattn_W_tgt"), f("L0_xattn_W_out")
    win, w_out1 = f("L1_attn_W_in"), f("L1_attn_W_out")
    qkv = f("L2_xattn_w_qkv")
    h3 = lambda n: f(n).transpose(1, 0, 2).reshape(P, P)
    tok = np.arange(P)
    step_ = np.exp(-0.001)
    dt = -np.log(-np.expm1(-0.001))
    lag = tok[None, :] % SEQ - tok[:, None] % SEQ
    same = tok[None, :] // SEQ == tok[:, None] // SEQ
    decay = np.where(same & (lag >= 0), step_ * np.exp(-dt * np.maximum(lag, 0)), 0.0)
    q = {
        "l0_q": heads(f("L0_attn_Wq"), perm_a), "l0_qb": heads(f("L0_attn_Wq"), perm_b),
        "l0_k": rep16(f("L0_attn_Wk")[:, perm_a]),
        "l0_v": rep16(f("L0_attn_Wv")), "l0_o": f("L0_attn_Wo"),
        "l0x_k0": wsrc[:P, :P].T, "l0x_k1": wsrc[:P, P:].T, "l0x_v0": wsrc[P:, :P].T, "l0x_v1": wsrc[P:, P:].T,
        "l0x_q": wtgt.T, "l0x_o0": wout[:, :P].T, "l0x_o1": wout[:, P:].T,
        "l1_x0": win[0:P].T, "l1_x1": win[P:2 * P].T, "l1_z0": win[2 * P:3 * P].T, "l1_z1": win[3 * P:4 * P].T,
        "l1_o0": w_out1[:, :P].T, "l1_o1": w_out1[:, P:].T,
        "l2_q": f("L2_attn_Wq").T, "l2_k": f("L2_attn_Wk").T, "l2_v": f("L2_attn_Wv").T, "l2_o": f("L2_attn_Wo").T,
        "l2x_q": qkv[:P].T, "l2x_k": qkv[P:2 * P].T, "l2x_v": qkv[2 * P:].T, "l2x_o": f("L2_xattn_w_proj").T,
        "l3_q": h3("L3_attn_Wq"), "l3_k": h3("L3_attn_Wk"), "l3_v": h3("L3_attn_Wv"), "l3_o": f("L3_attn_Wo"),
        "l3_in": f("L3_xattn_W_in").T,
        "ident": np.eye(P), "ones": np.ones((P, P)), "before": tok[:, None] < tok[None, :],
        "block8": tok[:, None] // 8 == tok[None, :] // 8, "decay": decay, "block64": same,
    }
    theta = (1.0 / 10000.0 ** (np.arange(0, 4, 2, dtype=np.float32) / 4)).astype(np.float32)
    ang = (tok // 8).astype(np.float32) * theta[np.array([0, 1, 0, 1])[tok % 4]]
    cos, sin = np.cos(ang), np.sin(ang) * np.where(tok % 4 < 2, -1, 1)
    z["squares"] = np.stack([q[n] for n in SQUARES], 1).astype(np.float32)
    bsrc = f("L0_xattn_b_src")
    rep_b = lambda b: np.tile(b, 16)
    cb, bdt, dd = f("L1_attn_conv_b"), f("L1_attn_b_dt"), f("L1_attn_D")
    c = {
        "cos": cos, "sin": sin, "l0_q": heads1(f("L0_attn_bq"), perm_a), "l0_qb": heads1(f("L0_attn_bq"), perm_b),
        "l0_k": rep_b(f("L0_attn_bk")[perm_a]),
        "l0x_k": bsrc[:P], "l0x_q": f("L0_xattn_b_tgt"), "l3_q": f("L3_attn_bq").reshape(P),
        "l3_k": f("L3_attn_bk").reshape(P), "l1_cb0": cb[:P], "l1_cb1": cb[P:], "l1_dt0": bdt[:P],
        "l1_dt1": bdt[P:], "l1_d0": dd[:P], "l1_d1": dd[P:], "l1x_b": np.repeat(f("L1_xattn_b"), P),
        "l3_res": f("L3_xattn_g_res"), "iota64": tok % SEQ, "one": np.ones(P), "zero": np.zeros(P),
    }
    z["cols"] = np.stack([c[n] for n in COLS], 1).astype(np.float32)
    r = {
        "l0_v": rep_b(f("L0_attn_bv")), "l0_o": f("L0_attn_bo"), "l0x_v": bsrc[P:], "l0x_o": f("L0_xattn_b_out"),
        "l2_q": f("L2_attn_bq"), "l2_k": f("L2_attn_bk"), "l2_v": f("L2_attn_bv"), "l2_o": f("L2_attn_bo"),
        "l2x_o": f("L2_xattn_b_proj"), "l3_v": f("L3_attn_bv").reshape(P), "l3_o": f("L3_attn_bo"),
        "l3_in": f("L3_xattn_b_in"), "ones": np.ones(P),
    }
    z["rows"] = np.stack([r[n] for n in ROWS])[None].astype(np.float32)
    g = np.zeros((P, 64), np.float32)
    for k, w in enumerate((f("L0_ffn_gate_w").T, f("L1_ffn_gate_w").T, f("L2_ffn_gate_w").T, f("L3_ffn_router_w"))):
        g[:, 16 * k:16 * k + w.shape[1]] = w
    z["gates"] = g
    z["rbias"] = np.tile(f("L3_ffn_router_b"), 4)[None]
    z["rank"] = np.tile(np.arange(16, 0, -1, dtype=np.float32), (P, 1))
    m8 = (tok[:, None] % 32 // 8 == np.arange(4)[None]).astype(np.float64)
    m16 = (tok[:, None] % 32 // 16 == np.arange(2)[None]).astype(np.float64)
    z["headmask"] = np.concatenate([m8, m8 / np.sqrt(8.0), m16, m16 / 4], 1).astype(np.float32)
    z["causal"] = np.where(np.arange(SEQ)[None] <= tok[:, None] % SEQ, 0.0, NEG).astype(np.float32)
    z["rope"] = np.tile(np.stack([cos, sin])[None], (P, 1, 1)).astype(np.float32)
    taps, alog = f("L1_attn_conv_w")[:, 0], f("L1_attn_A_log")
    z["l1w"] = np.concatenate([taps, alog], 1).reshape(2, P, 4 + D_STATE).transpose(1, 0, 2)
    z["bcw"] = np.concatenate([win[4 * P:4 * P + 2 * D_STATE]] * 3 + [win[4 * P + 2 * D_STATE:]]).T
    one_bf16 = np.uint16(0x3F80)
    z["ident16"] = np.eye(P, dtype=np.uint16) * one_bf16
    z["pick"] = np.tile(np.eye(2 * D_STATE, dtype=np.uint16) * one_bf16, (3, 1))
    z["wdt"] = f("L1_attn_W_dt").T.reshape(8, 2, P)
    z["ln_g"], z["ln_b"], z["g_init"] = f("L1_attn_ln_g"), f("L1_attn_ln_b"), f("L3_xattn_g_init")[:P]
    z["maskcol"] = f("mask_BxS2_fk1").reshape(-1, P).T
    z["mask_f"] = f("mask_BxS2_fk1")
    z["mask_i"], z["patch_lens"] = np.asarray(a["mask_BxS2_ik0"]), np.asarray(a["mask_BxS2_if0"])

    def ffn(gate, up, down):
        nf = gate.shape[1]
        t = -(-nf // P)
        o = np.zeros((P, 3, t * P), np.float32)
        o[:, 0, :nf], o[:, 1, :nf] = gate, up
        dp = np.zeros((t * P, P), np.float32)
        dp[:nf] = down
        o[:, 2] = dp.reshape(t, P, P).transpose(1, 0, 2).reshape(P, t * P)
        return o
    efd = lambda n: f(n).transpose(2, 0, 1).reshape(P, -1)
    edf = lambda n: f(n).transpose(0, 2, 1).reshape(-1, P)
    hei = lambda n: f(n).transpose(1, 0, 2).reshape(P, -1)
    z["ffn_l0"] = ffn(efd("L0_ffn_wi_gate"), efd("L0_ffn_wi_up"), edf("L0_ffn_wo"))
    l1 = ffn(np.concatenate([efd("L1_ffn_wg"), f("L1_ffn_sg").T], 1),
             np.concatenate([efd("L1_ffn_wu"), f("L1_ffn_su").T], 1),
             np.concatenate([edf("L1_ffn_wd"), f("L1_ffn_sd").T], 0))
    l2 = ffn(np.concatenate([hei("L2_ffn_wg"), f("L2_ffn_swg")], 1),
             np.concatenate([hei("L2_ffn_wu"), f("L2_ffn_swu")], 1),
             np.concatenate([f("L2_ffn_wd").reshape(-1, P), f("L2_ffn_swd")], 0))
    z["ffn_mid"] = np.concatenate([l1, l2], 2)
    z["ffn_l3"] = ffn(np.concatenate([hei("L3_ffn_w_gate"), f("L3_ffn_sw_gate")], 1),
                      np.concatenate([hei("L3_ffn_w_up"), f("L3_ffn_sw_up")], 1),
                      np.concatenate([f("L3_ffn_w_down").reshape(-1, P), f("L3_ffn_sw_down")], 0))
    for ph, m in MOE.items():
        n = m["e"] * P if ph == L0F else m["nf"]
        per = P if ph == L0F else m["f"]
        one = np.minimum(np.arange(n) // per, m["cols"] - 1)[None] == np.arange(32)[:, None]
        z[f"sel{ph}"] = np.tile(one.astype(np.uint16) * one_bf16, (3, 1))[0:64 + m["cols"]]
    z["x"] = f("x").reshape(TOKENS, P)
    z["ctx"] = f("ctx_2048").reshape(TOKENS, CTX)
    return {k: np.ascontiguousarray(v) for k, v in z.items()}


def build(Bacc, arrays, counts):
    nc = Bacc("TRN2", target_bir_lowering=False, num_devices=1)
    d = {n: nc.dram_tensor(f"in_{n}", v.shape, mybir.dt.from_np(v.dtype), kind="ExternalInput").ap()
         for n, v in arrays.items()}
    d["plug"] = nc.dram_tensor("plug", (BATCH, SEQ), F32, kind="Internal").ap()
    out = nc.dram_tensor("out_x", (TOKENS, P), F32, kind="ExternalOutput").ap()
    return nc, decoder(nc, d, out, counts)


COUNTS = {
    "gpsimd": {L0A: (0, 0, 0), L0X: (0, 0, 0), L0F: (0, 0, 0), L1A: (0, 0, 0), L1X: (0, 0, 0), L1F: (0, 0, 0), L2A: (0, 0, 0), L2X: (0, 0, 0), L2F: (0, 0, 0), L3A: (0, 0, 0), L3F: (0, 0, 0)},
    "scalar": {L0A: (0, 0, 0), L0X: (0, 0, 0), L0F: (0, 0, 0), L1A: (1, 1, 0), L1X: (0, 0, 0), L1F: (0, 0, 0), L2A: (0, 0, 0), L2X: (0, 0, 0), L2F: (0, 0, 0), L3A: (0, 0, 0), L3F: (0, 0, 0)},
    "tensor": {L0A: (0, 0, 0), L0X: (0, 0, 0), L0F: (0, 0, 0), L1A: (0, 0, 0), L1X: (0, 0, 0), L1F: (0, 0, 0), L2A: (0, 0, 0), L2X: (0, 0, 0), L2F: (0, 0, 0), L3A: (0, 0, 0), L3F: (0, 0, 0)},
    "vector": {L0A: (2, 22, 20), L0X: (2, 14, 12), L0F: (35, 35, 0), L1A: (16, 38, 23), L1X: (4, 16, 12), L1F: (24, 24, 0), L2A: (4, 6, 2), L2X: (2, 50, 48), L2F: (29, 29, 0), L3A: (2, 22, 20), L3X: 7, L3F: (38, 37, 0)},
}


def kernel(**inputs):
    import concourse.bacc as _bacc
    from concourse.bass_utils import run_bass_kernel_spmd as _run

    arrays = host_arrays(inputs)
    nc = build(_bacc.Bacc, arrays, COUNTS)[0]
    r = _run(nc, [{f"in_{n}": v for n, v in arrays.items()}], core_ids=[0])
    return r.results[0]["out_x"].reshape(BATCH, SEQ, P)
```
